# Optimizing a Trainium2 kernel written in Bass

```python
import numpy as np
import jax
import jax.numpy as jnp

def _softmax(x, axis=-1):
    return jax.nn.softmax(x, axis=axis)

def _gelu(x):
    return jax.nn.gelu(x, approximate=True)

def _silu(x):
    return jax.nn.silu(x)

def _sigmoid(x):
    return jax.nn.sigmoid(x)

def _layernorm(x, axis=-1, eps=1e-05):
    m = jnp.mean(x, axis=axis, keepdims=True)
    v = jnp.var(x, axis=axis, keepdims=True)
    return (x - m) / jnp.sqrt(v + eps)

def _scatter_add(tgt, idx, src, axis=0):
    return tgt.at[idx].add(src)

def _segment_sum(src, seg, n):
    return jax.ops.segment_sum(src, seg, n)
kernel_name = 'mk_flamingo_gated_d2_seqx_r8_9c915e'

def setup_inputs(seed: int=0):
    np.random.seed(seed)
    _w = jnp.asarray

    def _rec_inputs():
        import jax
        import jax.numpy as jnp
        _rk = jax.random.key(seed)
        x = 7.22e-05 + 1 * jax.random.normal(jax.random.fold_in(_rk, 1), (16, 64, 512), jnp.float32)
        _lenS = 64 - jax.random.randint(jax.random.fold_in(_rk, 7), (16,), 0, max(1, 64 // 4) + 1, jnp.int32)
        _lenS2 = 64 - jax.random.randint(jax.random.fold_in(_rk, 8), (16,), 0, max(1, 64 // 4) + 1, jnp.int32)
        _ctx_4096P = jax.random.normal(jax.random.fold_in(_rk, 11), (16, 16, 512), jnp.float32)
        _ctx_4096c = jax.random.dirichlet(jax.random.fold_in(_rk, 511), 0.3 * jnp.ones((16,), jnp.float32), (16, 64))
        _ctx_4096t = jnp.einsum('bsk,bkd->bsd', _ctx_4096c, _ctx_4096P)
        _ctx_4096t = _ctx_4096t * jax.lax.rsqrt(jnp.mean(jnp.square(_ctx_4096t)) + 1e-12) * 0.953939
        ctx_4096 = 4.13588e-05 + 0.999923 * (_ctx_4096t + 0.3 * jax.random.normal(jax.random.fold_in(_rk, 611), (16, 64, 512), jnp.float32))
        _validS = jnp.arange(64)[None, :] < _lenS[:, None]
        _validS2 = jnp.arange(64)[None, :] < _lenS2[:, None]
        _causal = jnp.tril(jnp.ones((64, 64), dtype=bool))
        mask_BxSxS2_ff1 = jnp.where(jnp.ones((16, 64, 64), dtype=bool), 1.0, 0.0).astype(jnp.float32)
        _g = jax.random.normal(jax.random.fold_in(_rk, 9001), (2, 2), jnp.float32)
        _g = jnp.sign(_g) * jnp.maximum(jnp.abs(_g), 1.0) + (_g == 0) * 1.0
        g_xattn = _g[0]
        g_ffn = _g[1]
        return (x, ctx_4096, mask_BxSxS2_ff1, g_xattn, g_ffn)
    x, ctx_4096, mask_BxSxS2_ff1, g_xattn, g_ffn = _rec_inputs()

    def _L0_xattn_setup():
        import jax, jax.numpy as jnp
        import numpy as np
        HEADS = 8
        WINDOW = 16

        def _pointwise(W, b, t):
            return jnp.einsum('oc,bct->bot', W, t) + b[None, :, None]
        key = jax.random.key(seed)
        ks = jax.random.split(key, 10)
        B, C, T = (4, 64, 512)
        s = 0.02
        return {'x': jax.random.normal(ks[0], (B, C, T), jnp.float32), 'cond': jax.random.normal(ks[1], (B, C, T), jnp.float32), 'Wq': jax.random.normal(ks[2], (C, C), jnp.float32) * s, 'bq': jnp.zeros((C,), jnp.float32), 'Wk': jax.random.normal(ks[3], (C, C), jnp.float32) * s, 'bk': jnp.zeros((C,), jnp.float32), 'Wv': jax.random.normal(ks[4], (C, C), jnp.float32) * s, 'bv': jnp.zeros((C,), jnp.float32), 'Wo': jax.random.normal(ks[5], (C, C), jnp.float32) * s, 'bo': jnp.zeros((C,), jnp.float32)}
    _L0_xattn_all = _L0_xattn_setup()
    _L0_xattn_in = {k: v for k, v in _L0_xattn_all.items() if k in ('Wq', 'bq', 'Wk', 'bk', 'Wv', 'bv', 'Wo', 'bo')}
    del _L0_xattn_all

    def _L0_ffn_setup():
        import jax, jax.numpy as jnp
        import numpy as np
        B, T, D_IN, D_OUT = (8, 256, 512, 512)
        N_LORAS, RANK = (16, 32)
        SCALING = 1.0
        key = jax.random.key(seed)
        ks = jax.random.split(key, 8)
        std = 1.0 / D_IN ** 0.5
        x = jax.random.normal(ks[0], (B, T, D_IN), dtype=jnp.float32)
        idx = jax.random.randint(ks[1], (B,), 0, N_LORAS)
        gate = jax.nn.one_hot(idx, N_LORAS, dtype=jnp.float32)
        kernel = jax.random.normal(ks[2], (D_IN, D_OUT), dtype=jnp.float32) * std
        bias = jnp.zeros((D_OUT,), dtype=jnp.float32)
        lora_A = jax.random.normal(ks[3], (N_LORAS, RANK, D_IN), dtype=jnp.float32) * std
        lora_B = jax.random.normal(ks[4], (N_LORAS, D_OUT, RANK), dtype=jnp.float32) * 0.01
        lora_A_shared = jax.random.normal(ks[5], (RANK, D_IN), dtype=jnp.float32) * std
        lora_B_shared = jax.random.normal(ks[6], (D_OUT, RANK), dtype=jnp.float32) * 0.01
        return {'x': x, 'gate': gate, 'kernel': kernel, 'bias': bias, 'lora_A': lora_A, 'lora_B': lora_B, 'lora_A_shared': lora_A_shared, 'lora_B_shared': lora_B_shared}
    _L0_ffn_all = _L0_ffn_setup()
    _L0_ffn_in = {k: v for k, v in _L0_ffn_all.items() if k in ('gate', 'kernel', 'bias', 'lora_A', 'lora_B', 'lora_A_shared', 'lora_B_shared')}
    del _L0_ffn_all

    def _L1_xattn_setup():
        import jax, jax.numpy as jnp
        import numpy as np
        N_Q_HEADS = 32
        N_KV_HEADS = 8
        D_MODEL = 512
        D_K = 128
        D_V = 128
        ROPE_BASE = 10000.0

        def _rope(x):
            d = x.shape[-1]
            s = x.shape[2]
            inv_freq = 1.0 / ROPE_BASE ** (jnp.arange(0, d, 2, dtype=jnp.float32) / d)
            ang = jnp.arange(s, dtype=jnp.float32)[:, None] * inv_freq[None, :]
            cos = jnp.concatenate([jnp.cos(ang), jnp.cos(ang)], axis=-1)[None, None]
            sin = jnp.concatenate([jnp.sin(ang), jnp.sin(ang)], axis=-1)[None, None]
            x1, x2 = (x[..., :d // 2], x[..., d // 2:])
            rot = jnp.concatenate([-x2, x1], axis=-1)
            return x * cos + rot * sin
        key = jax.random.key(seed)
        ks = jax.random.split(key, 8)
        bs, s = (2, 128)
        inp = {'query': jax.random.normal(ks[0], (bs, s, D_MODEL), dtype=jnp.float32), 'key': jax.random.normal(ks[1], (bs, s, D_MODEL), dtype=jnp.float32), 'value': jax.random.normal(ks[2], (bs, s, D_MODEL), dtype=jnp.float32), 'mask': jnp.ones((bs, s, s), dtype=jnp.float32), 'wq': jax.random.normal(ks[3], (D_MODEL, N_Q_HEADS * D_K), dtype=jnp.float32) * 0.02, 'wk': jax.random.normal(ks[4], (D_MODEL, N_KV_HEADS * D_K), dtype=jnp.float32) * 0.02, 'wv': jax.random.normal(ks[5], (D_MODEL, N_KV_HEADS * D_V), dtype=jnp.float32) * 0.02, 'wo': jax.random.normal(ks[6], (N_Q_HEADS * D_V, D_MODEL), dtype=jnp.float32) * 0.02}
        return inp
    _L1_xattn_all = _L1_xattn_setup()
    _L1_xattn_in = {k: v for k, v in _L1_xattn_all.items() if k in ('wq', 'wk', 'wv', 'wo')}
    del _L1_xattn_all

    def _L1_ffn_setup():
        import jax, jax.numpy as jnp
        import numpy as np
        LORA_SCALE = 16.0 / jnp.sqrt(16.0)
        TOP_K = 2
        key = jax.random.key(seed)
        k1, k2, k3, k4 = jax.random.split(key, 4)
        B_, S, D, O, E, R = (4, 256, 512, 512, 4, 16)
        x = jax.random.normal(k1, (B_, S, D), dtype=jnp.float32)
        router_w = jax.random.normal(k2, (E, D), dtype=jnp.float32) * 0.02
        A = jax.random.normal(k3, (E, R, D), dtype=jnp.float32) * 0.02
        B = jax.random.normal(k4, (O,), dtype=jnp.float32)
        B = jax.random.normal(k4, (E, O, R), dtype=jnp.float32) * 0.02
        return {'x': x, 'router_w': router_w, 'A': A, 'B': B}
    _L1_ffn_all = _L1_ffn_setup()
    _L1_ffn_in = {k: v for k, v in _L1_ffn_all.items() if k in ('router_w', 'A', 'B')}
    del _L1_ffn_all
    return {'x': x, 'ctx_4096': ctx_4096, 'mask_BxSxS2_ff1': mask_BxSxS2_ff1, 'g_xattn': g_xattn, 'g_ffn': g_ffn, 'L0_xattn_Wq': _L0_xattn_in['Wq'], 'L0_xattn_bq': _L0_xattn_in['bq'], 'L0_xattn_Wk': _L0_xattn_in['Wk'], 'L0_xattn_bk': _L0_xattn_in['bk'], 'L0_xattn_Wv': _L0_xattn_in['Wv'], 'L0_xattn_bv': _L0_xattn_in['bv'], 'L0_xattn_Wo': _L0_xattn_in['Wo'], 'L0_xattn_bo': _L0_xattn_in['bo'], 'L0_ffn_gate': _L0_ffn_in['gate'], 'L0_ffn_kernel': _L0_ffn_in['kernel'], 'L0_ffn_bias': _L0_ffn_in['bias'], 'L0_ffn_lora_A': _L0_ffn_in['lora_A'], 'L0_ffn_lora_B': _L0_ffn_in['lora_B'], 'L0_ffn_lora_A_shared': _L0_ffn_in['lora_A_shared'], 'L0_ffn_lora_B_shared': _L0_ffn_in['lora_B_shared'], 'L1_xattn_wq': _L1_xattn_in['wq'], 'L1_xattn_wk': _L1_xattn_in['wk'], 'L1_xattn_wv': _L1_xattn_in['wv'], 'L1_xattn_wo': _L1_xattn_in['wo'], 'L1_ffn_router_w': _L1_ffn_in['router_w'], 'L1_ffn_A': _L1_ffn_in['A'], 'L1_ffn_B': _L1_ffn_in['B']}

def reference(x, ctx_4096, mask_BxSxS2_ff1, g_xattn, g_ffn, L0_xattn_Wq, L0_xattn_bq, L0_xattn_Wk, L0_xattn_bk, L0_xattn_Wv, L0_xattn_bv, L0_xattn_Wo, L0_xattn_bo, L0_ffn_gate, L0_ffn_kernel, L0_ffn_bias, L0_ffn_lora_A, L0_ffn_lora_B, L0_ffn_lora_A_shared, L0_ffn_lora_B_shared, L1_xattn_wq, L1_xattn_wk, L1_xattn_wv, L1_xattn_wo, L1_ffn_router_w, L1_ffn_A, L1_ffn_B):
    import jax
    import jax.numpy as jnp

    def _L0_xattn_ref(x, cond, Wq, bq, Wk, bk, Wv, bv, Wo, bo):
        import jax, jax.numpy as jnp
        import numpy as np
        HEADS = 8
        WINDOW = 16

        def _pointwise(W, b, t):
            return jnp.einsum('oc,bct->bot', W, t) + b[None, :, None]
        B, C, T = x.shape
        H, W = (HEADS, WINDOW)
        hd = C // H
        scale = hd ** (-0.5)
        pad_left = W // 2
        pad_right = W - pad_left - 1
        q = _pointwise(Wq, bq, x)
        k = _pointwise(Wk, bk, cond)
        v = _pointwise(Wv, bv, cond)
        k = jnp.pad(k, ((0, 0), (0, 0), (pad_left, pad_right)))
        v = jnp.pad(v, ((0, 0), (0, 0), (pad_left, pad_right)))
        idx = jnp.arange(T)[:, None] + jnp.arange(W)[None, :]
        k_win = k[:, :, idx].reshape(B, H, hd, T, W)
        v_win = v[:, :, idx].reshape(B, H, hd, T, W)
        qh = q.reshape(B, H, hd, T)
        dots = jnp.einsum('bhdt,bhdtw->bhtw', qh, k_win) * scale
        attn = jax.nn.softmax(dots, axis=-1)
        out = jnp.einsum('bhtw,bhdtw->bhdt', attn, v_win)
        out = out.reshape(B, C, T)
        return _pointwise(Wo, bo, out)

    def _L0_ffn_ref(x, gate, kernel, bias, lora_A, lora_B, lora_A_shared, lora_B_shared):
        import jax, jax.numpy as jnp
        import numpy as np
        B, T, D_IN, D_OUT = (8, 256, 512, 512)
        N_LORAS, RANK = (16, 32)
        SCALING = 1.0
        base_out = jnp.matmul(x, kernel) + bias
        b = gate.shape[0]
        x_flat = x.reshape(b, -1, x.shape[-1])
        A_eff = jnp.einsum('bn,nri->bri', gate, lora_A)
        B_eff = jnp.einsum('bn,nor->bor', gate, lora_B)
        Ax = jnp.einsum('bri,bti->btr', A_eff, x_flat)
        delta_flat = jnp.einsum('bor,btr->bto', B_eff, Ax)
        Ax_s = jnp.einsum('ri,bti->btr', lora_A_shared, x_flat)
        delta_flat = delta_flat + jnp.einsum('or,btr->bto', lora_B_shared, Ax_s)
        delta = delta_flat.reshape(x.shape[:-1] + (kernel.shape[-1],))
        return base_out + (SCALING * delta).astype(base_out.dtype)

    def _L1_xattn_ref(query, key, value, mask, wq, wk, wv, wo):
        import jax, jax.numpy as jnp
        import numpy as np
        N_Q_HEADS = 32
        N_KV_HEADS = 8
        D_MODEL = 512
        D_K = 128
        D_V = 128
        ROPE_BASE = 10000.0

        def _rope(x):
            d = x.shape[-1]
            s = x.shape[2]
            inv_freq = 1.0 / ROPE_BASE ** (jnp.arange(0, d, 2, dtype=jnp.float32) / d)
            ang = jnp.arange(s, dtype=jnp.float32)[:, None] * inv_freq[None, :]
            cos = jnp.concatenate([jnp.cos(ang), jnp.cos(ang)], axis=-1)[None, None]
            sin = jnp.concatenate([jnp.sin(ang), jnp.sin(ang)], axis=-1)[None, None]
            x1, x2 = (x[..., :d // 2], x[..., d // 2:])
            rot = jnp.concatenate([-x2, x1], axis=-1)
            return x * cos + rot * sin
        bs, s, _ = query.shape
        g = N_Q_HEADS // N_KV_HEADS
        q = (query @ wq).reshape(bs, s, N_Q_HEADS, D_K).transpose(0, 2, 1, 3)
        k = (key @ wk).reshape(bs, s, N_KV_HEADS, D_K).transpose(0, 2, 1, 3)
        v = (value @ wv).reshape(bs, s, N_KV_HEADS, D_V).transpose(0, 2, 1, 3)
        q = _rope(q)
        k = _rope(k)
        scale = jnp.sqrt(jnp.float32(D_K))
        qg = q.reshape(bs, N_KV_HEADS, g, s, D_K)
        scores = jnp.einsum('bhgqd,bhkd->bhgqk', qg, k) / scale
        masked = jnp.where(mask[:, None, None].astype(bool), scores, -1000000000.0)
        w = jax.nn.softmax(masked, axis=-1)
        out = jnp.einsum('bhgqk,bhkd->bhgqd', w, v)
        out = out.reshape(bs, N_Q_HEADS, s, D_V).transpose(0, 2, 1, 3).reshape(bs, s, N_Q_HEADS * D_V)
        return out @ wo

    def _L1_ffn_ref(x, router_w, A, B):
        import jax, jax.numpy as jnp
        import numpy as np
        LORA_SCALE = 16.0 / jnp.sqrt(16.0)
        TOP_K = 2
        D = x.shape[-1]
        flat = x.reshape(-1, D)
        logits = flat @ router_w.T
        topk_vals, topk_idx = jax.lax.top_k(logits, TOP_K)
        sparse = jnp.full_like(logits, -jnp.inf)
        rows = jnp.arange(logits.shape[0])[:, None]
        sparse = sparse.at[rows, topk_idx].set(topk_vals)
        gates = jax.nn.softmax(sparse, axis=-1)
        mid = jnp.einsum('tf,erf->ter', flat, A)
        all_deltas = jnp.einsum('ter,eor->teo', mid, B) * LORA_SCALE
        delta = jnp.einsum('te,teo->to', gates, all_deltas)
        return delta.reshape(*x.shape[:-1], -1)
    x = x + jnp.tanh(g_xattn[0]) * _L0_xattn_ref(_layernorm(x, axis=-1), ctx_4096, L0_xattn_Wq, L0_xattn_bq, L0_xattn_Wk, L0_xattn_bk, L0_xattn_Wv, L0_xattn_bv, L0_xattn_Wo, L0_xattn_bo)
    x = x + jnp.tanh(g_ffn[0]) * _L0_ffn_ref(_layernorm(x, axis=-1), L0_ffn_gate, L0_ffn_kernel, L0_ffn_bias, L0_ffn_lora_A, L0_ffn_lora_B, L0_ffn_lora_A_shared, L0_ffn_lora_B_shared)
    x = x + jnp.tanh(g_xattn[1]) * _L1_xattn_ref(_layernorm(x, axis=-1), ctx_4096, ctx_4096, mask_BxSxS2_ff1, L1_xattn_wq, L1_xattn_wk, L1_xattn_wv, L1_xattn_wo)
    x = x + jnp.tanh(g_ffn[1]) * _L1_ffn_ref(_layernorm(x, axis=-1), L1_ffn_router_w, L1_ffn_A, L1_ffn_B)
    return x

_drawn_inputs = setup_inputs


def setup_inputs(seed=0):
    import zlib

    import numpy as np

    out = dict(_drawn_inputs(seed))
    spreads = {'g_ffn': (-1.0, 0.6),
     'L0_xattn_bq': (0.0, 0.8),
     'L0_xattn_bk': (0.0, 0.8),
     'L0_xattn_bv': (0.0, 0.8),
     'L0_xattn_bo': (0.0, 0.1),
     'L0_ffn_bias': (0.0, 0.1)}
    factors = {'L0_xattn_Wq': 8.0,
     'L0_xattn_Wk': 8.0,
     'L0_xattn_Wv': 8.0,
     'L0_xattn_Wo': 4.696,
     'L1_xattn_wq': 3.577,
     'L1_xattn_wk': 3.545}
    for name, (base, spread) in spreads.items():
        noise = np.random.default_rng([zlib.crc32(name.encode()), seed]).standard_normal(out[name].shape)
        drawn = base * np.exp(spread * noise) if base else spread * noise
        out[name] = jnp.asarray(drawn.astype(out[name].dtype))
    for name, factor in factors.items():
        out[name] = (out[name] * factor).astype(out[name].dtype)
    return out
```

```python
from contextlib import ExitStack

import numpy as np

import concourse.bass as bass
from concourse import mybir

F32 = mybir.dt.float32
F32R = mybir.dt.float32r
ALU = mybir.AluOpType
ACT = mybir.ActivationFunctionType
AX_X = mybir.AxisListType.X

P = 128
BATCH, SEQ, D = 16, 64, 512
PAIRS = BATCH * SEQ // P
KT = D // P
EPS = 1e-5

WIN, PAD, HD0 = 16, 8, 8
ROWS0 = P // HD0
PADDED = PAD + D + WIN - PAD - 1

LORAS, RANK = 16, 32
LORA_CHUNKS = LORAS * RANK // P
HALF = P // RANK

GROUPS, GH, DK = 8, 4, 128
MASKED = -1e9
HUGE = 3e38

EXPERTS, ERANK = 4, 16
MID = EXPERTS * ERANK
LORA_SCALE = 4.0

ds = bass.ds


def after(eng, sem, value):
    if not isinstance(value, int) or value > 0:
        eng.wait_ge(sem, value)


def three_passes(pe, out, weights, moving, k_steps):
    last = None
    for k in range(k_steps):
        wh, wl = weights(k)
        mh, ml = moving(k)
        for n, (w, m) in enumerate(((wl, mh), (wh, ml), (wh, mh))):
            last = pe.matmul(out, w, m, start=(k == 0 and n == 0), stop=(k == k_steps - 1 and n == 2))
    return last


class Pool:

    def __init__(self, nc, ctx, stage):
        self.nc, self.ctx, self.stage = nc, ctx, stage

    def sb(self, name, shape, dt=F32):
        return self.ctx.enter_context(self.nc.sbuf_tensor(f"{self.stage}_{name}", shape, dt))

    def ps(self, name, shape):
        return self.ctx.enter_context(self.nc.psum_tensor(f"{self.stage}_{name}", shape, F32))

    def sem(self, name):
        return self.ctx.enter_context(self.nc.semaphore(f"{self.stage}_{name}"))


def variances(dve, steps, base, sources, stats, moments, spare):
    dve.memset(spare[:, 0:1], 0.0).then_inc(steps, 1)
    for t, src in enumerate(sources):
        last = dve.bn_stats(stats[:, t], src)
    last.then_inc(steps, 1)
    dve.wait_ge(steps, base + 2)
    dve.memset(spare[:, 1:2], 0.0).then_inc(steps, 1)
    for t in range(len(sources)):
        last = dve.bn_aggr(moments[:, t], stats[:, t])
    last.then_inc(steps, 1)
    dve.wait_ge(steps, base + 4)
    dve.tensor_scalar(moments[:, :, 1], moments[:, :, 1], EPS, None, ALU.add).then_inc(steps, 1)


def inverse_roots(dve, steps, base, moments, root, rstd, tmp):
    dve.reciprocal(rstd, root).then_inc(steps, 1)
    dve.wait_ge(steps, base + 1)
    dve.tensor_tensor(tmp, rstd, rstd, ALU.mult).then_inc(steps, 1)
    dve.wait_ge(steps, base + 2)
    dve.tensor_tensor(tmp, tmp, moments[:, :, 1], ALU.mult).then_inc(steps, 1)
    dve.wait_ge(steps, base + 3)
    dve.tensor_scalar(tmp, tmp, -0.5, 1.5, ALU.mult, ALU.add).then_inc(steps, 1)
    dve.wait_ge(steps, base + 4)
    dve.tensor_tensor(rstd, rstd, tmp, ALU.mult).then_inc(steps, 1)
    dve.wait_ge(steps, base + 5)


class RowStatistics:

    def __init__(self, al, name, tiles):
        self.stats, self.moments = al.sb(f"{name}_stats", [P, tiles, 6]), al.sb(f"{name}_moments", [P, tiles, 2])
        self.root, self.rstd, self.tmp = (al.sb(f"{name}_{n}", [P, tiles]) for n in ("root", "rstd", "tmp"))
        self.spare = al.sb(f"{name}_spare", [P, 2])
        self.steps, self.rooted = al.sem(f"{name}_steps"), al.sem(f"{name}_rooted")

    STEPS = 10

    def on_vector(self, dve, sources, turn=0):
        base = self.STEPS * turn
        after(dve, self.steps, base)
        variances(dve, self.steps, base, sources, self.stats, self.moments, self.spare)
        dve.wait_ge(self.rooted, turn + 1)
        inverse_roots(dve, self.steps, base + 5, self.moments, self.root[:], self.rstd[:], self.tmp[:])

    def on_scalar(self, act, turn=0):
        act.wait_ge(self.steps, self.STEPS * turn + 5)
        act.activation(self.root[:], self.moments[:, :, 1], ACT.Sqrt).then_inc(self.rooted, 1)

    def apply(self, dve, out, src, t):
        return dve.tensor_scalar(out, src, self.moments[:, ds(t, 1), 0], self.rstd[:, ds(t, 1)], ALU.subtract, ALU.mult)


def layer_0_attention(nc, a, x_all, ident, gates, k_dram, v_dram):
    with ExitStack() as ctx:
        al = Pool(nc, ctx, "a")
        ctx_all = al.sb("ctx_all", [P, PAIRS, D])
        ctxT = al.sb("ctxT", [P, KT, PAIRS * P])
        ctxTh = al.sb("ctxTh", [P, KT, PAIRS * P], F32R)
        ctxTl = al.sb("ctxTl", [P, KT, PAIRS * P], F32R)
        w_diag = al.sb("w_diag", [P, 4, P])
        bias = al.sb("bias", [P, 4])
        pick = al.sb("pick", [P, 15 * ROWS0])
        cosk = al.sb("cosk", [P, SEQ])
        sink = al.sb("sink", [P, SEQ])
        gbo = al.sb("gbo", [P, 1])
        xn = al.sb("xn", [P, D])
        rows = RowStatistics(al, "rows", PAIRS)
        kpad, vpad = al.sb("kpad", [P, PADDED]), al.sb("vpad", [P, PADDED])
        prod = al.sb("prod", [P, 4, D])
        sT = al.sb("sT", [P, 2, D])
        probs = al.sb("probs", [P, 4, WIN, ROWS0])
        smax, ssum = al.sb("smax", [P, 4, ROWS0]), al.sb("ssum", [P, 4, ROWS0])
        srec = al.sb("srec", [P, 4, ROWS0])
        rep = al.sb("rep", [P, 2, 4, P])
        ev = al.sb("ev", [P, 4, D])
        evp = al.sb("evp", [P, 2, D])
        otmp = al.sb("otmp", [P, D])
        land = al.sb("land", [P, 2, KT, DK])
        wh, wl = al.sb("wh", [P, 2, KT, DK], F32R), al.sb("wl", [P, 2, KT, DK], F32R)
        ksw = al.sb("ksw", [P, 2, D])
        krot = al.sb("krot", [P, 2, D])
        vrow = al.sb("vrow", [P, PAIRS, DK])

        q_ps = al.ps("q_ps", [P, D])
        k_ps = al.ps("k_ps", [P, D])
        s_ps = al.ps("s_ps", [P, 2, D])
        e_ps = [al.ps("e_ps0", [P, D]), al.ps("e_ps1", [P, D])]
        kv_ps = [al.ps("kv_ps0", [P, D]), al.ps("kv_ps1", [P, D])]
        po = q_ps

        s = {n: al.sem(n) for n in (
            "x_in", "ctx_in", "ctxT_in", "small_in", "wkv_in", "zeroed", "w_in", "gate", "ctx_hi", "ctx_lo",
            "ln", "l0q", "l0k", "l0v", "k_ev", "v_ev", "prod", "score", "sT_ev", "sc", "mx", "sub", "expd",
            "ssum", "srec", "norm", "rep", "e", "ev", "evp", "osum", "o_ev", "x_add",
            "whi", "wlo", "k0", "k1", "v0", "v1", "ksw", "kcos", "kt2", "kready", "v0_ev", "v1_ev",
            "k_st", "v_st")}

        wkv = [a["wk"].rearrange("(k p) n -> p k n", p=P), a["wv"].rearrange("(k p) n -> p k n", p=P)]
        block = ctx.enter_context(nc.Block())

        @block.sync
        def _(sp):
            sp.wait_ge(s["zeroed"], 1)
            for n, name in enumerate(("WqT", "WkT", "WvT", "WoT")):
                for h in (0, 64):
                    sp.dma_start(w_diag[h:h + 64, n, h:h + 64], a[name]).then_inc(s["w_in"], 16)
            for n, name in enumerate(("bq", "bk", "bv", "bo")):
                for h in (0, 64):
                    sp.dma_start(bias[h:h + 64, n:n + 1], a[name]).then_inc(s["small_in"], 16)
            sp.dma_start(gates[:, 0:2], a["g_xattn"].partition_broadcast(P)).then_inc(s["small_in"], 16)
            sp.dma_start(gates[:, 2:4], a["g_ffn"].partition_broadcast(P)).then_inc(s["small_in"], 16)
            sp.dma_start(cosk[:], a["cosk"]).then_inc(s["small_in"], 16)
            sp.dma_start(sink[:], a["sink"]).then_inc(s["small_in"], 16)
            sp.dma_start(pick[:], a["pick"]).then_inc(s["small_in"], 16)
            sp.dma_start(ident[:], a["ident"]).then_inc(s["small_in"], 16)
            sp.dma_start(ctx_all[:], a["ctx"].rearrange("(t p) d -> p t d", p=P)).then_inc(s["ctx_in"], 16)
            sp.dma_start(x_all[:], a["x"].rearrange("(t p) d -> p t d", p=P)).then_inc(s["x_in"], 16)

            def load(g):
                after(sp, s["wlo"], 2 * g)
                for n in range(2):
                    sp.dma_start(land[:, n], wkv[n][:, :, ds(g * DK, DK)]).then_inc(s["wkv_in"], 16)

            def store(g):
                sp.wait_ge(s["kready"], 2 * g + 2)
                sp.dma_start(k_dram[ds(g, 1)].rearrange("o p n -> p (o n)"),
                             krot[:].rearrange("p h n -> p (h n)")).then_inc(s["k_st"], 16)
                sp.wait_ge(s["v1_ev"], g + 1)
                sp.dma_start(v_dram[ds(g, 1)].rearrange("o p n -> p (o n)"),
                             vrow[:].rearrange("p t n -> p (t n)")).then_inc(s["v_st"], 16)

            load(0)
            sp.dma_start(ctxT[:], a["ctxT"].rearrange("(k p) t -> p k t", p=P)).then_inc(s["ctxT_in"], 16)
            load(1)
            store(0)
            with sp.Fori(1, GROUPS - 1) as g:
                load(g + 1)
                store(g)
            store(GROUPS - 1)
            sp.wait_ge(s["k_st"], 16 * GROUPS)
            sp.wait_ge(s["v_st"], 16 * GROUPS)

        @block.scalar
        def _(act):
            act.wait_ge(s["small_in"], 16 * 14)
            act.activation(gates[:], gates[:], ACT.Tanh).then_inc(s["gate"], 1)
            act.wait_ge(s["gate"], 1)
            act.activation(gbo[:], bias[:, 3:4], ACT.Copy, scale=gates[:, 0:1]).then_inc(s["gate"], 1)
            act.wait_ge(s["gate"], 2)
            rows.on_scalar(act)
            act.wait_ge(s["zeroed"], 3)
            act.wait_ge(s["ctxT_in"], 16)
            for k in range(KT):
                act.activation(ctxTh[:, k], ctxT[:, k], ACT.Copy).then_inc(s["ctx_hi"], 1)
            def pair(p):
                act.wait_ge(s["wkv_in"], 32 * p + 32)
                after(act, s["v1"], p)
                for n in range(2):
                    act.activation(wh[:, n], land[:, n], ACT.Copy).then_inc(s["whi"], 1)
                act.wait_ge(s["l0k"], p + 1)
                after(act, s["prod"], WIN * p)
                act.activation(kpad[:, PAD:PAD + D], k_ps[:], ACT.Identity, bias=bias[:, 1:2]).then_inc(s["k_ev"], 1)
                act.wait_ge(s["l0v"], p + 1)
                after(act, s["ev"], WIN * p)
                act.activation(vpad[:, PAD:PAD + D], kv_ps[0][:], ACT.Identity, bias=bias[:, 2:3]).then_inc(s["v_ev"], 1)
                for h, ready in ((0, "k0"), (1, "k1")):
                    act.wait_ge(s[ready], p + 1)
                    after(act, s["kready"], 2 * p)
                    act.activation(ksw[0:64, h], kv_ps[1 - h][64:128, :], ACT.Copy).then_inc(s["ksw"], 1)
                    act.activation(ksw[64:128, h], kv_ps[1 - h][0:64, :], ACT.Copy).then_inc(s["ksw"], 1)
                    act.wait_ge(s["score"], WIN * p + 8 * h + 8)
                    after(act, s["sc"], p)
                    act.activation(sT[:, h], s_ps[:, h], ACT.Copy).then_inc(s["sT_ev"], 1)
                act.wait_ge(s["v0"], p + 1)
                after(act, s["v_st"], 16 * p)
                act.activation(vrow[:, 0:4].rearrange("p t n -> p (t n)"), kv_ps[1][:], ACT.Copy).then_inc(s["v0_ev"], 1)
                act.wait_ge(s["v1"], p + 1)
                act.activation(vrow[:, 4:8].rearrange("p t n -> p (t n)"), kv_ps[0][:], ACT.Copy).then_inc(s["v1_ev"], 1)
                act.wait_ge(s["sub"], p + 1)
                act.activation(probs[:], probs[:], ACT.Exp, scale=float(HD0) ** -0.5).then_inc(s["expd"], 1)
                act.wait_ge(s["norm"], p + 1)
                for w in range(WIN):
                    after(act, s["e"], WIN * p + max(w - 1, 0))
                    act.activation(rep[:, w % 2].rearrange("p t (h c) -> p t h c", c=HD0),
                                   probs[:, :, w, :].rearrange("p t (h o) -> p t h o", o=1)
                                   .broadcast_to([P, 4, ROWS0, HD0]), ACT.Copy).then_inc(s["rep"], 1)
                act.wait_ge(s["osum"], 8 * p + 8)
                after(act, s["x_add"], p)
                act.activation(otmp[:], po[:], ACT.Identity, bias=gbo[:], scale=gates[:, 0:1]).then_inc(s["o_ev"], 1)

            pair(0)
            with act.Fori(1, PAIRS) as p:
                pair(p)

        @block.gpsimd
        def _(pool):
            pool.memset(w_diag[:], 0.0).then_inc(s["zeroed"], 1)
            pool.memset(kpad[:], 0.0).then_inc(s["zeroed"], 1)
            pool.memset(vpad[:], 0.0).then_inc(s["zeroed"], 1)
            pool.wait_ge(s["small_in"], 16 * 14)
            def pair(p):
                after(pool, s["v1"], p)
                for n in range(2):
                    pool.wait_ge(s["whi"], 2 * p + n + 1)
                    pool.tensor_tensor(wl[:, n], land[:, n], wh[:, n].bitcast(F32), ALU.subtract).then_inc(s["wlo"], 1)
                for h in range(2):
                    pool.wait_ge(s["ksw"], 4 * p + 2 * h + 2)
                    kv = ksw[:, h].rearrange("p (b q) -> p b q", q=SEQ)
                    pool.tensor_tensor(kv, kv, sink[:].rearrange("p (o q) -> p o q", o=1)
                                       .broadcast_to([P, D // SEQ, SEQ]), ALU.mult).then_inc(s["kt2"], 1)
                    pool.wait_ge(s["kt2"], 2 * p + h + 1)
                    pool.wait_ge(s["kcos"], 2 * p + h + 1)
                    pool.tensor_tensor(krot[:, h], krot[:, h], ksw[:, h], ALU.add).then_inc(s["kready"], 1)
                for j in range(WIN // 2):
                    pool.wait_ge(s["ev"], WIN * p + 2 * j + 2)
                    after(pool, s["osum"], 8 * p + max(j - 1, 0))
                    pool.tensor_tensor(evp[:, j % 2], ev[:, 2 * j % 4], ev[:, (2 * j + 1) % 4], ALU.add)\
                        .then_inc(s["evp"], 1)
                pool.wait_ge(s["o_ev"], p + 1)
                xp = x_all[:, ds(p, 1), :].rearrange("p o d -> p (o d)")
                pool.tensor_tensor(xp, xp, otmp[:], ALU.add).then_inc(s["x_add"], 1)

            pair(0)
            with pool.Fori(1, PAIRS) as p:
                pair(p)

        @block.vector
        def _(dve):
            dve.wait_ge(s["x_in"], 16)
            rows.on_vector(dve, [x_all[:, t] for t in range(PAIRS)])
            dve.wait_ge(s["ctxT_in"], 16)
            for k in range(KT):
                dve.wait_ge(s["ctx_hi"], k + 1)
                dve.tensor_tensor(ctxTl[:, k], ctxT[:, k], ctxTh[:, k].bitcast(F32), ALU.subtract).then_inc(s["ctx_lo"], 1)
            dve.wait_ge(s["zeroed"], 3)
            dve.wait_ge(s["small_in"], 16 * 14)

            def k_cos(p, h):
                dve.wait_ge(s["ksw"], 4 * p + 2 * h + 2)
                after(dve, s["k_st"], 16 * p)
                dve.tensor_tensor(krot[:, h].rearrange("p (b q) -> p b q", q=SEQ),
                                  kv_ps[1 - h][:].rearrange("p (b q) -> p b q", q=SEQ),
                                  cosk[:].rearrange("p (o q) -> p o q", o=1).broadcast_to([P, D // SEQ, SEQ]),
                                  ALU.mult).then_inc(s["kcos"], 1)

            def pair(p):
                after(dve, s["l0q"], p)
                rows.apply(dve, xn[:], x_all[:, ds(p, 1), :].rearrange("p o d -> p (o d)"), p).then_inc(s["ln"], 1)
                k_cos(p, 0)
                dve.wait_ge(s["l0q"], p + 1)
                dve.wait_ge(s["k_ev"], p + 1)
                for w in range(WIN):
                    after(dve, s["score"], WIN * p + max(w - 3, 0))
                    dve.scalar_tensor_tensor(prod[:, w % 4], q_ps[:], bias[:, 0:1], kpad[:, w:w + D],
                                             ALU.add, ALU.mult).then_inc(s["prod"], 1)
                    if w == 10:
                        k_cos(p, 1)
                scores = s_ps[:].rearrange("p h n -> p (h n)").rearrange("p (t w r) -> p t w r", t=4, w=WIN)
                dve.wait_ge(s["sc"], p + 1)
                dve.tensor_reduce(smax[:], scores.rearrange("p t w r -> p t r w"), AX_X, ALU.max).then_inc(s["mx"], 1)
                dve.wait_ge(s["mx"], p + 1)
                after(dve, s["rep"], WIN * p)
                for t in range(4):
                    last = dve.tensor_tensor(probs[:, t], scores[:, t], smax[:, t:t + 1, :].broadcast_to([P, WIN, ROWS0]),
                                             ALU.subtract)
                last.then_inc(s["sub"], 1)
                dve.wait_ge(s["expd"], p + 1)
                dve.tensor_reduce(ssum[:], probs[:].rearrange("p t w r -> p t r w"), AX_X, ALU.add).then_inc(s["ssum"], 1)
                dve.wait_ge(s["ssum"], p + 1)
                dve.reciprocal(srec[:], ssum[:]).then_inc(s["srec"], 1)
                dve.wait_ge(s["srec"], p + 1)
                for t in range(4):
                    last = dve.tensor_tensor(probs[:, t], probs[:, t], srec[:, t:t + 1, :].broadcast_to([P, WIN, ROWS0]),
                                             ALU.mult)
                last.then_inc(s["norm"], 1)
                dve.wait_ge(s["v_ev"], p + 1)
                for w in range(WIN):
                    dve.wait_ge(s["e"], WIN * p + w + 1)
                    if w % 2 == 0:
                        after(dve, s["evp"], 8 * p + max(w // 2 - 1, 0))
                    dve.tensor_tensor(ev[:, w % 4], e_ps[w % 2][:], vpad[:, w:w + D], ALU.mult).then_inc(s["ev"], 1)

            pair(0)
            with dve.Fori(1, PAIRS) as p:
                pair(p)

        @block.tensor
        def _(pe):
            pe.wait_ge(s["w_in"], 16 * 8)
            pe.wait_ge(s["small_in"], 16 * 14)
            pe.wait_ge(s["ctx_in"], 16)
            pe.wait_ge(s["ctx_lo"], KT)

            def k_proj(h):
                return three_passes(pe, kv_ps[1 - h][:], lambda k: (wh[:, 0, k], wl[:, 0, k]),
                                    lambda k: (ctxTh[:, k, h * D:h * D + D], ctxTl[:, k, h * D:h * D + D]), KT)

            def v_proj(h):
                for t in range(4):
                    c = slice((4 * h + t) * P, (4 * h + t + 1) * P)
                    last = three_passes(pe, kv_ps[1 - h][:, t * DK:t * DK + DK],
                                        lambda k: (ctxTh[:, k, c], ctxTl[:, k, c]),
                                        lambda k: (wh[:, 1, k], wl[:, 1, k]), KT)
                return last

            def pair(p):
                ctx_p = ctx_all[:, ds(p, 1), :].rearrange("p o d -> p (o d)")
                after(pe, s["k_ev"], p)
                pe.matmul(k_ps[:], w_diag[:, 1], ctx_p, start=True, stop=True).then_inc(s["l0k"], 1)
                after(pe, s["v1_ev"], p)
                pe.matmul(kv_ps[0][:], w_diag[:, 2], ctx_p, start=True, stop=True).then_inc(s["l0v"], 1)
                pe.wait_ge(s["wlo"], 2 * p + 2)
                after(pe, s["v0_ev"], p)
                k_proj(0).then_inc(s["k0"], 1)
                pe.wait_ge(s["ln"], p + 1)
                after(pe, s["o_ev"], p)
                pe.matmul(q_ps[:], w_diag[:, 0], xn[:], start=True, stop=True).then_inc(s["l0q"], 1)
                for w in range(WIN):
                    pe.wait_ge(s["prod"], WIN * p + w + 1)
                    if w == 0:
                        after(pe, s["sub"], p)
                    c = (7 - w % 8) * ROWS0
                    pe.matmul(s_ps[:, w // 8], pick[:, c:c + P], prod[:, w % 4], start=(w % 8 == 0),
                              stop=(w % 8 == 7)).then_inc(s["score"], 1)
                    if w == 7:
                        pe.wait_ge(s["v_ev"], p + 1)
                        k_proj(1).then_inc(s["k1"], 1)
                pe.wait_ge(s["ksw"], 4 * p + 2)
                pe.wait_ge(s["kcos"], 2 * p + 1)
                v_proj(0).then_inc(s["v0"], 1)
                pe.wait_ge(s["sT_ev"], 2 * p + 2)
                for t in range(4):
                    for h in range(2):
                        c = (2 * (t % 2) + h) * P
                        last = pe.transpose(s_ps[:, t // 2, c:c + P], sT[:, h, t * P:t * P + P], ident[:])
                last.then_inc(s["sc"], 1)
                pe.wait_ge(s["ksw"], 4 * p + 4)
                pe.wait_ge(s["kcos"], 2 * p + 2)
                v_proj(1).then_inc(s["v1"], 1)

                def out_sum(j):
                    pe.wait_ge(s["evp"], 8 * p + j + 1)
                    pe.matmul(po[:], w_diag[:, 3], evp[:, j % 2], start=(j == 0), stop=(j == WIN // 2 - 1))\
                        .then_inc(s["osum"], 1)

                for w in range(WIN):
                    pe.wait_ge(s["rep"], WIN * p + w + 1)
                    after(pe, s["ev"], WIN * p + max(w - 1, 0))
                    for t in range(4):
                        last = pe.transpose(e_ps[w % 2][:, t * P:t * P + P], rep[:, w % 2, t], ident[:])
                    last.then_inc(s["e"], 1)
                    if w % 2 and w >= 5:
                        out_sum((w - 5) // 2)
                out_sum(6)
                out_sum(7)

            pair(0)
            with pe.Fori(1, PAIRS) as p:
                pair(p)


def layer_0_ffn(nc, a, x_all, ident, gates, xTh, xTl):
    with ExitStack() as ctx:
        al = Pool(nc, ctx, "f")
        kern = al.sb("kern", [P, KT, D])
        lora_a = al.sb("lora_a", [P, LORA_CHUNKS, D])
        lora_b = al.sb("lora_b", [P, LORA_CHUNKS, D])
        gcol = al.sb("gcol", [P, LORA_CHUNKS, PAIRS])
        eye_r = al.sb("eye_r", [P, RANK])
        mix = al.sb("mix", [P, LORA_CHUNKS, PAIRS, RANK])
        a_shared = al.sb("a_shared", [P, KT, RANK])
        b_shared = al.sb("b_shared", [RANK + 1, D])
        own = al.sb("own", [P, HALF])
        a_eff = al.sb("a_eff", [P, KT, 2, P])
        b_eff = al.sb("b_eff", [P, 2, D])
        xn, xn2 = al.sb("xn", [P, D]), al.sb("xn2", [P, D])
        rows, rows2 = RowStatistics(al, "rows", PAIRS), RowStatistics(al, "rows2", 1)
        xnT = al.sb("xnT", [P, KT, P])
        ax = al.sb("ax", [P, P])
        axs = al.sb("axs", [RANK + 1, P])

        t1_ps = al.ps("t1_ps", [P, KT, P])
        ax_ps = al.ps("ax_ps", [P, P])
        axs_ps = al.ps("axs_ps", [RANK, P])
        out_ps = [al.ps("out_ps0", [P, D]), al.ps("out_ps1", [P, D])]
        t2_ps = al.ps("t2_ps", [P, KT, P])
        s = {n: al.sem(n) for n in (
            "in", "mix", "eff", "eff_ev", "ln", "t1", "t1_ev", "ax", "ax_ev", "axs_ev", "out", "x2", "ln2",
            "t2", "hi", "lo", "ones")}
        N_IN = 8
        block = ctx.enter_context(nc.Block())

        @block.sync
        def _(sp):
            sp.dma_start(gcol[:], a["gate"].rearrange("(c p) b -> p c b", p=P)).then_inc(s["in"], 16)
            sp.dma_start(eye_r[:], a["eye_r"]).then_inc(s["in"], 16)
            sp.dma_start(own[:], a["own"]).then_inc(s["in"], 16)
            sp.dma_start(lora_a[:], a["lora_A"].rearrange("(c p) i -> p c i", p=P)).then_inc(s["in"], 16)
            sp.dma_start(lora_b[:], a["lora_B"].rearrange("(c p) o -> p c o", p=P)).then_inc(s["in"], 16)
            sp.dma_start(a_shared[:], a["A_shared"].rearrange("(k p) r -> p k r", p=P)).then_inc(s["in"], 16)
            sp.dma_start(b_shared[:], a["B_shared"]).then_inc(s["in"], 16)
            sp.dma_start(kern[:], a["kernel"].rearrange("(k p) o -> p k o", p=P)).then_inc(s["in"], 16)

        @block.gpsimd
        def _(pool):
            pool.memset(axs[RANK:RANK + 1, :], 1.0).then_inc(s["ones"], 1)

        @block.scalar
        def _(act):
            rows.on_scalar(act)
            for k in range(KT):
                act.wait_ge(s["eff"], k + 1)
                act.activation(a_eff[:, k], (out_ps[k % 2][:, 0:2 * P]).rearrange("p (h n) -> p h n", h=2),
                               ACT.Copy).then_inc(s["eff_ev"], 1)
            for h in range(2):
                act.wait_ge(s["eff"], KT + h + 1)
                act.activation(b_eff[:, h], out_ps[h][:], ACT.Copy).then_inc(s["eff_ev"], 1)

            def first(p):
                act.wait_ge(s["t1"], p + 1)
                after(act, s["out"], p)
                act.activation(xnT[:], t1_ps[:], ACT.Copy).then_inc(s["t1_ev"], 1)
                act.wait_ge(s["ax"], p + 1)
                act.activation(axs[0:RANK, :], axs_ps[:], ACT.Copy).then_inc(s["axs_ev"], 1)

            def second(p):
                rows2.on_scalar(act, p)
                act.wait_ge(s["t2"], p + 1)
                act.activation(xTh[:, :, ds(p * P, P)], t2_ps[:], ACT.Copy).then_inc(s["hi"], 1)

            first(0)
            with act.Fori(1, PAIRS) as p:
                first(p)
                second(p - 1)
            second(PAIRS - 1)

        @block.vector
        def _(dve):
            rows.on_vector(dve, [x_all[:, t] for t in range(PAIRS)])
            dve.wait_ge(s["in"], 16 * N_IN)
            for c in range(LORA_CHUNKS):
                dve.tensor_tensor(mix[:, c], gcol[:, c].rearrange("p (b o) -> p b o", o=1).broadcast_to([P, PAIRS, RANK]),
                                  eye_r[:].rearrange("p (o r) -> p o r", o=1).broadcast_to([P, PAIRS, RANK]),
                                  ALU.mult).then_inc(s["mix"], 1)

            def norm(p):
                after(dve, s["t1"], p)
                rows.apply(dve, xn[:], x_all[:, ds(p, 1), :].rearrange("p o d -> p (o d)"), p).then_inc(s["ln"], 1)

            def middle(p, q):
                dve.wait_ge(s["ax"], p + 1)
                after(dve, s["out"], p)
                dve.tensor_scalar(ax[:], ax_ps[:], own[:, ds(q, 1)], None, ALU.mult).then_inc(s["ax_ev"], 1)

            def update(p):
                xp = x_all[:, ds(p, 1), :].rearrange("p o d -> p (o d)")
                dve.wait_ge(s["out"], p + 1)
                dve.scalar_tensor_tensor(xp, out_ps[0][:], gates[:, 2:3], xp, ALU.mult, ALU.add).then_inc(s["x2"], 1)
                dve.wait_ge(s["x2"], p + 1)
                after(dve, s["t2"], p)
                rows2.on_vector(dve, [xp], p)
                rows2.apply(dve, xn2[:], xp, 0).then_inc(s["ln2"], 1)

            def low(p):
                dve.wait_ge(s["hi"], p + 1)
                cols = ds(p * P, P)
                dve.tensor_tensor(xTl[:, :, cols], t2_ps[:], xTh[:, :, cols].bitcast(F32), ALU.subtract)\
                    .then_inc(s["lo"], 1)

            def tile(p, q, more):
                middle(p, q)
                if more:
                    norm(p + 1)
                update(p)
                low(p)

            norm(0)
            tile(0, 0, True)
            with dve.Fori(1, HALF) as q:
                tile(q, q, True)
            with dve.Fori(0, HALF - 1) as q:
                tile(q + HALF, q, True)
            tile(PAIRS - 1, HALF - 1, False)

        @block.tensor
        def _(pe):
            pe.wait_ge(s["mix"], LORA_CHUNKS)
            for k in range(KT):
                after(pe, s["eff_ev"], max(k - 1, 0))
                for h in range(2):
                    for c in range(LORA_CHUNKS):
                        last = pe.matmul(out_ps[k % 2][:, h * P:h * P + P], lora_a[:, c, k * P:k * P + P],
                                         mix[:, c, h * HALF:h * HALF + HALF].rearrange("p b r -> p (b r)"),
                                         start=(c == 0), stop=(c == LORA_CHUNKS - 1))
                last.then_inc(s["eff"], 1)
            for h in range(2):
                pe.wait_ge(s["eff_ev"], KT - 1 + h)
                for c in range(LORA_CHUNKS):
                    last = pe.matmul(out_ps[h][:], mix[:, c, h * HALF:h * HALF + HALF].rearrange("p b r -> p (b r)"),
                                     lora_b[:, c], start=(c == 0), stop=(c == LORA_CHUNKS - 1))
                last.then_inc(s["eff"], 1)
            pe.wait_ge(s["eff_ev"], KT + 2)
            pe.wait_ge(s["ones"], 1)

            def first(p, h):
                pe.wait_ge(s["ln"], p + 1)
                after(pe, s["t1_ev"], p)
                for k in range(KT):
                    last = pe.transpose(t1_ps[:, k], xn[:, k * P:k * P + P], ident[:])
                last.then_inc(s["t1"], 1)
                pe.wait_ge(s["t1_ev"], p + 1)
                after(pe, s["ax_ev"], p)
                for k in range(KT):
                    pe.matmul(ax_ps[:], a_eff[:, k, h], xnT[:, k], start=(k == 0), stop=(k == KT - 1))
                after(pe, s["axs_ev"], p)
                for k in range(KT):
                    last = pe.matmul(axs_ps[:], a_shared[:, k], xnT[:, k], start=(k == 0), stop=(k == KT - 1))
                last.then_inc(s["ax"], 1)
                after(pe, s["x2"], p)
                for k in range(KT):
                    pe.matmul(out_ps[0][:], xnT[:, k], kern[:, k], start=(k == 0), stop=False)

            def second(p):
                pe.wait_ge(s["ln2"], p + 1)
                after(pe, s["lo"], p)
                for k in range(KT):
                    last = pe.transpose(t2_ps[:, k], xn2[:, k * P:k * P + P], ident[:])
                last.then_inc(s["t2"], 1)

            def third(p, h):
                pe.wait_ge(s["ax_ev"], p + 1)
                pe.matmul(out_ps[0][:], ax[:], b_eff[:, h], start=False, stop=False)
                pe.wait_ge(s["axs_ev"], p + 1)
                pe.matmul(out_ps[0][:], axs[:], b_shared[:], start=False, stop=True).then_inc(s["out"], 1)

            first(0, 0)
            third(0, 0)
            first(1, 0)
            second(0)
            third(1, 0)
            for h, begin, end in ((0, 2, HALF), (1, HALF, PAIRS)):
                with pe.Fori(begin, end) as p:
                    first(p, h)
                    second(p - 1)
                    third(p, h)
            second(PAIRS - 1)


def layer_1_attention(nc, a, x_all, gates, ident, xTh, xTl, k_dram, v_dram):
    with ExitStack() as ctx:
        al = Pool(nc, ctx, "g")
        cosq, sinq = al.sb("cosq", [P, SEQ]), al.sb("sinq", [P, SEQ])
        cap = al.sb("cap", [P, PAIRS, 2, SEQ])
        wq_land = al.sb("wq_land", [P, KT, GH * DK])
        wqh, wql = al.sb("wqh", [P, KT, GH * DK], F32R), al.sb("wql", [P, KT, GH * DK], F32R)
        wo_land = al.sb("wo_land", [P, GH, D])
        woh, wol = al.sb("woh", [P, GH, D], F32R), al.sb("wol", [P, GH, D], F32R)
        kT = al.sb("kT", [P, PAIRS * P])
        vr = al.sb("vr", [P, PAIRS, DK])
        qT = al.sb("qT", [P, BATCH, GH, SEQ])
        qcos, qsw = al.sb("qcos", [P, 2, D]), al.sb("qsw", [P, 2, D])
        S = al.sb("S", [P, PAIRS, 2, P])
        smax, ssum, srec = (al.sb(n, [P, PAIRS, 4]) for n in ("smax", "ssum", "srec"))
        PT = al.sb("PT", [P, PAIRS, 2 * P])
        oh, ol = al.sb("oh", [P, 2, GH, P], F32R), al.sb("ol", [P, 2, GH, P], F32R)

        a_ps = [al.ps("a_ps0", [P, D]), al.ps("a_ps1", [P, D])]
        s_ps = [al.ps("s_ps0", [P, D]), al.ps("s_ps1", [P, D])]
        o_ps = [[al.ps(f"o_ps{r}{b}", [P, D]) for b in range(2)] for r in range(2)]
        s = {n: al.sem(n) for n in (
            "tab_in", "mask_in", "cap0", "wq_in", "wo_in", "k_in", "v_in", "wq_hi", "wq_lo", "wo_hi", "wo_lo",
            "q", "qsw", "qcos", "qsin", "qrot", "score", "cap", "mx", "sub", "expd", "ssum", "srec", "norm",
            "t", "pt", "av", "ohi", "olo", "wo", "x")}
        wq_view = a["wq"].rearrange("(k p) n -> p k n", p=P)
        wo_view = a["wo"].rearrange("(h p) n -> p h n", p=P)
        QT = 2 * GH
        CH = 4
        per_seq = "p (b q) -> p b q"
        block = ctx.enter_context(nc.Block())

        @block.sync
        def _(sp):
            def load_wq(g):
                after(sp, s["wq_lo"], KT * g)
                sp.dma_start(wq_land[:], wq_view[:, :, ds(g * (GH * DK), GH * DK)]).then_inc(s["wq_in"], 16)

            def load_wo(g):
                after(sp, s["wo_lo"], GH * g)
                sp.dma_start(wo_land[:], wo_view[:, ds(g * GH, GH), :]).then_inc(s["wo_in"], 16)

            def load_k(g):
                after(sp, s["score"], CH * g)
                sp.dma_start(kT[:], k_dram[ds(g, 1)].rearrange("o p n -> p (o n)")).then_inc(s["k_in"], 16)

            def load_v(g):
                after(sp, s["av"], PAIRS * g)
                sp.dma_start(vr[:].rearrange("p t n -> p (t n)"),
                             v_dram[ds(g, 1)].rearrange("o p n -> p (o n)")).then_inc(s["v_in"], 16)

            load_wq(0)
            sp.dma_start(cosq[:], a["cosq"]).then_inc(s["tab_in"], 16)
            sp.dma_start(sinq[:], a["sinq"]).then_inc(s["tab_in"], 16)
            for h in (0, 64):
                sp.dma_start(cap[h:h + 64].rearrange("p t b k -> p (t b) k"), a["mask"].rearrange("b q k -> q b k"))\
                  .then_inc(s["mask_in"], 16)
            load_k(0)
            load_wo(0)
            load_v(0)
            load_wq(1)

            def group(g, wq=True):
                if wq:
                    load_wq(g + 2)
                load_k(g + 1)
                load_wo(g + 1)
                load_v(g + 1)

            group(0)
            with sp.Fori(1, GROUPS - 2) as g:
                group(g)
            group(GROUPS - 2, wq=False)

        @block.scalar
        def _(act):
            def split_wq(g):
                act.wait_ge(s["wq_in"], 16 * g + 16)
                after(act, s["q"], QT * g)
                for k in range(KT):
                    act.activation(wqh[:, k], wq_land[:, k], ACT.Copy).then_inc(s["wq_hi"], 1)

            def swap(g, i):
                n = QT * g + i
                act.wait_ge(s["q"], n + 1)
                if i >= 2 or not isinstance(g, int) or g > 0:
                    act.wait_ge(s["qrot"], n - 1)
                for h in (0, 64):
                    act.activation(qsw[h:h + 64, i % 2], a_ps[i % 2][64 - h:128 - h, :], ACT.Copy)\
                       .then_inc(s["qsw"], 1)

            def exp(g, c):
                act.wait_ge(s["sub"], CH * g + c + 1)
                t = S[:, 2 * c:2 * c + 2]
                act.activation(t, t, ACT.Exp).then_inc(s["expd"], 1)

            def group(g, q=True, wq=True):
                act.wait_ge(s["wo_in"], 16 * g + 16)
                after(act, s["wo"], PAIRS * g)
                for h in range(GH):
                    act.activation(woh[:, h], wo_land[:, h], ACT.Copy).then_inc(s["wo_hi"], 1)
                for i in range(QT):
                    if q:
                        swap(g + 1, i)
                    if 1 <= i <= CH:
                        exp(g, i - 1)
                if wq:
                    split_wq(g + 2)

                def out_high(t):
                    act.wait_ge(s["av"], PAIRS * g + t + 1)
                    after(act, s["wo"], PAIRS * g + max(t - 1, 0))
                    for b in range(2):
                        act.activation(oh[:, t % 2, :, b * SEQ:b * SEQ + SEQ],
                                       o_ps[t % 2][b][:, 0:GH * SEQ].rearrange("p (h q) -> p h q", h=GH),
                                       ACT.Copy).then_inc(s["ohi"], 1)

                for t in range(PAIRS):
                    act.wait_ge(s["t"], PAIRS * g + t + 1)
                    act.activation(PT[:, t], s_ps[t % 2][:, 0:2 * P], ACT.Copy).then_inc(s["pt"], 1)
                    if t:
                        out_high(t - 1)
                out_high(PAIRS - 1)

            split_wq(0)
            for i in range(QT):
                swap(0, i)
            split_wq(1)
            group(0)
            with act.Fori(1, GROUPS - 2) as g:
                group(g)
            group(GROUPS - 2, wq=False)
            group(GROUPS - 1, q=False, wq=False)

        @block.gpsimd
        def _(pool):
            def split_wq(g):
                after(pool, s["q"], QT * g)
                for k in range(KT):
                    pool.wait_ge(s["wq_hi"], KT * g + k + 1)
                    pool.tensor_tensor(wql[:, k], wq_land[:, k], wqh[:, k].bitcast(F32), ALU.subtract)\
                        .then_inc(s["wq_lo"], 1)

            def sine(g, i):
                n = QT * g + i
                pool.wait_ge(s["qsw"], 2 * n + 2)
                t = qsw[:, i % 2].rearrange(per_seq, q=SEQ)
                pool.tensor_tensor(t, t, sinq[:].rearrange("p (o q) -> p o q", o=1).broadcast_to([P, D // SEQ, SEQ]),
                                   ALU.mult).then_inc(s["qsin"], 1)

            def group(g, q=True, wq=True):
                after(pool, s["wo"], PAIRS * g)
                for h in range(GH):
                    pool.wait_ge(s["wo_hi"], GH * g + h + 1)
                    pool.tensor_tensor(wol[:, h], wo_land[:, h], woh[:, h].bitcast(F32), ALU.subtract)\
                        .then_inc(s["wo_lo"], 1)
                if q:
                    for i in range(QT):
                        sine(g + 1, i)
                if wq:
                    split_wq(g + 2)

            pool.wait_ge(s["tab_in"], 32)
            split_wq(0)
            for i in range(QT):
                sine(0, i)
            split_wq(1)
            group(0)
            with pool.Fori(1, GROUPS - 2) as g:
                group(g)
            group(GROUPS - 2, wq=False)
            group(GROUPS - 1, q=False, wq=False)

        @block.vector
        def _(dve):
            dve.wait_ge(s["tab_in"], 32)
            dve.wait_ge(s["mask_in"], 32)
            flat = cap[:].rearrange("p t b k -> p (t b k)")
            dve.tensor_scalar(flat, flat, 0.0, HUGE, ALU.not_equal, ALU.mult).then_inc(s["cap0"], 1)
            dve.wait_ge(s["cap0"], 1)
            dve.tensor_scalar(flat, flat, MASKED, None, ALU.add).then_inc(s["cap0"], 1)
            dve.wait_ge(s["cap0"], 2)

            def cosine(g, i):
                n = QT * g + i
                dve.wait_ge(s["qsw"], 2 * n + 2)
                dve.tensor_tensor(qcos[:, i % 2].rearrange(per_seq, q=SEQ), a_ps[i % 2][:].rearrange(per_seq, q=SEQ),
                                  cosq[:].rearrange("p (o q) -> p o q", o=1).broadcast_to([P, D // SEQ, SEQ]),
                                  ALU.mult).then_inc(s["qcos"], 1)

            def rotate(g, i):
                n = QT * g + i
                if i == 0:
                    after(dve, s["score"], CH * g)
                dve.wait_ge(s["qcos"], n + 1)
                dve.wait_ge(s["qsin"], n + 1)
                h, half = i // 2, i % 2
                dve.tensor_tensor(qT[:, half * 8:half * 8 + 8, h, :], qcos[:, i % 2].rearrange(per_seq, q=SEQ),
                                  qsw[:, i % 2].rearrange(per_seq, q=SEQ), ALU.add).then_inc(s["qrot"], 1)

            def rows(t, c):
                return t[:, 2 * c:2 * c + 2].rearrange("p t n -> p (t n)").rearrange("p (n o) -> p n o", o=1)\
                    .broadcast_to([P, 8, SEQ])

            def chunk(c):
                return S[:, 2 * c:2 * c + 2].rearrange("p t h n -> p (t h n)").rearrange("p (n k) -> p n k", k=SEQ)

            def stat(t, c):
                return t[:, 2 * c:2 * c + 2].rearrange("p t n -> p (t n)")

            def group(g, q=True):
                after(dve, s["t"], PAIRS * g)
                for c in range(CH):
                    dve.wait_ge(s["score"], CH * g + c + 1)
                    for t in range(2):
                        last = dve.tensor_tensor(
                            S[:, 2 * c + t], s_ps[c % 2][:, t * 2 * P:(t + 1) * 2 * P].rearrange("p (h n) -> p h n", h=2),
                            cap[:, 2 * c + t].rearrange("p b k -> p (b k)").rearrange("p (o n) -> p o n", o=1)
                            .broadcast_to([P, 2, P]), ALU.min)
                    last.then_inc(s["cap"], 1)
                for i in range(QT + 1):
                    if q and i < QT:
                        cosine(g + 1, i)
                    if i < CH:
                        c = i
                        dve.wait_ge(s["cap"], CH * g + c + 1)
                        dve.tensor_reduce(stat(smax, c), chunk(c), AX_X, ALU.max).then_inc(s["mx"], 1)
                        dve.wait_ge(s["mx"], CH * g + c + 1)
                        dve.tensor_tensor(chunk(c), chunk(c), rows(smax, c), ALU.subtract).then_inc(s["sub"], 1)
                    if q and i >= 1:
                        rotate(g + 1, i - 1)
                    if 2 <= i < CH + 2:
                        c = i - 2
                        dve.wait_ge(s["expd"], CH * g + c + 1)
                        dve.tensor_reduce(stat(ssum, c), chunk(c), AX_X, ALU.add).then_inc(s["ssum"], 1)
                        dve.wait_ge(s["ssum"], CH * g + c + 1)
                        dve.reciprocal(stat(srec, c), stat(ssum, c)).then_inc(s["srec"], 1)
                        dve.wait_ge(s["srec"], CH * g + c + 1)
                        dve.tensor_tensor(chunk(c), chunk(c), rows(srec, c), ALU.mult).then_inc(s["norm"], 1)

                def add(t):
                    dve.wait_ge(s["wo"], PAIRS * g + t + 1)
                    after(dve, s["x"], PAIRS * g)
                    dve.scalar_tensor_tensor(x_all[:, t], a_ps[t % 2][:], gates[:, 1:2], x_all[:, t],
                                             ALU.mult, ALU.add).then_inc(s["x"], 1)

                for t in range(PAIRS):
                    for b in range(2):
                        dve.wait_ge(s["ohi"], 2 * (PAIRS * g + t) + b + 1)
                        cols = slice(b * SEQ, b * SEQ + SEQ)
                        dve.tensor_tensor(ol[:, t % 2, :, cols],
                                          o_ps[t % 2][b][:, 0:GH * SEQ].rearrange("p (h q) -> p h q", h=GH),
                                          oh[:, t % 2, :, cols].bitcast(F32), ALU.subtract).then_inc(s["olo"], 1)
                    if t:
                        add(t - 1)
                add(PAIRS - 1)

            for i in range(QT + 1):
                if i < QT:
                    cosine(0, i)
                if i:
                    rotate(0, i - 1)
            group(0)
            with dve.Fori(1, GROUPS - 1) as g:
                group(g)
            group(GROUPS - 1, q=False)

        @block.tensor
        def _(pe):
            def project_q(g, i):
                n = QT * g + i
                if i == 0:
                    pe.wait_ge(s["wq_lo"], KT * g + KT)
                if i >= 2:
                    pe.wait_ge(s["qcos"], n - 1)
                elif not isinstance(g, int) or g > 0:
                    after(pe, s["x"], PAIRS * (g - 1))
                h, half = i // 2, i % 2
                three_passes(pe, a_ps[i % 2][:], lambda k: (wqh[:, k, h * DK:h * DK + DK], wql[:, k, h * DK:h * DK + DK]),
                             lambda k: (xTh[:, k, half * D:half * D + D], xTl[:, k, half * D:half * D + D]), KT)\
                    .then_inc(s["q"], 1)

            def group(g, q=True):
                pe.wait_ge(s["qrot"], QT * g + QT)
                pe.wait_ge(s["k_in"], 16 * g + 16)
                for c in range(CH):
                    if c < 2:
                        after(pe, s["pt"], PAIRS * g)
                    else:
                        pe.wait_ge(s["cap"], CH * g + c - 1)
                    for t in range(2):
                        for h in range(2):
                            for b in range(2):
                                n = 4 * c + 2 * t + b
                                col = ((2 * t + h) * 2 + b) * SEQ
                                last = pe.matmul(s_ps[c % 2][:, col:col + SEQ],
                                                 qT[:, n, 2 * h:2 * h + 2, :].rearrange("p h q -> p (h q)"),
                                                 kT[:, n * SEQ:n * SEQ + SEQ], start=True, stop=True)
                    last.then_inc(s["score"], 1)
                if q:
                    for i in range(QT):
                        project_q(g + 1, i)
                pe.wait_ge(s["cap"], CH * g + CH)
                pe.wait_ge(s["v_in"], 16 * g + 16)

                def attend(t):
                    pe.wait_ge(s["pt"], PAIRS * g + t + 1)
                    after(pe, s["olo"], 2 * (PAIRS * g + max(t - 1, 0)))
                    for b in range(2):
                        r = slice(b * SEQ, b * SEQ + SEQ)
                        last = pe.matmul(o_ps[t % 2][b][:, 0:GH * SEQ], vr[r, t, :], PT[r, t, :],
                                         start=True, stop=True)
                    last.then_inc(s["av"], 1)

                def project_out(t):
                    if t == 0:
                        pe.wait_ge(s["wo_lo"], GH * g + GH)
                        pe.wait_ge(s["qcos"], QT * (g + 2) if q else QT * GROUPS)
                    if t >= 2:
                        pe.wait_ge(s["x"], PAIRS * g + t - 1)
                    pe.wait_ge(s["olo"], 2 * (PAIRS * g + t) + 2)
                    three_passes(pe, a_ps[t % 2][:], lambda h: (oh[:, t % 2, h], ol[:, t % 2, h]),
                                 lambda h: (woh[:, h], wol[:, h]), GH).then_inc(s["wo"], 1)

                for t in range(PAIRS + 2):
                    if t < PAIRS:
                        pe.wait_ge(s["norm"], CH * g + t // 2 + 1)
                        if t >= 2:
                            pe.wait_ge(s["pt"], PAIRS * g + t - 1)
                        for h in range(2):
                            last = pe.transpose(s_ps[t % 2][:, h * P:h * P + P], S[:, t, h], ident[:])
                        last.then_inc(s["t"], 1)
                    if 1 <= t <= PAIRS:
                        attend(t - 1)
                    if t >= 2:
                        project_out(t - 2)

            for i in range(QT):
                project_q(0, i)
            group(0)
            with pe.Fori(1, GROUPS - 1) as g:
                group(g)
            group(GROUPS - 1, q=False)


def layer_1_ffn(nc, a, x_all, ident, gates, out):
    with ExitStack() as ctx:
        al = Pool(nc, ctx, "h")
        router_a = al.sb("router_a", [P, KT, MID + EXPERTS])
        b_all = al.sb("b_all", [MID, D])
        g4 = al.sb("g4", [P, 1])
        xn = al.sb("xn", [P, 2, D])
        rows = RowStatistics(al, "rows", PAIRS)
        xnT = al.sb("xnT", [P, 2, KT, P])
        mid = al.sb("mid", [P, PAIRS, MID + EXPERTS])
        beats = al.sb("beats", [P, PAIRS, EXPERTS, EXPERTS])
        ties = al.sb("ties", [P, PAIRS, EXPERTS, EXPERTS])
        first = al.sb("first", [P, EXPERTS, EXPERTS])
        rank = al.sb("rank", [P, PAIRS, EXPERTS])
        chosen = al.sb("chosen", [P, PAIRS, EXPERTS])
        top = al.sb("top", [P, PAIRS])
        e = al.sb("e", [P, PAIRS, EXPERTS])
        total = al.sb("total", [P, PAIRS])
        inverse = al.sb("inverse", [P, PAIRS])
        midT = al.sb("midT", [MID, 2, P])
        t_ps = [al.ps(f"t_ps{i}", [P, KT, P]) for i in range(2)]
        m_ps = [al.ps(f"m_ps{i}", [P, MID + EXPERTS]) for i in range(2)]
        d_ps = [al.ps(f"d_ps{i}", [P, D]) for i in range(2)]
        s = {n: al.sem(n) for n in ("in", "g4", "ln", "t", "t_ev", "m", "m_ev", "gate", "expd", "mt", "mt_ev",
                                    "d", "x", "out")}
        block = ctx.enter_context(nc.Block())

        @block.sync
        def _(sp):
            sp.dma_start(router_a[:], a["router_A"].rearrange("(k p) n -> p k n", p=P)).then_inc(s["in"], 16)
            sp.dma_start(b_all[:], a["B"]).then_inc(s["in"], 16)
            sp.dma_start(first[:].rearrange("p a b -> p (a b)"), a["first"]).then_inc(s["in"], 16)
            out_rows = out.rearrange("(t p) d -> p t d", p=P)
            for t in range(PAIRS):
                sp.wait_ge(s["x"], t + 1)
                sp.dma_start(out_rows[:, t], x_all[:, t]).then_inc(s["out"], 16)
            sp.wait_ge(s["out"], 16 * PAIRS)

        @block.scalar
        def _(act):
            act.activation(g4[:], gates[:, 3:4], ACT.Copy, scale=LORA_SCALE).then_inc(s["g4"], 1)
            rows.on_scalar(act)
            for t in range(PAIRS):
                act.wait_ge(s["t"], t + 1)
                after(act, s["m"], t - 1)
                act.activation(xnT[:, t % 2], t_ps[t % 2][:], ACT.Copy).then_inc(s["t_ev"], 1)
            act.wait_ge(s["gate"], 1)
            act.activation(e[:], e[:], ACT.Exp).then_inc(s["expd"], 1)
            for t in range(PAIRS):
                act.wait_ge(s["mt"], t + 1)
                after(act, s["d"], t - 1)
                act.activation(midT[:, t % 2], t_ps[t % 2][0:MID, 0], ACT.Copy).then_inc(s["mt_ev"], 1)

        @block.vector
        def _(dve):
            rows.on_vector(dve, [x_all[:, t] for t in range(PAIRS)])
            for t in range(PAIRS):
                after(dve, s["t"], t - 1)
                rows.apply(dve, xn[:, t % 2], x_all[:, t], t).then_inc(s["ln"], 1)
                if t:
                    dve.wait_ge(s["m"], t)
                    dve.tensor_copy(mid[:, t - 1], m_ps[(t - 1) % 2][:]).then_inc(s["m_ev"], 1)
            dve.wait_ge(s["m"], PAIRS)
            dve.tensor_copy(mid[:, PAIRS - 1], m_ps[(PAIRS - 1) % 2][:]).then_inc(s["m_ev"], 1)
            dve.wait_ge(s["m_ev"], PAIRS)
            dve.wait_ge(s["in"], 48)
            step = [0]

            def link(instruction):
                step[0] += 1
                instruction.then_inc(chain, 1)
                dve.wait_ge(chain, step[0])

            chain = al.sem("chain")
            logits = mid[:, :, MID:]
            rival = logits.rearrange("p t (o j) -> p t o j", o=1).broadcast_to([P, PAIRS, EXPERTS, EXPERTS])
            own = logits.rearrange("p t (j o) -> p t j o", o=1).broadcast_to([P, PAIRS, EXPERTS, EXPERTS])
            link(dve.tensor_tensor(beats[:], rival, own, ALU.is_gt))
            link(dve.tensor_tensor(ties[:], rival, own, ALU.is_equal))
            link(dve.tensor_tensor(ties[:], ties[:], first[:].rearrange("p (o i) j -> p o i j", o=1)
                                   .broadcast_to([P, PAIRS, EXPERTS, EXPERTS]), ALU.mult))
            link(dve.tensor_tensor(beats[:], beats[:], ties[:], ALU.add))
            link(dve.tensor_reduce(rank[:], beats[:], AX_X, ALU.add))
            link(dve.tensor_scalar(chosen[:], rank[:], 1.5, None, ALU.is_lt))
            link(dve.tensor_reduce(top[:], logits, AX_X, ALU.max))
            dve.tensor_tensor(e[:], logits, top[:].rearrange("p (t o) -> p t o", o=1)
                              .broadcast_to([P, PAIRS, EXPERTS]), ALU.subtract).then_inc(s["gate"], 1)
            dve.wait_ge(s["expd"], 1)
            link(dve.tensor_tensor(e[:], e[:], chosen[:], ALU.mult))
            link(dve.tensor_reduce(total[:], e[:], AX_X, ALU.add))
            link(dve.reciprocal(inverse[:], total[:]))
            link(dve.tensor_tensor(e[:], e[:], inverse[:].rearrange("p (t o) -> p t o", o=1)
                                   .broadcast_to([P, PAIRS, EXPERTS]), ALU.mult))
            weighed = mid[:, :, 0:MID].rearrange("p t (e r) -> p t e r", e=EXPERTS)
            for t in range(PAIRS):
                last = dve.tensor_tensor(weighed[:, t], weighed[:, t], e[:, t].rearrange("p (e o) -> p e o", o=1)
                                         .broadcast_to([P, EXPERTS, ERANK]), ALU.mult)
            last.then_inc(s["gate"], 1)
            dve.wait_ge(s["g4"], 1)
            for t in range(PAIRS):
                dve.wait_ge(s["d"], t + 1)
                dve.scalar_tensor_tensor(x_all[:, t], d_ps[t % 2][:], g4[:], x_all[:, t], ALU.mult, ALU.add)\
                   .then_inc(s["x"], 1)

        @block.tensor
        def _(pe):
            pe.wait_ge(s["in"], 48)

            def logits(t):
                pe.wait_ge(s["t_ev"], t + 1)
                after(pe, s["m_ev"], t - 1)
                for k in range(KT):
                    last = pe.matmul(m_ps[t % 2][:], xnT[:, t % 2, k], router_a[:, k], start=(k == 0), stop=(k == KT - 1))
                last.then_inc(s["m"], 1)

            for t in range(PAIRS):
                pe.wait_ge(s["ln"], t + 1)
                after(pe, s["t_ev"], t - 1)
                for k in range(KT):
                    last = pe.transpose(t_ps[t % 2][:, k], xn[:, t % 2, k * P:k * P + P], ident[:])
                last.then_inc(s["t"], 1)
                if t:
                    logits(t - 1)
            logits(PAIRS - 1)
            pe.wait_ge(s["gate"], 2)
            pe.wait_ge(s["t_ev"], PAIRS)

            def delta(t):
                pe.wait_ge(s["mt_ev"], t + 1)
                after(pe, s["x"], t - 1)
                pe.matmul(d_ps[t % 2][:], midT[:, t % 2], b_all[:], start=True, stop=True).then_inc(s["d"], 1)

            for t in range(PAIRS):
                after(pe, s["mt_ev"], t - 1)
                pe.transpose(t_ps[t % 2][0:MID, 0], mid[:, t, 0:MID], ident[:]).then_inc(s["mt"], 1)
                if t:
                    delta(t - 1)
            delta(PAIRS - 1)


def flamingo_gated(nc, a, out):
    k_dram = nc.dram_tensor("k_scratch", (GROUPS, P, PAIRS * P), F32, kind="Internal").ap()
    v_dram = nc.dram_tensor("v_scratch", (GROUPS, P, PAIRS * DK), F32, kind="Internal").ap()
    with ExitStack() as ctx:
        al = Pool(nc, ctx, "all")
        x_all = al.sb("x_all", [P, PAIRS, D])
        ident = al.sb("ident", [P, P])
        gates = al.sb("gates", [P, 4])
        layer_0_attention(nc, a, x_all, ident, gates, k_dram, v_dram)
        with ExitStack() as inner:
            al = Pool(nc, inner, "split")
            xTh = al.sb("xTh", [P, KT, PAIRS * P], F32R)
            xTl = al.sb("xTl", [P, KT, PAIRS * P], F32R)
            layer_0_ffn(nc, a, x_all, ident, gates, xTh, xTl)
            layer_1_attention(nc, a, x_all, gates, ident, xTh, xTl, k_dram, v_dram)
        layer_1_ffn(nc, a, x_all, ident, gates, out)


def rotary_tables(scale):
    freq = 1.0 / np.float32(10000.0) ** (np.arange(0, DK, 2, dtype=np.float32) / np.float32(DK))
    angle = (np.arange(SEQ, dtype=np.float32)[:, None] * freq[None, :]).T.astype(np.float64)
    cos, sin = np.cos(angle) * scale, np.sin(angle) * scale
    return (np.concatenate([cos, cos]).astype(np.float32), np.concatenate([-sin, sin]).astype(np.float32))


def constants():
    c = {"ident": np.eye(P, dtype=np.float32)}
    pick = np.zeros((P, 15 * ROWS0), np.float32)
    pick[np.arange(P), 7 * ROWS0 + np.arange(P) // HD0] = 1.0
    c["pick"] = pick
    c["cosk"], c["sink"] = rotary_tables(1.0)
    c["cosq"], c["sinq"] = rotary_tables(float(DK) ** -0.5)
    c["eye_r"] = (np.arange(P)[:, None] % RANK == np.arange(RANK)[None, :]).astype(np.float32)
    c["own"] = (np.arange(P)[:, None] // RANK == np.arange(HALF)[None, :]).astype(np.float32)
    lower = np.arange(EXPERTS)[None, :] < np.arange(EXPERTS)[:, None]
    c["first"] = np.tile(lower.astype(np.float32).reshape(1, -1), (P, 1))
    return c


def kernel(**inputs):
    import concourse.bacc as bacc
    from concourse.bass_utils import run_bass_kernel_spmd

    i = {k: np.asarray(v) for k, v in inputs.items()}
    rows = BATCH * SEQ
    arrays = {
        "x": i["x"].reshape(rows, D),
        "ctx": i["ctx_4096"].reshape(rows, D),
        "ctxT": i["ctx_4096"].reshape(rows, D).T,
        "mask": i["mask_BxSxS2_ff1"],
        "g_xattn": i["g_xattn"], "g_ffn": i["g_ffn"],
        "WqT": i["L0_xattn_Wq"].T, "WkT": i["L0_xattn_Wk"].T, "WvT": i["L0_xattn_Wv"].T, "WoT": i["L0_xattn_Wo"].T,
        "bq": i["L0_xattn_bq"][:, None], "bk": i["L0_xattn_bk"][:, None],
        "bv": i["L0_xattn_bv"][:, None], "bo": i["L0_xattn_bo"][:, None],
        "gate": np.repeat(i["L0_ffn_gate"].T, RANK, axis=0),
        "kernel": i["L0_ffn_kernel"],
        "lora_A": i["L0_ffn_lora_A"].reshape(LORAS * RANK, D),
        "lora_B": i["L0_ffn_lora_B"].transpose(0, 2, 1).reshape(LORAS * RANK, D),
        "A_shared": i["L0_ffn_lora_A_shared"].T,
        "B_shared": np.concatenate([i["L0_ffn_lora_B_shared"].T, i["L0_ffn_bias"][None, :]]),
        "wq": i["L1_xattn_wq"], "wk": i["L1_xattn_wk"], "wv": i["L1_xattn_wv"], "wo": i["L1_xattn_wo"],
        "router_A": np.concatenate([i["L1_ffn_A"].reshape(MID, D), i["L1_ffn_router_w"]]).T,
        "B": i["L1_ffn_B"].transpose(0, 2, 1).reshape(MID, D),
        **constants(),
    }
    nc = bacc.Bacc("TRN2", target_bir_lowering=False, num_devices=1)
    feed, a = {}, {}
    for name, array in arrays.items():
        feed[f"in_{name}"] = np.ascontiguousarray(array)
        a[name] = nc.dram_tensor(f"in_{name}", array.shape, F32, kind="ExternalInput").ap()
    out = nc.dram_tensor("out_x", (rows, D), F32, kind="ExternalOutput").ap()
    flamingo_gated(nc, a, out)
    result = run_bass_kernel_spmd(nc, [feed], core_ids=[0])
    return result.results[0]["out_x"].reshape(BATCH, SEQ, D)
```

```python
from contextlib import ExitStack

import numpy as np

import concourse.bass as bass
from concourse import mybir

F32 = mybir.dt.float32
F32R = mybir.dt.float32r
ALU = mybir.AluOpType
ACT = mybir.ActivationFunctionType
AX_X = mybir.AxisListType.X

P = 128
BATCH, SEQ, D = 16, 64, 512
PAIRS = BATCH * SEQ // P
KT = D // P
EPS = 1e-5

WIN, PAD, HD0 = 16, 8, 8
ROWS0 = P // HD0
PADDED = PAD + D + WIN - PAD - 1

LORAS, RANK = 16, 32
LORA_CHUNKS = LORAS * RANK // P
HALF = P // RANK

GROUPS, GH, DK = 8, 4, 128
MASKED = -1e9
HUGE = 3e38

EXPERTS, ERANK = 4, 16
MID = EXPERTS * ERANK
LORA_SCALE = 4.0

ds = bass.ds


def after(eng, sem, value):
    if not isinstance(value, int) or value > 0:
        eng.wait_ge(sem, value)


def three_passes(pe, out, weights, moving, k_steps):
    last = None
    for k in range(k_steps):
        wh, wl = weights(k)
        mh, ml = moving(k)
        for n, (w, m) in enumerate(((wl, mh), (wh, ml), (wh, mh))):
            last = pe.matmul(out, w, m, start=(k == 0 and n == 0), stop=(k == k_steps - 1 and n == 2))
    return last


class Pool:

    def __init__(self, nc, ctx, stage):
        self.nc, self.ctx, self.stage = nc, ctx, stage

    def sb(self, name, shape, dt=F32):
        return self.ctx.enter_context(self.nc.sbuf_tensor(f"{self.stage}_{name}", shape, dt))

    def ps(self, name, shape):
        return self.ctx.enter_context(self.nc.psum_tensor(f"{self.stage}_{name}", shape, F32))

    def sem(self, name):
        return self.ctx.enter_context(self.nc.semaphore(f"{self.stage}_{name}"))


class RowNorm:

    STEPS = 5

    def __init__(self, al, name):
        self.stats, self.moments = al.sb(f"{name}_stats", [P, 6]), al.sb(f"{name}_moments", [P, 2])
        self.rstd, self.power, self.spare = (al.sb(f"{name}_{n}", [P, w]) for n, w in
                                             (("rstd", 1), ("power", 1), ("spare", 2)))
        self.steps, self.rooted, self.applied = (al.sem(f"{name}_{n}") for n in ("steps", "rooted", "applied"))

    def moments_of(self, dve, src, turn):
        base = self.STEPS * turn
        after(dve, self.applied, turn)
        dve.memset(self.spare[:, 0:1], 0.0).then_inc(self.steps, 1)
        dve.bn_stats(self.stats[:], src).then_inc(self.steps, 1)
        dve.wait_ge(self.steps, base + 2)
        dve.memset(self.spare[:, 1:2], 0.0).then_inc(self.steps, 1)
        dve.bn_aggr(self.moments[:], self.stats[:]).then_inc(self.steps, 1)
        dve.wait_ge(self.steps, base + 4)
        dve.tensor_scalar(self.moments[:, 1:2], self.moments[:, 1:2], EPS, None, ALU.add).then_inc(self.steps, 1)

    def start(self, pool):
        pool.memset(self.power[:], -0.5).then_inc(self.rooted, 1)
        pool.wait_ge(self.rooted, 1)

    def root(self, pool, turn):
        pool.wait_ge(self.steps, self.STEPS * turn + 5)
        pool.tensor_tensor(self.rstd[:], self.moments[:, 1:2], self.power[:], ALU.pow).then_inc(self.rooted, 1)

    def apply(self, dve, out, src, turn):
        dve.wait_ge(self.rooted, turn + 2)
        dve.tensor_scalar(out, src, self.moments[:, 0:1], self.rstd[:], ALU.subtract, ALU.mult)\
           .then_inc(self.applied, 1)


def tile_of(x, t):
    return x[:, ds(t, 1), :].rearrange("p o d -> p (o d)")


def layer_0_attention(nc, a, x_all, ident, gates, k_dram, v_dram, ffn):
    with ExitStack() as ctx:
        al = Pool(nc, ctx, "a")
        ctx_t = al.sb("ctx_t", [P, 2, D])
        big = al.sb("big", [P, KT, PAIRS * P])
        ctxTh = al.sb("ctxTh", [P, KT, PAIRS * P], F32R)
        ctxTl = al.sb("ctxTl", [P, KT, PAIRS * P], F32R)
        wvh = al.sb("wvh", [P, KT, GROUPS * DK], F32R)
        wvl = al.sb("wvl", [P, KT, GROUPS * DK], F32R)
        w_diag = al.sb("w_diag", [P, 4, P])
        bias = al.sb("bias", [P, 4])
        pick = al.sb("pick", [P, 15 * ROWS0])
        cosk, sink = al.sb("cosk", [P, SEQ]), al.sb("sink", [P, SEQ])
        gbo = al.sb("gbo", [P, 1])
        xn = al.sb("xn", [P, D])
        norm = RowNorm(al, "norm")
        kpad, vpad = al.sb("kpad", [P, PADDED]), al.sb("vpad", [P, PADDED])
        prod = al.sb("prod", [P, 4, D])
        sT = al.sb("sT", [P, 2, D])
        probs = al.sb("probs", [P, 4, WIN, ROWS0])
        smax, ssum, srec = (al.sb(n, [P, 4, ROWS0]) for n in ("smax", "ssum", "srec"))
        rep = al.sb("rep", [P, 2, 4, P])
        ev = al.sb("ev", [P, 4, D])
        evs = al.sb("evs", [P, 4, D])
        otmp = al.sb("otmp", [P, D])
        land = al.sb("land", [P, KT, DK])
        wh, wl = al.sb("wh", [P, KT, DK], F32R), al.sb("wl", [P, KT, DK], F32R)
        tokh, tokl = al.sb("tokh", [P, KT, P], F32R), al.sb("tokl", [P, KT, P], F32R)
        ksw, krot = al.sb("ksw", [P, 2, D]), al.sb("krot", [P, 2, D])
        vrow = al.sb("vrow", [P, 2, D])

        q_ps, k_ps = al.ps("q_ps", [P, D]), al.ps("k_ps", [P, D])
        s_ps = al.ps("s_ps", [P, 2, D])
        e_ps = [al.ps("e_ps0", [P, D]), al.ps("e_ps1", [P, D])]
        kv_ps = [al.ps("kv_ps0", [P, D]), al.ps("kv_ps1", [P, D])]
        po = k_ps

        s = {n: al.sem(n) for n in (
            "x0_in", "x_in", "ctx_in", "small_in", "wk_in", "zeroed", "w_in", "gate", "ctx_hi", "ctx_lo",
            "wv_hi", "wv_lo",
            "l0q", "l0k", "l0v", "k_ev", "v_ev", "prod", "score", "sT_ev", "sc", "mx", "sub", "expd",
            "ssum", "srec", "norm", "rep", "e", "ev", "pair", "quad", "osum", "o_ev", "x_add",
            "whi", "wlo", "tok", "k0", "k1", "v0", "v1", "ksw", "kcos", "kt2", "kready", "v0_ev", "v1_ev",
            "k_st", "v_st")}
        ctxT_in = [al.sem(f"ctxT_in{k}") for k in range(KT)]
        wv_in = [al.sem(f"wv_in{k}") for k in range(KT)]
        SMALL = 16 * 8
        QUADS = WIN // 4

        wk_view = a["wk"].rearrange("(k p) n -> p k n", p=P)
        x_view = a["x"].rearrange("(t p) d -> p t d", p=P)
        ctx_view = a["ctx"].rearrange("(t p) d -> p t d", p=P)
        block = ctx.enter_context(nc.Block())

        @block.sync
        def _(sp):
            def load_wk(g):
                after(sp, s["wlo"], g)
                sp.dma_start(land[:], wk_view[:, :, ds(g * DK, DK)]).then_inc(s["wk_in"], 16)

            def load_ctx(p):
                if not isinstance(p, int) or p >= 2:
                    sp.wait_ge(s["l0v"], p - 1)
                    sp.wait_ge(s["ctx_in"], 16 * p)
                sp.dma_start(tile_of(ctx_t, p % 2), ctx_view[:, ds(p, 1), :].rearrange("p o d -> p (o d)"))\
                  .then_inc(s["ctx_in"], 16)

            def store(g):
                sp.wait_ge(s["kready"], 2 * g + 2)
                sp.dma_start(k_dram[ds(g, 1)].rearrange("o p n -> p (o n)"),
                             krot[:].rearrange("p h n -> p (h n)")).then_inc(s["k_st"], 16)
                sp.wait_ge(s["v1_ev"], g + 1)
                sp.dma_start(v_dram[:, :, ds(g, 1), :].rearrange("g p o n -> p g (o n)"),
                             vrow[:].rearrange("p h n -> p (h n)").rearrange("p (g n) -> p g n", n=DK))\
                  .then_inc(s["v_st"], 16)

            sp.dma_start(x_all[:, 0], x_view[:, 0]).then_inc(s["x0_in"], 16)
            load_ctx(0)
            load_wk(0)
            for k in range(KT):
                sp.dma_start(big[:, k], a["ctxT"][k * P:k * P + P, :]).then_inc(ctxT_in[k], 16)
            sp.dma_start(x_all[:, 1:], x_view[:, 1:]).then_inc(s["x_in"], 16)
            for k in range(KT):
                sp.wait_ge(s["ctx_lo"], k + 1)
                sp.dma_start(big[:, k], a["wv"][k * P:k * P + P, :]).then_inc(wv_in[k], 16)
            sp.wait_ge(s["ctx_in"], 16)
            load_ctx(1)
            ffn.load(sp, a)
            load_wk(1)
            store(0)
            with sp.Fori(1, GROUPS - 1) as g:
                load_ctx(g + 1)
                load_wk(g + 1)
                store(g)
            store(GROUPS - 1)
            sp.wait_ge(s["k_st"], 16 * GROUPS)
            sp.wait_ge(s["v_st"], 16 * GROUPS)

        @block.scalar
        def _(act):
            act.wait_ge(s["zeroed"], 1)
            for h in (0, 64):
                act.dma_start(w_diag[h:h + 64, :, h:h + 64], a["W4"].rearrange("c (n o) -> c n o", n=4)).then_inc(s["small_in"], 16)
                act.dma_start(bias[h:h + 64, :], a["b4"]).then_inc(s["small_in"], 16)
            act.dma_start(gates[:], a["g4"].partition_broadcast(P)).then_inc(s["small_in"], 16)
            act.dma_start(pick[:], a["pick"]).then_inc(s["small_in"], 16)
            act.dma_start(cosk[:], a["cosk"]).then_inc(s["small_in"], 16)
            act.dma_start(sink[:], a["sink"]).then_inc(s["small_in"], 16)
            act.dma_start(ident[:], a["ident"]).then_inc(s["w_in"], 16)
            act.wait_ge(s["small_in"], SMALL)
            act.activation(gates[:], gates[:], ACT.Tanh).then_inc(s["gate"], 1)

            def split_wk(g):
                act.wait_ge(s["wk_in"], 16 * g + 16)
                after(act, s["k1"], g)
                act.activation(wh[:], land[:], ACT.Copy).then_inc(s["whi"], 1)

            def take_tile(p):
                after(act, s["v1"], p)
                cols = ds(p * P, P)
                act.activation(tokh[:], ctxTh[:, :, cols].bitcast(F32), ACT.Copy)
                act.activation(tokl[:], ctxTl[:, :, cols].bitcast(F32), ACT.Copy).then_inc(s["tok"], 1)

            def k_evacuate(p):
                act.wait_ge(s["l0k"], p + 1)
                after(act, s["prod"], WIN * p)
                act.activation(kpad[:, PAD:PAD + D], k_ps[:], ACT.Identity, bias=bias[:, 1:2]).then_inc(s["k_ev"], 1)

            def out_evacuate(p):
                act.wait_ge(s["osum"], QUADS * p + QUADS)
                after(act, s["x_add"], p)
                act.activation(otmp[:], po[:], ACT.Identity, bias=gbo[:], scale=gates[:, 0:1]).then_inc(s["o_ev"], 1)

            def swap_k(p, h, ready):
                act.wait_ge(s[ready], p + 1)
                after(act, s["kready"], 2 * p)
                act.activation(ksw[0:64, h], kv_ps[1 - h][64:128, :], ACT.Copy).then_inc(s["ksw"], 1)
                act.activation(ksw[64:128, h], kv_ps[1 - h][0:64, :], ACT.Copy).then_inc(s["ksw"], 1)

            def body(p, more=True, before=True):
                act.wait_ge(s["l0v"], p + 1)
                after(act, s["ev"], WIN * p)
                act.activation(vpad[:, PAD:PAD + D], kv_ps[0][:], ACT.Identity, bias=bias[:, 2:3]).then_inc(s["v_ev"], 1)
                if before:
                    out_evacuate(p - 1)
                swap_k(p, 0, "k0")
                for h in range(2):
                    act.wait_ge(s["score"], WIN * p + 8 * h + 8)
                    after(act, s["sc"], p)
                    act.activation(sT[:, h], s_ps[:, h], ACT.Copy).then_inc(s["sT_ev"], 1)
                swap_k(p, 1, "k1")
                act.wait_ge(s["sub"], p + 1)
                act.activation(probs[:], probs[:], ACT.Exp, scale=float(HD0) ** -0.5).then_inc(s["expd"], 1)
                act.wait_ge(s["v0"], p + 1)
                after(act, s["v_st"], 16 * p)
                act.activation(vrow[:, 0], kv_ps[1][:], ACT.Copy).then_inc(s["v0_ev"], 1)
                if more:
                    k_evacuate(p + 1)
                    split_wk(p + 1)
                act.wait_ge(s["norm"], p + 1)
                for w in range(WIN):
                    after(act, s["e"], WIN * p + max(w - 1, 0))
                    act.activation(rep[:, w % 2].rearrange("p t (h c) -> p t h c", c=HD0),
                                   probs[:, :, w, :].rearrange("p t (h o) -> p t h o", o=1)
                                   .broadcast_to([P, 4, ROWS0, HD0]), ACT.Copy).then_inc(s["rep"], 1)
                    if w == 2:
                        act.wait_ge(s["v1"], p + 1)
                        act.activation(vrow[:, 1], kv_ps[0][:], ACT.Copy).then_inc(s["v1_ev"], 1)
                    if w == 5 and more:
                        take_tile(p + 1)

            act.wait_ge(ctxT_in[0], 16)
            for k in range(KT):
                act.wait_ge(ctxT_in[k], 16)
                act.activation(ctxTh[:, k], big[:, k], ACT.Copy).then_inc(s["ctx_hi"], 1)
                if k == 0:
                    split_wk(0)
                if k == 1:
                    act.wait_ge(s["gate"], 1)
                    act.activation(gbo[:], bias[:, 3:4], ACT.Copy, scale=gates[:, 0:1]).then_inc(s["gate"], 1)
                    act.wait_ge(s["zeroed"], 3)
                    k_evacuate(0)
            act.wait_ge(s["ctx_lo"], KT)
            take_tile(0)
            for k in range(KT):
                act.wait_ge(wv_in[k], 16)
                act.activation(wvh[:, k], big[:, k], ACT.Copy).then_inc(s["wv_hi"], 1)
            act.wait_ge(s["gate"], 2)
            body(0, before=False)
            with act.Fori(1, PAIRS - 1) as p:
                body(p)
            body(PAIRS - 1, more=False)
            out_evacuate(PAIRS - 1)

        @block.gpsimd
        def _(pool):
            pool.memset(w_diag[:], 0.0).then_inc(s["zeroed"], 1)
            pool.memset(kpad[:], 0.0).then_inc(s["zeroed"], 1)
            pool.memset(vpad[:], 0.0).then_inc(s["zeroed"], 1)
            norm.start(pool)
            norm.root(pool, 0)

            def split_wk(g):
                pool.wait_ge(s["whi"], g + 1)
                after(pool, s["k1"], g)
                pool.tensor_tensor(wl[:], land[:], wh[:].bitcast(F32), ALU.subtract).then_inc(s["wlo"], 1)

            def rotate_k(p, h):
                pool.wait_ge(s["ksw"], 4 * p + 2 * h + 2)
                kv = ksw[:, h].rearrange("p (b q) -> p b q", q=SEQ)
                pool.tensor_tensor(kv, kv, sink[:].rearrange("p (o q) -> p o q", o=1)
                                   .broadcast_to([P, D // SEQ, SEQ]), ALU.mult).then_inc(s["kt2"], 1)
                pool.wait_ge(s["kt2"], 2 * p + h + 1)
                pool.wait_ge(s["kcos"], 2 * p + h + 1)
                pool.tensor_tensor(krot[:, h], krot[:, h], ksw[:, h], ALU.add).then_inc(s["kready"], 1)

            def x_update(p):
                pool.wait_ge(s["o_ev"], p + 1)
                xp = tile_of(x_all, p)
                pool.tensor_tensor(xp, xp, otmp[:], ALU.add).then_inc(s["x_add"], 1)

            def body(p, more=True, before=True):
                if more:
                    norm.root(pool, p + 1)
                if before:
                    x_update(p - 1)
                rotate_k(p, 0)
                rotate_k(p, 1)
                if more:
                    split_wk(p + 1)
                for j in range(WIN // 2):
                    pool.wait_ge(s["ev"], WIN * p + 2 * j + 2)
                    after(pool, s["osum"], QUADS * p + max(j // 2 - 1, 0))
                    pool.tensor_tensor(evs[:, j % 4], ev[:, 2 * j % 4], ev[:, (2 * j + 1) % 4], ALU.add)\
                        .then_inc(s["pair"], 1)
                    if j % 2:
                        pool.wait_ge(s["pair"], 8 * p + j + 1)
                        pool.tensor_tensor(evs[:, j % 4 - 1], evs[:, j % 4 - 1], evs[:, j % 4], ALU.add)\
                            .then_inc(s["quad"], 1)

            pool.wait_ge(s["small_in"], SMALL)
            split_wk(0)
            for k in range(KT):
                pool.wait_ge(s["wv_hi"], k + 1)
                pool.tensor_tensor(wvl[:, k], big[:, k], wvh[:, k].bitcast(F32), ALU.subtract).then_inc(s["wv_lo"], 1)
            body(0, before=False)
            with pool.Fori(1, PAIRS - 1) as p:
                body(p)
            body(PAIRS - 1, more=False)
            x_update(PAIRS - 1)

        @block.vector
        def _(dve):
            def k_cos(p, h):
                dve.wait_ge(s["ksw"], 4 * p + 2 * h + 2)
                after(dve, s["k_st"], 16 * p)
                dve.tensor_tensor(krot[:, h].rearrange("p (b q) -> p b q", q=SEQ),
                                  kv_ps[1 - h][:].rearrange("p (b q) -> p b q", q=SEQ),
                                  cosk[:].rearrange("p (o q) -> p o q", o=1).broadcast_to([P, D // SEQ, SEQ]),
                                  ALU.mult).then_inc(s["kcos"], 1)

            def body(p, more=True):
                dve.wait_ge(s["l0q"], p + 1)
                dve.wait_ge(s["k_ev"], p + 1)
                for w in range(WIN):
                    after(dve, s["score"], WIN * p + max(w - 3, 0))
                    dve.scalar_tensor_tensor(prod[:, w % 4], q_ps[:], bias[:, 0:1], kpad[:, w:w + D],
                                             ALU.add, ALU.mult).then_inc(s["prod"], 1)
                    if w == 4 and more:
                        norm.moments_of(dve, tile_of(x_all, p + 1), p + 1)
                    if w == 8 and more:
                        norm.apply(dve, xn[:], tile_of(x_all, p + 1), p + 1)
                    if w == 12:
                        k_cos(p, 0)
                scores = s_ps[:].rearrange("p h n -> p (h n)").rearrange("p (t w r) -> p t w r", t=4, w=WIN)
                dve.wait_ge(s["sc"], p + 1)
                dve.tensor_reduce(smax[:], scores.rearrange("p t w r -> p t r w"), AX_X, ALU.max).then_inc(s["mx"], 1)
                dve.wait_ge(s["mx"], p + 1)
                after(dve, s["rep"], WIN * p)

                def by_row(stat):
                    return stat[:].rearrange("p t (o r) -> p t o r", o=1).broadcast_to([P, 4, WIN, ROWS0])

                dve.tensor_tensor(probs[:], scores, by_row(smax), ALU.subtract).then_inc(s["sub"], 1)
                k_cos(p, 1)
                dve.wait_ge(s["expd"], p + 1)
                dve.tensor_reduce(ssum[:], probs[:].rearrange("p t w r -> p t r w"), AX_X, ALU.add).then_inc(s["ssum"], 1)
                dve.wait_ge(s["ssum"], p + 1)
                dve.reciprocal(srec[:], ssum[:]).then_inc(s["srec"], 1)
                dve.wait_ge(s["srec"], p + 1)
                dve.tensor_tensor(probs[:], probs[:], by_row(srec), ALU.mult).then_inc(s["norm"], 1)
                dve.wait_ge(s["v_ev"], p + 1)
                for w in range(WIN):
                    dve.wait_ge(s["e"], WIN * p + w + 1)
                    if w % 2 == 0:
                        after(dve, s["pair"], 8 * p + max(w // 2 - 1, 0))
                    dve.tensor_tensor(ev[:, w % 4], e_ps[w % 2][:], vpad[:, w:w + D], ALU.mult).then_inc(s["ev"], 1)

            dve.wait_ge(s["x0_in"], 16)
            norm.moments_of(dve, x_all[:, 0], 0)
            norm.apply(dve, xn[:], x_all[:, 0], 0)
            for k in range(KT):
                dve.wait_ge(s["ctx_hi"], k + 1)
                dve.tensor_tensor(ctxTl[:, k], big[:, k], ctxTh[:, k].bitcast(F32), ALU.subtract).then_inc(s["ctx_lo"], 1)
            dve.wait_ge(s["x_in"], 16)
            dve.wait_ge(s["small_in"], SMALL)
            body(0)
            with dve.Fori(1, PAIRS - 1) as p:
                body(p)
            body(PAIRS - 1, more=False)

        @block.tensor
        def _(pe):
            def k_proj(h):
                return three_passes(pe, kv_ps[1 - h][:], lambda k: (wh[:, k], wl[:, k]),
                                    lambda k: (ctxTh[:, k, h * D:h * D + D], ctxTl[:, k, h * D:h * D + D]), KT)

            def v_proj(h):
                return three_passes(pe, kv_ps[1 - h][:], lambda k: (tokh[:, k], tokl[:, k]),
                                    lambda k: (wvh[:, k, h * D:h * D + D], wvl[:, k, h * D:h * D + D]), KT)

            def q_and_k(p):
                pe.wait_ge(norm.applied, p + 1)
                pe.matmul(q_ps[:], w_diag[:, 0], xn[:], start=True, stop=True).then_inc(s["l0q"], 1)
                pe.wait_ge(s["ctx_in"], 16 * p + 16)
                if not isinstance(p, int) or p >= 2:
                    pe.wait_ge(s["o_ev"], p - 1)
                pe.matmul(k_ps[:], w_diag[:, 1], tile_of(ctx_t, p % 2), start=True, stop=True).then_inc(s["l0k"], 1)

            def out_sum(p, j):
                pe.wait_ge(s["quad"], QUADS * p + j + 1)
                pe.matmul(po[:], w_diag[:, 3], evs[:, 2 * j % 4], start=(j == 0), stop=(j == QUADS - 1))\
                    .then_inc(s["osum"], 1)

            def body(p, more=True, before=True):
                after(pe, s["v1_ev"], p)
                pe.matmul(kv_ps[0][:], w_diag[:, 2], tile_of(ctx_t, p % 2), start=True, stop=True).then_inc(s["l0v"], 1)
                for w in range(WIN):
                    pe.wait_ge(s["prod"], WIN * p + w + 1)
                    c = (7 - w % 8) * ROWS0
                    pe.matmul(s_ps[:, w // 8], pick[:, c:c + P], prod[:, w % 4], start=(w % 8 == 0),
                              stop=(w % 8 == 7)).then_inc(s["score"], 1)
                    if w == 1 and before:
                        out_sum(p - 1, QUADS - 1)
                    if w == 4:
                        pe.wait_ge(s["wlo"], p + 1)
                        after(pe, s["v0_ev"], p)
                        if isinstance(p, int) and p == 0:
                            pe.wait_ge(s["ctx_lo"], KT)
                        k_proj(0).then_inc(s["k0"], 1)
                pe.wait_ge(s["v_ev"], p + 1)
                k_proj(1).then_inc(s["k1"], 1)
                pe.wait_ge(s["sT_ev"], 2 * p + 2)
                for t in range(4):
                    for h in range(2):
                        c = (2 * (t % 2) + h) * P
                        last = pe.transpose(s_ps[:, t // 2, c:c + P], sT[:, h, t * P:t * P + P], ident[:])
                last.then_inc(s["sc"], 1)
                pe.wait_ge(s["ksw"], 4 * p + 2)
                pe.wait_ge(s["kcos"], 2 * p + 1)
                pe.wait_ge(s["tok"], p + 1)
                if isinstance(p, int) and p == 0:
                    pe.wait_ge(s["wv_lo"], KT)
                v_proj(0).then_inc(s["v0"], 1)
                if more:
                    q_and_k(p + 1)
                pe.wait_ge(s["ksw"], 4 * p + 4)
                pe.wait_ge(s["kcos"], 2 * p + 2)
                v_proj(1).then_inc(s["v1"], 1)
                for w in range(WIN):
                    pe.wait_ge(s["rep"], WIN * p + w + 1)
                    after(pe, s["ev"], WIN * p + max(w - 1, 0))
                    for t in range(4):
                        last = pe.transpose(e_ps[w % 2][:, t * P:t * P + P], rep[:, w % 2, t], ident[:])
                    last.then_inc(s["e"], 1)
                    if w == 8:
                        if more:
                            pe.wait_ge(s["k_ev"], p + 2)
                        elif before:
                            pe.wait_ge(s["o_ev"], p)
                        out_sum(p, 0)
                    if w == 12:
                        out_sum(p, 1)
                out_sum(p, 2)

            pe.wait_ge(s["small_in"], SMALL)
            pe.wait_ge(s["w_in"], 16)
            q_and_k(0)
            body(0, before=False)
            with pe.Fori(1, PAIRS - 1) as p:
                body(p)
            body(PAIRS - 1, more=False)
            out_sum(PAIRS - 1, QUADS - 1)


class FfnInputs:

    LOADS = 8

    def __init__(self, al):
        self.kern = al.sb("kern", [P, KT, D])
        self.lora_a = al.sb("lora_a", [P, LORA_CHUNKS, D])
        self.lora_b = al.sb("lora_b", [P, LORA_CHUNKS, D])
        self.gcol = al.sb("gcol", [P, LORA_CHUNKS, PAIRS])
        self.eye_r = al.sb("eye_r", [P, RANK])
        self.a_shared = al.sb("a_shared", [P, KT, RANK])
        self.b_shared = al.sb("b_shared", [RANK + 1, D])
        self.own = al.sb("own", [P, HALF])
        self.loaded = al.sem("ffn_in")

    def load(self, sp, a):
        for tensor, view in ((self.gcol, a["gate"].rearrange("(c p) b -> p c b", p=P)),
                             (self.eye_r, a["eye_r"]), (self.own, a["own"]),
                             (self.lora_a, a["lora_A"].rearrange("(c p) i -> p c i", p=P)),
                             (self.lora_b, a["lora_B"].rearrange("(c p) o -> p c o", p=P)),
                             (self.a_shared, a["A_shared"].rearrange("(k p) r -> p k r", p=P)),
                             (self.b_shared, a["B_shared"]),
                             (self.kern, a["kernel"].rearrange("(k p) o -> p k o", p=P))):
            sp.dma_start(tensor[:], view).then_inc(self.loaded, 16)


def layer_0_ffn(nc, a, x_all, ident, gates, xTh, xTl, ffn, att):
    with ExitStack() as ctx:
        al = Pool(nc, ctx, "f")
        kern, lora_a, lora_b, gcol, eye_r = ffn.kern, ffn.lora_a, ffn.lora_b, ffn.gcol, ffn.eye_r
        a_shared, b_shared, own = ffn.a_shared, ffn.b_shared, ffn.own
        mix = al.sb("mix", [P, LORA_CHUNKS, PAIRS, RANK])
        a_eff = al.sb("a_eff", [P, KT, 2, P])
        b_eff = al.sb("b_eff", [P, 2, D])
        xn, xn2 = al.sb("xn", [P, D]), al.sb("xn2", [P, D])
        norm1, norm2 = RowNorm(al, "norm1"), RowNorm(al, "norm2")
        xnT = al.sb("xnT", [P, KT, P])
        ax = al.sb("ax", [P, P])
        axs = al.sb("axs", [RANK + 1, P])

        t1_ps = al.ps("t1_ps", [P, KT, P])
        ax_ps = al.ps("ax_ps", [P, P])
        axs_ps = al.ps("axs_ps", [RANK, P])
        out_ps = [al.ps("out_ps0", [P, D]), al.ps("out_ps1", [P, D])]
        t2_ps = al.ps("t2_ps", [P, KT, P])
        s = {n: al.sem(n) for n in (
            "mix", "eff", "eff_ev", "t1", "t1_ev", "ax", "ax_ev", "axs_ev", "out", "x2",
            "t2", "hi", "lo", "ones")}
        block = ctx.enter_context(nc.Block())

        @block.sync
        def _(sp):
            att.load_first(sp, a)

        @block.gpsimd
        def _(pool):
            pool.memset(axs[RANK:RANK + 1, :], 1.0).then_inc(s["ones"], 1)
            pool.wait_ge(s["ones"], 1)
            norm1.start(pool)
            norm2.start(pool)
            norm1.root(pool, 0)
            norm1.root(pool, 1)
            att.wq_low(pool, 0)

            def tile(p, more=True):
                norm2.root(pool, p)
                if more:
                    norm1.root(pool, p + 2)

            tile(0)
            with pool.Fori(1, PAIRS - 2) as p:
                tile(p)
            tile(PAIRS - 2, False)
            tile(PAIRS - 1, False)

        @block.scalar
        def _(act):
            for k in range(KT):
                act.wait_ge(s["eff"], k + 1)
                act.activation(a_eff[:, k], (out_ps[k % 2][:, 0:2 * P]).rearrange("p (h n) -> p h n", h=2),
                               ACT.Copy).then_inc(s["eff_ev"], 1)
            for h in range(2):
                act.wait_ge(s["eff"], KT + h + 1)
                act.activation(b_eff[:, h], out_ps[h][:], ACT.Copy).then_inc(s["eff_ev"], 1)
            att.wq_high(act, 0)

            def tile(p, before=True):
                act.wait_ge(s["t1"], p + 1)
                after(act, s["out"], p)
                act.activation(xnT[:], t1_ps[:], ACT.Copy).then_inc(s["t1_ev"], 1)
                act.wait_ge(s["ax"], p + 1)
                act.activation(axs[0:RANK, :], axs_ps[:], ACT.Copy).then_inc(s["axs_ev"], 1)
                if before:
                    high(p - 1)

            def high(p):
                act.wait_ge(s["t2"], p + 1)
                act.activation(xTh[:, :, ds(p * P, P)], t2_ps[:], ACT.Copy).then_inc(s["hi"], 1)

            tile(0, before=False)
            with act.Fori(1, PAIRS) as p:
                tile(p)
            high(PAIRS - 1)

        @block.vector
        def _(dve):
            def norm(p):
                norm1.moments_of(dve, tile_of(x_all, p), p)
                after(dve, s["t1"], p)
                norm1.apply(dve, xn[:], tile_of(x_all, p), p)

            def middle(p, q):
                dve.wait_ge(s["ax"], p + 1)
                after(dve, s["out"], p)
                dve.tensor_scalar(ax[:], ax_ps[:], own[:, ds(q, 1)], None, ALU.mult).then_inc(s["ax_ev"], 1)

            def update(p):
                xp = tile_of(x_all, p)
                dve.wait_ge(s["out"], p + 1)
                dve.scalar_tensor_tensor(xp, out_ps[0][:], gates[:, 2:3], xp, ALU.mult, ALU.add).then_inc(s["x2"], 1)
                dve.wait_ge(s["x2"], p + 1)
                norm2.moments_of(dve, xp, p)
                after(dve, s["t2"], p)
                norm2.apply(dve, xn2[:], xp, p)

            def low(p):
                dve.wait_ge(s["hi"], p + 1)
                cols = ds(p * P, P)
                dve.tensor_tensor(xTl[:, :, cols], t2_ps[:], xTh[:, :, cols].bitcast(F32), ALU.subtract)\
                    .then_inc(s["lo"], 1)

            def tile(p, q, more=True):
                update(p)
                middle(p + 1, q)
                low(p)
                if more:
                    norm(p + 2)

            norm(0)
            dve.wait_ge(ffn.loaded, 16 * ffn.LOADS)
            for c in range(LORA_CHUNKS):
                dve.tensor_tensor(mix[:, c], gcol[:, c].rearrange("p (b o) -> p b o", o=1).broadcast_to([P, PAIRS, RANK]),
                                  eye_r[:].rearrange("p (o r) -> p o r", o=1).broadcast_to([P, PAIRS, RANK]),
                                  ALU.mult).then_inc(s["mix"], 1)
            middle(0, 0)
            norm(1)
            tile(0, 1)
            with dve.Fori(1, HALF - 1) as p:
                tile(p, p + 1)
            tile(HALF - 1, 0)
            with dve.Fori(HALF, PAIRS - 2) as p:
                tile(p, p - (HALF - 1))
            tile(PAIRS - 2, HALF - 1, more=False)
            update(PAIRS - 1)
            low(PAIRS - 1)

        @block.tensor
        def _(pe):
            pe.wait_ge(s["mix"], LORA_CHUNKS)
            for k in range(KT):
                after(pe, s["eff_ev"], max(k - 1, 0))
                for h in range(2):
                    for c in range(LORA_CHUNKS):
                        last = pe.matmul(out_ps[k % 2][:, h * P:h * P + P], lora_a[:, c, k * P:k * P + P],
                                         mix[:, c, h * HALF:h * HALF + HALF].rearrange("p b r -> p (b r)"),
                                         start=(c == 0), stop=(c == LORA_CHUNKS - 1))
                last.then_inc(s["eff"], 1)
            for h in range(2):
                pe.wait_ge(s["eff_ev"], KT - 1 + h)
                for c in range(LORA_CHUNKS):
                    last = pe.matmul(out_ps[h][:], mix[:, c, h * HALF:h * HALF + HALF].rearrange("p b r -> p (b r)"),
                                     lora_b[:, c], start=(c == 0), stop=(c == LORA_CHUNKS - 1))
                last.then_inc(s["eff"], 1)
            pe.wait_ge(s["eff_ev"], KT + 2)
            pe.wait_ge(s["ones"], 1)

            def first(p, h):
                pe.wait_ge(norm1.applied, p + 1)
                after(pe, s["t1_ev"], p)
                for k in range(KT):
                    last = pe.transpose(t1_ps[:, k], xn[:, k * P:k * P + P], ident[:])
                last.then_inc(s["t1"], 1)
                pe.wait_ge(s["t1_ev"], p + 1)
                after(pe, s["ax_ev"], p)
                for k in range(KT):
                    pe.matmul(ax_ps[:], a_eff[:, k, h], xnT[:, k], start=(k == 0), stop=(k == KT - 1))
                after(pe, s["axs_ev"], p)
                for k in range(KT):
                    last = pe.matmul(axs_ps[:], a_shared[:, k], xnT[:, k], start=(k == 0), stop=(k == KT - 1))
                last.then_inc(s["ax"], 1)
                after(pe, s["x2"], p)
                for k in range(KT):
                    pe.matmul(out_ps[0][:], xnT[:, k], kern[:, k], start=(k == 0), stop=False)

            def second(p):
                pe.wait_ge(norm2.applied, p + 1)
                after(pe, s["lo"], p)
                for k in range(KT):
                    last = pe.transpose(t2_ps[:, k], xn2[:, k * P:k * P + P], ident[:])
                last.then_inc(s["t2"], 1)

            def third(p, h):
                pe.wait_ge(s["ax_ev"], p + 1)
                pe.matmul(out_ps[0][:], ax[:], b_eff[:, h], start=False, stop=False)
                pe.wait_ge(s["axs_ev"], p + 1)
                pe.matmul(out_ps[0][:], axs[:], b_shared[:], start=False, stop=True).then_inc(s["out"], 1)

            first(0, 0)
            third(0, 0)
            first(1, 0)
            second(0)
            third(1, 0)
            for h, begin, end in ((0, 2, HALF), (1, HALF, PAIRS)):
                with pe.Fori(begin, end) as p:
                    first(p, h)
                    second(p - 1)
                    third(p, h)
            second(PAIRS - 1)


class AttentionInputs:

    def __init__(self, al, k_dram, v_dram):
        self.cosq, self.sinq = al.sb("cosq", [P, SEQ]), al.sb("sinq", [P, SEQ])
        self.cap = al.sb("cap", [P, PAIRS, 2, SEQ])
        self.wq_land = al.sb("wq_land", [P, KT, GH * DK])
        self.wqh, self.wql = al.sb("wqh", [P, KT, GH * DK], F32R), al.sb("wql", [P, KT, GH * DK], F32R)
        self.wo_land = al.sb("wo_land", [P, GH, D])
        self.kT = al.sb("kT", [P, PAIRS * P])
        self.vr = al.sb("vr", [P, PAIRS, DK])
        self.s = {n: al.sem(n) for n in ("tab_in", "mask_in", "wq_in", "wo_in", "k_in", "v_in", "wq_hi", "wq_lo")}
        self.k_dram, self.v_dram = k_dram, v_dram

    def load_wq(self, sp, a, g):
        sp.dma_start(self.wq_land[:], a["wq"].rearrange("(k p) n -> p k n", p=P)[:, :, ds(g * (GH * DK), GH * DK)])\
          .then_inc(self.s["wq_in"], 16)

    def load_wo(self, sp, a, g):
        sp.dma_start(self.wo_land[:], a["wo"].rearrange("(h p) n -> p h n", p=P)[:, ds(g * GH, GH), :])\
          .then_inc(self.s["wo_in"], 16)

    def load_k(self, sp, g):
        sp.dma_start(self.kT[:], self.k_dram[ds(g, 1)].rearrange("o p n -> p (o n)")).then_inc(self.s["k_in"], 16)

    def load_v(self, sp, g):
        sp.dma_start(self.vr[:], self.v_dram[ds(g, 1)].rearrange("o p t n -> p (o t) n")).then_inc(self.s["v_in"], 16)

    def load_first(self, sp, a):
        self.load_wq(sp, a, 0)
        sp.dma_start(self.cosq[:], a["cosq"]).then_inc(self.s["tab_in"], 16)
        sp.dma_start(self.sinq[:], a["sinq"]).then_inc(self.s["tab_in"], 16)
        for h in (0, 64):
            sp.dma_start(self.cap[h:h + 64].rearrange("p t b k -> p (t b) k"), a["mask"].rearrange("b q k -> q b k"))\
              .then_inc(self.s["mask_in"], 16)
        self.load_k(sp, 0)
        self.load_wo(sp, a, 0)
        self.load_v(sp, 0)
        sp.wait_ge(self.s["wq_lo"], KT)
        self.load_wq(sp, a, 1)

    def wq_high(self, act, g):
        act.wait_ge(self.s["wq_in"], 16 * g + 16)
        for k in range(KT):
            act.activation(self.wqh[:, k], self.wq_land[:, k], ACT.Copy).then_inc(self.s["wq_hi"], 1)

    def wq_low(self, pool, g):
        for k in range(KT):
            pool.wait_ge(self.s["wq_hi"], KT * g + k + 1)
            pool.tensor_tensor(self.wql[:, k], self.wq_land[:, k], self.wqh[:, k].bitcast(F32), ALU.subtract)\
                .then_inc(self.s["wq_lo"], 1)


def layer_1_attention(nc, a, x_all, gates, ident, xTh, xTl, att):
    with ExitStack() as ctx:
        al = Pool(nc, ctx, "g")
        cosq, sinq, cap, wqh, wql = att.cosq, att.sinq, att.cap, att.wqh, att.wql
        wo_land, kT, vr = att.wo_land, att.kT, att.vr
        woh, wol = al.sb("woh", [P, GH, D], F32R), al.sb("wol", [P, GH, D], F32R)
        qT = al.sb("qT", [P, BATCH, GH, SEQ])
        qcos, qsw = al.sb("qcos", [P, 2, D]), al.sb("qsw", [P, 2, D])
        S = al.sb("S", [P, PAIRS, 2, P])
        smax, ssum, srec = (al.sb(n, [P, PAIRS, 4]) for n in ("smax", "ssum", "srec"))
        PT = al.sb("PT", [P, PAIRS, 2 * P])
        oh, ol = al.sb("oh", [P, 2, GH, P], F32R), al.sb("ol", [P, 2, GH, P], F32R)

        a_ps = [al.ps("a_ps0", [P, D]), al.ps("a_ps1", [P, D])]
        s_ps = [al.ps("s_ps0", [P, D]), al.ps("s_ps1", [P, D])]
        o_ps = [[al.ps(f"o_ps{r}{b}", [P, D]) for b in range(2)] for r in range(2)]
        s = {n: al.sem(n) for n in (
            "cap0", "wo_hi", "wo_lo",
            "q", "qsw", "qcos", "qsin", "qrot", "score", "cap", "mx", "sub", "expd", "ssum", "srec", "norm",
            "t", "pt", "av", "ohi", "olo", "wo", "x")}
        s.update(att.s)
        QT = 2 * GH
        CH = 4
        per_seq = "p (b q) -> p b q"
        block = ctx.enter_context(nc.Block())

        @block.sync
        def _(sp):
            def group(g, wq=True):
                if wq:
                    sp.wait_ge(s["wq_lo"], KT * g + 2 * KT)
                    att.load_wq(sp, a, g + 2)
                sp.wait_ge(s["score"], CH * g + CH)
                att.load_k(sp, g + 1)
                sp.wait_ge(s["wo_lo"], GH * g + GH)
                att.load_wo(sp, a, g + 1)
                sp.wait_ge(s["av"], PAIRS * g + PAIRS)
                att.load_v(sp, g + 1)

            group(0)
            with sp.Fori(1, GROUPS - 2) as g:
                group(g)
            group(GROUPS - 2, wq=False)

        @block.scalar
        def _(act):
            def swap(g, i):
                n = QT * g + i
                act.wait_ge(s["q"], n + 1)
                if i >= 2 or not isinstance(g, int) or g > 0:
                    act.wait_ge(s["qrot"], n - 1)
                for h in (0, 64):
                    act.activation(qsw[h:h + 64, i % 2], a_ps[i % 2][64 - h:128 - h, :], ACT.Copy)\
                       .then_inc(s["qsw"], 1)

            def exp(g, c):
                act.wait_ge(s["sub"], CH * g + c + 1)
                t = S[:, 2 * c:2 * c + 2]
                act.activation(t, t, ACT.Exp).then_inc(s["expd"], 1)

            def group(g, q=True, wq=True):
                act.wait_ge(s["wo_in"], 16 * g + 16)
                after(act, s["wo"], PAIRS * g)
                for h in range(GH):
                    act.activation(woh[:, h], wo_land[:, h], ACT.Copy).then_inc(s["wo_hi"], 1)
                for i in range(QT):
                    if q:
                        swap(g + 1, i)
                    if 1 <= i <= CH:
                        exp(g, i - 1)

                def out_high(t):
                    act.wait_ge(s["av"], PAIRS * g + t + 1)
                    after(act, s["wo"], PAIRS * g + max(t - 1, 0))
                    for b in range(2):
                        act.activation(oh[:, t % 2, :, b * SEQ:b * SEQ + SEQ],
                                       o_ps[t % 2][b][:, 0:GH * SEQ].rearrange("p (h q) -> p h q", h=GH),
                                       ACT.Copy).then_inc(s["ohi"], 1)

                for t in range(PAIRS):
                    act.wait_ge(s["t"], PAIRS * g + t + 1)
                    act.activation(PT[:, t], s_ps[t % 2][:, 0:2 * P], ACT.Copy).then_inc(s["pt"], 1)
                    if t:
                        out_high(t - 1)
                    if t == 2 and wq:
                        act.wait_ge(s["q"], QT * (g + 2))
                        att.wq_high(act, g + 2)
                out_high(PAIRS - 1)

            for i in range(QT):
                swap(0, i)
            act.wait_ge(s["q"], QT)
            att.wq_high(act, 1)
            group(0)
            with act.Fori(1, GROUPS - 2) as g:
                group(g)
            group(GROUPS - 2, wq=False)
            group(GROUPS - 1, q=False, wq=False)

        @block.gpsimd
        def _(pool):
            def sine(g, i):
                n = QT * g + i
                pool.wait_ge(s["qsw"], 2 * n + 2)
                t = qsw[:, i % 2].rearrange(per_seq, q=SEQ)
                pool.tensor_tensor(t, t, sinq[:].rearrange("p (o q) -> p o q", o=1).broadcast_to([P, D // SEQ, SEQ]),
                                   ALU.mult).then_inc(s["qsin"], 1)

            def group(g, q=True, wq=True):
                after(pool, s["wo"], PAIRS * g)
                for h in range(GH):
                    pool.wait_ge(s["wo_hi"], GH * g + h + 1)
                    pool.tensor_tensor(wol[:, h], wo_land[:, h], woh[:, h].bitcast(F32), ALU.subtract)\
                        .then_inc(s["wo_lo"], 1)
                if q:
                    for i in range(QT):
                        sine(g + 1, i)
                if wq:
                    att.wq_low(pool, g + 2)

            pool.wait_ge(s["tab_in"], 32)
            for i in range(QT):
                sine(0, i)
            att.wq_low(pool, 1)
            group(0)
            with pool.Fori(1, GROUPS - 2) as g:
                group(g)
            group(GROUPS - 2, wq=False)
            group(GROUPS - 1, q=False, wq=False)

        @block.vector
        def _(dve):
            dve.wait_ge(s["tab_in"], 32)
            dve.wait_ge(s["mask_in"], 32)
            flat = cap[:].rearrange("p t b k -> p (t b k)")
            dve.tensor_scalar(flat, flat, 0.0, HUGE, ALU.not_equal, ALU.mult).then_inc(s["cap0"], 1)
            dve.wait_ge(s["cap0"], 1)
            dve.tensor_scalar(flat, flat, MASKED, None, ALU.add).then_inc(s["cap0"], 1)
            dve.wait_ge(s["cap0"], 2)

            def cosine(g, i):
                n = QT * g + i
                dve.wait_ge(s["qsw"], 2 * n + 2)
                dve.tensor_tensor(qcos[:, i % 2].rearrange(per_seq, q=SEQ), a_ps[i % 2][:].rearrange(per_seq, q=SEQ),
                                  cosq[:].rearrange("p (o q) -> p o q", o=1).broadcast_to([P, D // SEQ, SEQ]),
                                  ALU.mult).then_inc(s["qcos"], 1)

            def rotate(g, i):
                n = QT * g + i
                if i == 0:
                    after(dve, s["score"], CH * g)
                dve.wait_ge(s["qcos"], n + 1)
                dve.wait_ge(s["qsin"], n + 1)
                h, half = i // 2, i % 2
                dve.tensor_tensor(qT[:, half * 8:half * 8 + 8, h, :], qcos[:, i % 2].rearrange(per_seq, q=SEQ),
                                  qsw[:, i % 2].rearrange(per_seq, q=SEQ), ALU.add).then_inc(s["qrot"], 1)

            def rows(t, c):
                return t[:, 2 * c:2 * c + 2].rearrange("p t n -> p (t n)").rearrange("p (n o) -> p n o", o=1)\
                    .broadcast_to([P, 8, SEQ])

            def chunk(c):
                return S[:, 2 * c:2 * c + 2].rearrange("p t h n -> p (t h n)").rearrange("p (n k) -> p n k", k=SEQ)

            def stat(t, c):
                return t[:, 2 * c:2 * c + 2].rearrange("p t n -> p (t n)")

            def group(g, q=True):
                after(dve, s["t"], PAIRS * g)
                for c in range(CH):
                    dve.wait_ge(s["score"], CH * g + c + 1)
                    for t in range(2):
                        last = dve.tensor_tensor(
                            S[:, 2 * c + t], s_ps[c % 2][:, t * 2 * P:(t + 1) * 2 * P].rearrange("p (h n) -> p h n", h=2),
                            cap[:, 2 * c + t].rearrange("p b k -> p (b k)").rearrange("p (o n) -> p o n", o=1)
                            .broadcast_to([P, 2, P]), ALU.min)
                    last.then_inc(s["cap"], 1)
                for i in range(QT + 1):
                    if q and i < QT:
                        cosine(g + 1, i)
                    if i < CH:
                        c = i
                        dve.wait_ge(s["cap"], CH * g + c + 1)
                        dve.tensor_reduce(stat(smax, c), chunk(c), AX_X, ALU.max).then_inc(s["mx"], 1)
                        dve.wait_ge(s["mx"], CH * g + c + 1)
                        dve.tensor_tensor(chunk(c), chunk(c), rows(smax, c), ALU.subtract).then_inc(s["sub"], 1)
                    if q and i >= 1:
                        rotate(g + 1, i - 1)
                    if 2 <= i < CH + 2:
                        c = i - 2
                        dve.wait_ge(s["expd"], CH * g + c + 1)
                        dve.tensor_reduce(stat(ssum, c), chunk(c), AX_X, ALU.add).then_inc(s["ssum"], 1)
                        dve.wait_ge(s["ssum"], CH * g + c + 1)
                        dve.reciprocal(stat(srec, c), stat(ssum, c)).then_inc(s["srec"], 1)
                        dve.wait_ge(s["srec"], CH * g + c + 1)
                        dve.tensor_tensor(chunk(c), chunk(c), rows(srec, c), ALU.mult).then_inc(s["norm"], 1)

                def add(t):
                    dve.wait_ge(s["wo"], PAIRS * g + t + 1)
                    after(dve, s["x"], PAIRS * g)
                    dve.scalar_tensor_tensor(x_all[:, t], a_ps[t % 2][:], gates[:, 1:2], x_all[:, t],
                                             ALU.mult, ALU.add).then_inc(s["x"], 1)

                for t in range(PAIRS):
                    for b in range(2):
                        dve.wait_ge(s["ohi"], 2 * (PAIRS * g + t) + b + 1)
                        cols = slice(b * SEQ, b * SEQ + SEQ)
                        dve.tensor_tensor(ol[:, t % 2, :, cols],
                                          o_ps[t % 2][b][:, 0:GH * SEQ].rearrange("p (h q) -> p h q", h=GH),
                                          oh[:, t % 2, :, cols].bitcast(F32), ALU.subtract).then_inc(s["olo"], 1)
                    if t:
                        add(t - 1)
                add(PAIRS - 1)

            for i in range(QT + 1):
                if i < QT:
                    cosine(0, i)
                if i:
                    rotate(0, i - 1)
            group(0)
            with dve.Fori(1, GROUPS - 1) as g:
                group(g)
            group(GROUPS - 1, q=False)

        @block.tensor
        def _(pe):
            def project_q(g, i):
                n = QT * g + i
                if i == 0:
                    pe.wait_ge(s["wq_lo"], KT * g + KT)
                if i >= 2:
                    pe.wait_ge(s["qcos"], n - 1)
                elif not isinstance(g, int) or g > 0:
                    after(pe, s["x"], PAIRS * (g - 1))
                h, half = i // 2, i % 2
                three_passes(pe, a_ps[i % 2][:], lambda k: (wqh[:, k, h * DK:h * DK + DK], wql[:, k, h * DK:h * DK + DK]),
                             lambda k: (xTh[:, k, half * D:half * D + D], xTl[:, k, half * D:half * D + D]), KT)\
                    .then_inc(s["q"], 1)

            def group(g, q=True):
                pe.wait_ge(s["qrot"], QT * g + QT)
                pe.wait_ge(s["k_in"], 16 * g + 16)
                for c in range(CH):
                    if c < 2:
                        after(pe, s["pt"], PAIRS * g)
                    else:
                        pe.wait_ge(s["cap"], CH * g + c - 1)
                    for t in range(2):
                        for h in range(2):
                            for b in range(2):
                                n = 4 * c + 2 * t + b
                                col = ((2 * t + h) * 2 + b) * SEQ
                                last = pe.matmul(s_ps[c % 2][:, col:col + SEQ],
                                                 qT[:, n, 2 * h:2 * h + 2, :].rearrange("p h q -> p (h q)"),
                                                 kT[:, n * SEQ:n * SEQ + SEQ], start=True, stop=True)
                    last.then_inc(s["score"], 1)
                if q:
                    for i in range(QT):
                        project_q(g + 1, i)
                pe.wait_ge(s["cap"], CH * g + CH)
                pe.wait_ge(s["v_in"], 16 * g + 16)

                def attend(t):
                    pe.wait_ge(s["pt"], PAIRS * g + t + 1)
                    after(pe, s["olo"], 2 * (PAIRS * g + max(t - 1, 0)))
                    for b in range(2):
                        r = slice(b * SEQ, b * SEQ + SEQ)
                        last = pe.matmul(o_ps[t % 2][b][:, 0:GH * SEQ], vr[r, t, :], PT[r, t, :],
                                         start=True, stop=True)
                    last.then_inc(s["av"], 1)

                def project_out(t):
                    if t == 0:
                        pe.wait_ge(s["wo_lo"], GH * g + GH)
                        pe.wait_ge(s["qcos"], QT * (g + 2) if q else QT * GROUPS)
                    if t >= 2:
                        pe.wait_ge(s["x"], PAIRS * g + t - 1)
                    pe.wait_ge(s["olo"], 2 * (PAIRS * g + t) + 2)
                    three_passes(pe, a_ps[t % 2][:], lambda h: (oh[:, t % 2, h], ol[:, t % 2, h]),
                                 lambda h: (woh[:, h], wol[:, h]), GH).then_inc(s["wo"], 1)

                for t in range(PAIRS + 2):
                    if t < PAIRS:
                        pe.wait_ge(s["norm"], CH * g + t // 2 + 1)
                        if t >= 2:
                            pe.wait_ge(s["pt"], PAIRS * g + t - 1)
                        for h in range(2):
                            last = pe.transpose(s_ps[t % 2][:, h * P:h * P + P], S[:, t, h], ident[:])
                        last.then_inc(s["t"], 1)
                    if 1 <= t <= PAIRS:
                        attend(t - 1)
                    if t >= 2:
                        project_out(t - 2)

            for i in range(QT):
                project_q(0, i)
            group(0)
            with pe.Fori(1, GROUPS - 1) as g:
                group(g)
            group(GROUPS - 1, q=False)


def layer_1_ffn(nc, a, x_all, ident, gates, out):
    with ExitStack() as ctx:
        al = Pool(nc, ctx, "h")
        router_a = al.sb("router_a", [P, KT, MID + EXPERTS])
        b_all = al.sb("b_all", [MID, D])
        g4 = al.sb("g4", [P, 1])
        xn = al.sb("xn", [P, 2, D])
        norm = RowNorm(al, "norm")
        xnT = al.sb("xnT", [P, 2, KT, P])
        mid = al.sb("mid", [P, PAIRS, MID + EXPERTS])
        beats = al.sb("beats", [P, PAIRS, EXPERTS, EXPERTS])
        ties = al.sb("ties", [P, PAIRS, EXPERTS, EXPERTS])
        first = al.sb("first", [P, EXPERTS, EXPERTS])
        rank = al.sb("rank", [P, PAIRS, EXPERTS])
        chosen = al.sb("chosen", [P, PAIRS, EXPERTS])
        top = al.sb("top", [P, PAIRS])
        e = al.sb("e", [P, PAIRS, EXPERTS])
        total = al.sb("total", [P, PAIRS])
        inverse = al.sb("inverse", [P, PAIRS])
        midT = al.sb("midT", [MID, 2, P])
        t_ps = [al.ps(f"t_ps{i}", [P, KT, P]) for i in range(2)]
        m_ps = [al.ps(f"m_ps{i}", [P, MID + EXPERTS]) for i in range(2)]
        d_ps = [al.ps(f"d_ps{i}", [P, D]) for i in range(2)]
        s = {n: al.sem(n) for n in ("in", "g4", "t", "t_ev", "m", "m_ev", "gate", "expd", "mt", "mt_ev",
                                    "d", "x", "out")}
        block = ctx.enter_context(nc.Block())

        @block.sync
        def _(sp):
            sp.dma_start(router_a[:], a["router_A"].rearrange("(k p) n -> p k n", p=P)).then_inc(s["in"], 16)
            sp.dma_start(b_all[:], a["B"]).then_inc(s["in"], 16)
            sp.dma_start(first[:].rearrange("p a b -> p (a b)"), a["first"]).then_inc(s["in"], 16)
            out_rows = out.rearrange("(t p) d -> p t d", p=P)
            for t in range(PAIRS):
                sp.wait_ge(s["x"], t + 1)
                sp.dma_start(out_rows[:, t], x_all[:, t]).then_inc(s["out"], 16)
            sp.wait_ge(s["out"], 16 * PAIRS)

        @block.gpsimd
        def _(pool):
            norm.start(pool)
            for t in range(PAIRS):
                norm.root(pool, t)

        @block.scalar
        def _(act):
            act.activation(g4[:], gates[:, 3:4], ACT.Copy, scale=LORA_SCALE).then_inc(s["g4"], 1)
            for t in range(PAIRS):
                act.wait_ge(s["t"], t + 1)
                after(act, s["m"], t - 1)
                act.activation(xnT[:, t % 2], t_ps[t % 2][:], ACT.Copy).then_inc(s["t_ev"], 1)
            act.wait_ge(s["gate"], 1)
            act.activation(e[:], e[:], ACT.Exp).then_inc(s["expd"], 1)
            for t in range(PAIRS):
                act.wait_ge(s["mt"], t + 1)
                after(act, s["d"], t - 1)
                act.activation(midT[:, t % 2], t_ps[t % 2][0:MID, 0], ACT.Copy).then_inc(s["mt_ev"], 1)

        @block.vector
        def _(dve):
            for t in range(PAIRS):
                norm.moments_of(dve, x_all[:, t], t)
                after(dve, s["t"], t - 1)
                norm.apply(dve, xn[:, t % 2], x_all[:, t], t)
                if t:
                    dve.wait_ge(s["m"], t)
                    dve.tensor_copy(mid[:, t - 1], m_ps[(t - 1) % 2][:]).then_inc(s["m_ev"], 1)
            dve.wait_ge(s["m"], PAIRS)
            dve.tensor_copy(mid[:, PAIRS - 1], m_ps[(PAIRS - 1) % 2][:]).then_inc(s["m_ev"], 1)
            dve.wait_ge(s["m_ev"], PAIRS)
            dve.wait_ge(s["in"], 48)
            step = [0]

            def link(instruction):
                step[0] += 1
                instruction.then_inc(chain, 1)
                dve.wait_ge(chain, step[0])

            chain = al.sem("chain")
            logits = mid[:, :, MID:]
            rival = logits.rearrange("p t (o j) -> p t o j", o=1).broadcast_to([P, PAIRS, EXPERTS, EXPERTS])
            own = logits.rearrange("p t (j o) -> p t j o", o=1).broadcast_to([P, PAIRS, EXPERTS, EXPERTS])
            link(dve.tensor_tensor(beats[:], rival, own, ALU.is_gt))
            link(dve.tensor_tensor(ties[:], rival, own, ALU.is_equal))
            link(dve.tensor_tensor(ties[:], ties[:], first[:].rearrange("p (o i) j -> p o i j", o=1)
                                   .broadcast_to([P, PAIRS, EXPERTS, EXPERTS]), ALU.mult))
            link(dve.tensor_tensor(beats[:], beats[:], ties[:], ALU.add))
            link(dve.tensor_reduce(rank[:], beats[:], AX_X, ALU.add))
            link(dve.tensor_scalar(chosen[:], rank[:], 1.5, None, ALU.is_lt))
            link(dve.tensor_reduce(top[:], logits, AX_X, ALU.max))
            dve.tensor_tensor(e[:], logits, top[:].rearrange("p (t o) -> p t o", o=1)
                              .broadcast_to([P, PAIRS, EXPERTS]), ALU.subtract).then_inc(s["gate"], 1)
            dve.wait_ge(s["expd"], 1)
            link(dve.tensor_tensor(e[:], e[:], chosen[:], ALU.mult))
            link(dve.tensor_reduce(total[:], e[:], AX_X, ALU.add))
            link(dve.reciprocal(inverse[:], total[:]))
            link(dve.tensor_tensor(e[:], e[:], inverse[:].rearrange("p (t o) -> p t o", o=1)
                                   .broadcast_to([P, PAIRS, EXPERTS]), ALU.mult))
            weighed = mid[:, :, 0:MID].rearrange("p t (e r) -> p t e r", e=EXPERTS)
            for t in range(PAIRS):
                last = dve.tensor_tensor(weighed[:, t], weighed[:, t], e[:, t].rearrange("p (e o) -> p e o", o=1)
                                         .broadcast_to([P, EXPERTS, ERANK]), ALU.mult)
            last.then_inc(s["gate"], 1)
            dve.wait_ge(s["g4"], 1)
            for t in range(PAIRS):
                dve.wait_ge(s["d"], t + 1)
                dve.scalar_tensor_tensor(x_all[:, t], d_ps[t % 2][:], g4[:], x_all[:, t], ALU.mult, ALU.add)\
                   .then_inc(s["x"], 1)

        @block.tensor
        def _(pe):
            pe.wait_ge(s["in"], 48)

            def logits(t):
                pe.wait_ge(s["t_ev"], t + 1)
                after(pe, s["m_ev"], t - 1)
                for k in range(KT):
                    last = pe.matmul(m_ps[t % 2][:], xnT[:, t % 2, k], router_a[:, k], start=(k == 0), stop=(k == KT - 1))
                last.then_inc(s["m"], 1)

            for t in range(PAIRS):
                pe.wait_ge(norm.applied, t + 1)
                after(pe, s["t_ev"], t - 1)
                for k in range(KT):
                    last = pe.transpose(t_ps[t % 2][:, k], xn[:, t % 2, k * P:k * P + P], ident[:])
                last.then_inc(s["t"], 1)
                if t:
                    logits(t - 1)
            logits(PAIRS - 1)
            pe.wait_ge(s["gate"], 2)
            pe.wait_ge(s["t_ev"], PAIRS)

            def delta(t):
                pe.wait_ge(s["mt_ev"], t + 1)
                after(pe, s["x"], t - 1)
                pe.matmul(d_ps[t % 2][:], midT[:, t % 2], b_all[:], start=True, stop=True).then_inc(s["d"], 1)

            for t in range(PAIRS):
                after(pe, s["mt_ev"], t - 1)
                pe.transpose(t_ps[t % 2][0:MID, 0], mid[:, t, 0:MID], ident[:]).then_inc(s["mt"], 1)
                if t:
                    delta(t - 1)
            delta(PAIRS - 1)


def flamingo_gated(nc, a, out):
    k_dram = nc.dram_tensor("k_scratch", (GROUPS, P, PAIRS * P), F32, kind="Internal").ap()
    v_dram = nc.dram_tensor("v_scratch", (GROUPS, P, PAIRS, DK), F32, kind="Internal").ap()
    with ExitStack() as ctx:
        al = Pool(nc, ctx, "all")
        x_all = al.sb("x_all", [P, PAIRS, D])
        ident = al.sb("ident", [P, P])
        gates = al.sb("gates", [P, 4])
        with ExitStack() as inner:
            ffn = FfnInputs(Pool(nc, inner, "ffn"))
            layer_0_attention(nc, a, x_all, ident, gates, k_dram, v_dram, ffn)
            al = Pool(nc, inner, "att")
            xTh = al.sb("xTh", [P, KT, PAIRS * P], F32R)
            xTl = al.sb("xTl", [P, KT, PAIRS * P], F32R)
            att = AttentionInputs(al, k_dram, v_dram)
            layer_0_ffn(nc, a, x_all, ident, gates, xTh, xTl, ffn, att)
            layer_1_attention(nc, a, x_all, gates, ident, xTh, xTl, att)
        layer_1_ffn(nc, a, x_all, ident, gates, out)


def rotary_tables(scale):
    freq = 1.0 / np.float32(10000.0) ** (np.arange(0, DK, 2, dtype=np.float32) / np.float32(DK))
    angle = (np.arange(SEQ, dtype=np.float32)[:, None] * freq[None, :]).T.astype(np.float64)
    cos, sin = np.cos(angle) * scale, np.sin(angle) * scale
    return (np.concatenate([cos, cos]).astype(np.float32), np.concatenate([-sin, sin]).astype(np.float32))


def constants():
    c = {"ident": np.eye(P, dtype=np.float32)}
    pick = np.zeros((P, 15 * ROWS0), np.float32)
    pick[np.arange(P), 7 * ROWS0 + np.arange(P) // HD0] = 1.0
    c["pick"] = pick
    c["cosk"], c["sink"] = rotary_tables(1.0)
    c["cosq"], c["sinq"] = rotary_tables(float(DK) ** -0.5)
    c["eye_r"] = (np.arange(P)[:, None] % RANK == np.arange(RANK)[None, :]).astype(np.float32)
    c["own"] = (np.arange(P)[:, None] // RANK == np.arange(HALF)[None, :]).astype(np.float32)
    lower = np.arange(EXPERTS)[None, :] < np.arange(EXPERTS)[:, None]
    c["first"] = np.tile(lower.astype(np.float32).reshape(1, -1), (P, 1))
    return c


def kernel(**inputs):
    import concourse.bacc as bacc
    from concourse.bass_utils import run_bass_kernel_spmd

    i = {k: np.asarray(v) for k, v in inputs.items()}
    rows = BATCH * SEQ
    arrays = {
        "x": i["x"].reshape(rows, D),
        "ctx": i["ctx_4096"].reshape(rows, D),
        "ctxT": i["ctx_4096"].reshape(rows, D).T,
        "mask": i["mask_BxSxS2_ff1"],
        "g4": np.concatenate([i["g_xattn"], i["g_ffn"]]),
        "W4": np.concatenate([i[f"L0_xattn_W{n}"].T for n in "qkvo"], axis=1),
        "b4": np.stack([i[f"L0_xattn_b{n}"] for n in "qkvo"], axis=1),
        "gate": np.repeat(i["L0_ffn_gate"].T, RANK, axis=0),
        "kernel": i["L0_ffn_kernel"],
        "lora_A": i["L0_ffn_lora_A"].reshape(LORAS * RANK, D),
        "lora_B": i["L0_ffn_lora_B"].transpose(0, 2, 1).reshape(LORAS * RANK, D),
        "A_shared": i["L0_ffn_lora_A_shared"].T,
        "B_shared": np.concatenate([i["L0_ffn_lora_B_shared"].T, i["L0_ffn_bias"][None, :]]),
        "wq": i["L1_xattn_wq"], "wk": i["L1_xattn_wk"], "wv": i["L1_xattn_wv"], "wo": i["L1_xattn_wo"],
        "router_A": np.concatenate([i["L1_ffn_A"].reshape(MID, D), i["L1_ffn_router_w"]]).T,
        "B": i["L1_ffn_B"].transpose(0, 2, 1).reshape(MID, D),
        **constants(),
    }
    nc = bacc.Bacc("TRN2", target_bir_lowering=False, num_devices=1)
    feed, a = {}, {}
    for name, array in arrays.items():
        feed[f"in_{name}"] = np.ascontiguousarray(array)
        a[name] = nc.dram_tensor(f"in_{name}", array.shape, F32, kind="ExternalInput").ap()
    out = nc.dram_tensor("out_x", (rows, D), F32, kind="ExternalOutput").ap()
    flamingo_gated(nc, a, out)
    result = run_bass_kernel_spmd(nc, [feed], core_ids=[0])
    return result.results[0]["out_x"].reshape(BATCH, SEQ, D)
```

```python
from contextlib import ExitStack

import numpy as np

import concourse.bass as bass
from concourse import mybir

F32 = mybir.dt.float32
F32R = mybir.dt.float32r
ALU = mybir.AluOpType
ACT = mybir.ActivationFunctionType
AX_X = mybir.AxisListType.X

P = 128
BATCH, SEQ, D = 16, 64, 512
PAIRS = BATCH * SEQ // P
KT = D // P
EPS = 1e-5

WIN, PAD, HD0 = 16, 8, 8
ROWS0 = P // HD0
PADDED = PAD + D + WIN - PAD - 1

LORAS, RANK = 16, 32
LORA_CHUNKS = LORAS * RANK // P
INNER = 2 * RANK + 1
HALF = P // RANK

GROUPS, GH, DK = 8, 4, 128
MASKED = -1e9
HUGE = 3e38

EXPERTS, ERANK = 4, 16
MID = EXPERTS * ERANK
LORA_SCALE = 4.0

ds = bass.ds


def after(eng, sem, value):
    if not isinstance(value, int) or value > 0:
        eng.wait_ge(sem, value)


def three_passes(pe, out, weights, moving, k_steps, part=None):
    last = None
    for k in part or range(k_steps):
        wh, wl = weights(k)
        mh, ml = moving(k)
        for n, (w, m) in enumerate(((wl, mh), (wh, ml), (wh, mh))):
            last = pe.matmul(out, w, m, start=(k == 0 and n == 0), stop=(k == k_steps - 1 and n == 2))
    return last


class Pool:

    def __init__(self, nc, ctx, stage):
        self.nc, self.ctx, self.stage = nc, ctx, stage

    def sb(self, name, shape, dt=F32):
        return self.ctx.enter_context(self.nc.sbuf_tensor(f"{self.stage}_{name}", shape, dt))

    def ps(self, name, shape):
        return self.ctx.enter_context(self.nc.psum_tensor(f"{self.stage}_{name}", shape, F32))

    def sem(self, name):
        return self.ctx.enter_context(self.nc.semaphore(f"{self.stage}_{name}"))


class RowNorm:

    STEPS = 5

    def __init__(self, al, name):
        self.stats, self.moments = al.sb(f"{name}_stats", [P, 6]), al.sb(f"{name}_moments", [P, 2])
        self.rstd, self.power, self.spare = (al.sb(f"{name}_{n}", [P, w]) for n, w in
                                             (("rstd", 1), ("power", 1), ("spare", 2)))
        self.steps, self.rooted, self.applied = (al.sem(f"{name}_{n}") for n in ("steps", "rooted", "applied"))

    def moments_of(self, dve, src, turn):
        base = self.STEPS * turn
        after(dve, self.applied, turn)
        dve.memset(self.spare[:, 0:1], 0.0).then_inc(self.steps, 1)
        dve.bn_stats(self.stats[:], src).then_inc(self.steps, 1)
        dve.wait_ge(self.steps, base + 2)
        dve.memset(self.spare[:, 1:2], 0.0).then_inc(self.steps, 1)
        dve.bn_aggr(self.moments[:], self.stats[:]).then_inc(self.steps, 1)
        dve.wait_ge(self.steps, base + 4)
        dve.tensor_scalar(self.moments[:, 1:2], self.moments[:, 1:2], EPS, None, ALU.add).then_inc(self.steps, 1)

    def start(self, pool):
        pool.memset(self.power[:], -0.5).then_inc(self.rooted, 1)
        pool.wait_ge(self.rooted, 1)

    def root(self, pool, turn):
        pool.wait_ge(self.steps, self.STEPS * turn + 5)
        pool.tensor_tensor(self.rstd[:], self.moments[:, 1:2], self.power[:], ALU.pow).then_inc(self.rooted, 1)

    def apply(self, dve, out, src, turn):
        dve.wait_ge(self.rooted, turn + 2)
        dve.tensor_scalar(out, src, self.moments[:, 0:1], self.rstd[:], ALU.subtract, ALU.mult)\
           .then_inc(self.applied, 1)


def tile_of(x, t):
    return x[:, ds(t, 1), :].rearrange("p o d -> p (o d)")


def layer_0_attention(nc, a, x_all, ident, gates, k_dram, v_dram, ffn):
    with ExitStack() as ctx:
        al = Pool(nc, ctx, "a")
        ctx_t = al.sb("ctx_t", [P, 2, D])
        big = ffn.lora[:].rearrange("p (k h) n -> p k (h n)", k=KT)
        ctxTh = al.sb("ctxTh", [P, KT, PAIRS * P], F32R)
        ctxTl = al.sb("ctxTl", [P, KT, PAIRS * P], F32R)
        wvh = al.sb("wvh", [P, KT, GROUPS * DK], F32R)
        wvl = al.sb("wvl", [P, KT, GROUPS * DK], F32R)
        w_diag = al.sb("w_diag", [P, 4, P])
        bias = al.sb("bias", [P, 4])
        pick = al.sb("pick", [P, 15 * ROWS0])
        cosk, sink = al.sb("cosk", [P, SEQ]), al.sb("sink", [P, SEQ])
        gbo = al.sb("gbo", [P, 1])
        xn = al.sb("xn", [P, D])
        norm = RowNorm(al, "norm")
        kpad, vpad = al.sb("kpad", [P, PADDED]), al.sb("vpad", [P, PADDED])
        DEPTH = 6
        prod = al.sb("prod", [P, DEPTH, D])
        halved = [5, 9, 12]
        score_order = [0, 1, 2, 3, 4, 6, 7, 5, 8, 10, 11, 9, 13, 14, 12, 15]
        EARLY = 2
        prodh, prodl = al.sb("prodh", [P, 2, D], F32R), al.sb("prodl", [P, 2, D], F32R)
        pick_r = al.sb("pick_r", [P, 15 * ROWS0], F32R)
        sT = al.sb("sT", [P, 2, D])
        probs = al.sb("probs", [P, 4, WIN, ROWS0])
        smax, ssum, srec = (al.sb(n, [P, 4, ROWS0]) for n in ("smax", "ssum", "srec"))
        rep = al.sb("rep", [P, 4, 4, P])
        ev = al.sb("ev", [P, 4, D])
        evs = al.sb("evs", [P, 4, D])
        evq = al.sb("evq", [P, 2, D])
        otmp = al.sb("otmp", [P, D])
        land = al.sb("land", [P, KT, DK])
        wh, wl = al.sb("wh", [P, KT, DK], F32R), al.sb("wl", [P, KT, DK], F32R)
        tokh, tokl = al.sb("tokh", [P, KT, P], F32R), al.sb("tokl", [P, KT, P], F32R)
        ksw, krot = al.sb("ksw", [P, 2, D]), al.sb("krot", [P, 2, D])
        vrow = al.sb("vrow", [P, 2, D])

        q_ps, k_ps = al.ps("q_ps", [P, D]), al.ps("k_ps", [P, D])
        s_ps = al.ps("s_ps", [P, 2, D])
        e_ps = [s_ps[:, 0], s_ps[:, 1]] + [al.ps(f"e_ps{i}", [P, D])[:] for i in range(2)]
        kv_ps = [al.ps("kv_ps0", [P, D]), al.ps("kv_ps1", [P, D])]
        eff_ps = [bank[:, 0:PAIRS * RANK] for bank in kv_ps]
        po = k_ps

        s = {n: al.sem(n) for n in (
            "x0_in", "x1_in", "x_in", "ctx_in", "small_in", "wk_in", "zeroed", "tab_in", "gate",
            "ctx_hi", "ctx_lo_a", "ctx_lo_b", "wv_hi", "wv_lo",
            "l0q", "l0k", "l0v", "k_ev", "v_ev", "prod", "score", "sT_ev", "sc", "mx", "sub", "expd",
            "ssum", "srec", "norm", "rep", "e", "ev", "pair", "quad", "pick_in", "pick_r",
            "prod_hi", "prod_lo", "osum", "o_ev", "x_add",
            "whi", "wlo", "tok", "k0", "k1", "v0", "v1", "ksw", "kcos", "kt2", "kready", "v0_ev", "v1_ev",
            "k_st", "v_st")}
        ctxT_in = [al.sem(f"ctxT_in{k}") for k in range(KT)]
        wv_in = [al.sem(f"wv_in{k}") for k in range(KT)]
        SMALL = 16 * 4
        TABLES = 16 * 4
        QUADS = WIN // 4

        def ctx_low(eng, chunks, done):
            for k in chunks:
                eng.wait_ge(s["ctx_hi"], k + 1)
                eng.tensor_tensor(ctxTl[:, k], big[:, k], ctxTh[:, k].bitcast(F32), ALU.subtract).then_inc(done, 1)

        wk_view = a["wk"].rearrange("(k p) n -> p k n", p=P)
        x_view = a["x"].rearrange("(t p) d -> p t d", p=P)
        ctx_view = a["ctx"].rearrange("(t p) d -> p t d", p=P)
        block = ctx.enter_context(nc.Block())

        @block.sync
        def _(sp):
            def load_wk(g):
                after(sp, s["wlo"], g)
                sp.dma_start(land[:], wk_view[:, :, ds(g * DK, DK)]).then_inc(s["wk_in"], 16)

            def load_ctx(p):
                if not isinstance(p, int) or p >= 2:
                    sp.wait_ge(s["l0v"], p - 1)
                    sp.wait_ge(s["ctx_in"], 16 * p)
                sp.dma_start(tile_of(ctx_t, p % 2), ctx_view[:, ds(p, 1), :].rearrange("p o d -> p (o d)"))\
                  .then_inc(s["ctx_in"], 16)

            def store(g):
                sp.wait_ge(s["kready"], 2 * g + 2)
                sp.dma_start(k_dram[ds(g, 1)].rearrange("o p n -> p (o n)"),
                             krot[:].rearrange("p h n -> p (h n)")).then_inc(s["k_st"], 16)
                sp.wait_ge(s["v1_ev"], g + 1)
                sp.dma_start(v_dram[:, :, ds(g, 1), :].rearrange("g p o n -> p g (o n)"),
                             vrow[:].rearrange("p h n -> p (h n)").rearrange("p (g n) -> p g n", n=DK))\
                  .then_inc(s["v_st"], 16)

            sp.dma_start(x_all[:, 0], x_view[:, 0]).then_inc(s["x0_in"], 16)
            load_ctx(0)
            load_wk(0)
            for k in range(KT):
                sp.dma_start(big[:, k], a["ctxT"][k * P:k * P + P, :]).then_inc(ctxT_in[k], 16)
            sp.dma_start(x_all[:, 1], x_view[:, 1]).then_inc(s["x1_in"], 16)
            for k in range(KT):
                sp.wait_ge(s["ctx_lo_a" if k < KT // 2 else "ctx_lo_b"], k % (KT // 2) + 1)
                sp.dma_start(big[:, k], a["wv"][k * P:k * P + P, :]).then_inc(wv_in[k], 16)
            sp.dma_start(x_all[:, 2:], x_view[:, 2:]).then_inc(s["x_in"], 16)
            sp.wait_ge(s["ctx_in"], 16)
            load_ctx(1)
            load_wk(1)
            sp.wait_ge(s["wv_lo"], KT)
            ffn.load(sp, a)
            store(0)
            with sp.Fori(1, GROUPS - 1) as g:
                load_ctx(g + 1)
                load_wk(g + 1)
                store(g)
            store(GROUPS - 1)
            sp.wait_ge(s["k_st"], 16 * GROUPS)
            sp.wait_ge(s["v_st"], 16 * GROUPS)

        @block.scalar
        def _(act):
            act.wait_ge(s["zeroed"], 1)
            for h in (0, 64):
                act.dma_start(w_diag[h:h + 64, :, h:h + 64], a["W4"].rearrange("c (n o) -> c n o", n=4))\
                   .then_inc(s["small_in"], 16)
                act.dma_start(bias[h:h + 64, :], a["b4"]).then_inc(s["small_in"], 16)
            act.dma_start(pick[:], a["pick"]).then_inc(s["pick_in"], 16)
            for tensor, view in ((ident[:], a["ident"]), (cosk[:], a["cosk"]), (sink[:], a["sink"]),
                                 (gates[:], a["g4"].partition_broadcast(P))):
                act.dma_start(tensor, view).then_inc(s["tab_in"], 16)

            def split_wk(g):
                act.wait_ge(s["wk_in"], 16 * g + 16)
                after(act, s["k1"], g)
                act.activation(wh[:], land[:], ACT.Copy).then_inc(s["whi"], 1)

            def take_tile(p):
                after(act, s["v1"], p)
                cols = ds(p * P, P)
                act.activation(tokh[:], ctxTh[:, :, cols].bitcast(F32), ACT.Copy)
                act.activation(tokl[:], ctxTl[:, :, cols].bitcast(F32), ACT.Copy).then_inc(s["tok"], 1)

            def k_evacuate(p):
                act.wait_ge(s["l0k"], p + 1)
                after(act, s["prod"], WIN * p)
                act.activation(kpad[:, PAD:PAD + D], k_ps[:], ACT.Identity, bias=bias[:, 1:2]).then_inc(s["k_ev"], 1)

            def out_evacuate(p):
                act.wait_ge(s["osum"], QUADS * p + QUADS)
                after(act, s["x_add"], p)
                act.activation(otmp[:], po[:], ACT.Identity, bias=gbo[:], scale=gates[:, 0:1]).then_inc(s["o_ev"], 1)

            def swap_k(p, h):
                act.wait_ge(s["kcos"], 2 * p + h + 1)
                after(act, s["kready"], 2 * p)
                act.activation(ksw[0:64, h], kv_ps[1 - h][64:128, :], ACT.Copy).then_inc(s["ksw"], 1)
                act.activation(ksw[64:128, h], kv_ps[1 - h][0:64, :], ACT.Copy).then_inc(s["ksw"], 1)

            def v_evacuate(p):
                act.wait_ge(s["l0v"], p + 1)
                after(act, s["ev"], WIN * p)
                act.activation(vpad[:, PAD:PAD + D], kv_ps[0][:], ACT.Identity, bias=bias[:, 2:3])\
                   .then_inc(s["v_ev"], 1)

            def high_part(p, i):
                act.wait_ge(s["prod"], WIN * p + halved[i] + 1)
                after(act, s["score"], WIN * p + (score_order.index(halved[i - 2]) + 1 if i >= 2 else 0))
                act.activation(prodh[:, i % 2], prod[:, halved[i] % DEPTH], ACT.Copy).then_inc(s["prod_hi"], 1)

            def body(p, more=True, before=True):
                if before:
                    split_wk(p)
                    v_evacuate(p)
                for i in range(EARLY if before else 0):
                    high_part(p, i)
                for h in range(2):
                    if h == 1 and before:
                        for i in range(EARLY, len(halved)):
                            high_part(p, i)
                    act.wait_ge(s["score"], WIN * p + 8 * h + 8)
                    after(act, s["sc"], p)
                    act.activation(sT[:, h], s_ps[:, h], ACT.Copy).then_inc(s["sT_ev"], 1)
                    if h == 0:
                        swap_k(p, 0)
                if before:
                    out_evacuate(p - 1)
                act.wait_ge(s["sub"], p + 1)
                act.activation(probs[:], probs[:], ACT.Exp, scale=float(HD0) ** -0.5).then_inc(s["expd"], 1)
                swap_k(p, 1)
                act.wait_ge(s["v0"], p + 1)
                after(act, s["v_st"], 16 * p)
                act.activation(vrow[:, 0], kv_ps[1][:], ACT.Copy).then_inc(s["v0_ev"], 1)
                act.wait_ge(s["norm"], p + 1)
                for w in range(WIN):
                    after(act, s["e"], WIN * p + max(w - 3, 0))
                    act.activation(rep[:, w % 4].rearrange("p t (h c) -> p t h c", c=HD0),
                                   probs[:, :, w, :].rearrange("p t (h o) -> p t h o", o=1)
                                   .broadcast_to([P, 4, ROWS0, HD0]), ACT.Copy).then_inc(s["rep"], 1)
                    if w == 2 and more:
                        k_evacuate(p + 1)
                    if w == 11:
                        act.wait_ge(s["v1"], p + 1)
                        act.activation(vrow[:, 1], kv_ps[0][:], ACT.Copy).then_inc(s["v1_ev"], 1)
                    if w == 13 and more:
                        take_tile(p + 1)

            act.wait_ge(s["small_in"], SMALL)
            for k in range(KT):
                act.wait_ge(ctxT_in[k], 16)
                act.activation(ctxTh[:, k], big[:, k], ACT.Copy).then_inc(s["ctx_hi"], 1)
                if k == 1:
                    act.wait_ge(s["zeroed"], 3)
                    k_evacuate(0)
            act.wait_ge(s["pick_in"], 16)
            act.activation(pick_r[:], pick[:], ACT.Copy).then_inc(s["pick_r"], 1)
            split_wk(0)
            act.wait_ge(s["ctx_lo_a"], KT // 2)
            act.wait_ge(s["ctx_lo_b"], KT // 2)
            take_tile(0)
            act.wait_ge(s["tab_in"], TABLES)
            act.activation(gates[:], gates[:], ACT.Tanh).then_inc(s["gate"], 1)
            act.wait_ge(s["gate"], 1)
            act.activation(gbo[:], bias[:, 3:4], ACT.Copy, scale=gates[:, 0:1]).then_inc(s["gate"], 1)
            act.wait_ge(s["gate"], 2)
            v_evacuate(0)
            for k in range(KT):
                act.wait_ge(wv_in[k], 16)
                act.activation(wvh[:, k], big[:, k], ACT.Copy).then_inc(s["wv_hi"], 1)
            body(0, before=False)
            with act.Fori(1, PAIRS - 1) as p:
                body(p)
            body(PAIRS - 1, more=False)
            ffn.keep_a(act, eff_ps[0], 0)
            ffn.keep_a(act, eff_ps[1], 1)
            out_evacuate(PAIRS - 1)
            ffn.keep_a(act, eff_ps[0], 2)
            ffn.keep_a(act, eff_ps[1], 3)

        @block.gpsimd
        def _(pool):
            pool.memset(w_diag[:], 0.0).then_inc(s["zeroed"], 1)
            pool.memset(kpad[:], 0.0).then_inc(s["zeroed"], 1)
            pool.memset(vpad[:], 0.0).then_inc(s["zeroed"], 1)
            norm.start(pool)
            norm.root(pool, 0)

            def split_wk(g):
                pool.wait_ge(s["whi"], g + 1)
                after(pool, s["k1"], g)
                pool.tensor_tensor(wl[:], land[:], wh[:].bitcast(F32), ALU.subtract).then_inc(s["wlo"], 1)

            def rotate_k(p, h):
                if isinstance(p, int) and p == 0 and h == 0:
                    pool.wait_ge(s["tab_in"], TABLES)
                pool.wait_ge(s["ksw"], 4 * p + 2 * h + 2)
                kv = ksw[:, h].rearrange("p (b q) -> p b q", q=SEQ)
                pool.tensor_tensor(kv, kv, sink[:].rearrange("p (o q) -> p o q", o=1)
                                   .broadcast_to([P, D // SEQ, SEQ]), ALU.mult).then_inc(s["kt2"], 1)
                pool.wait_ge(s["kt2"], 2 * p + h + 1)
                pool.wait_ge(s["kcos"], 2 * p + h + 1)
                pool.tensor_tensor(krot[:, h], krot[:, h], ksw[:, h], ALU.add).then_inc(s["kready"], 1)

            def x_update(p):
                pool.wait_ge(s["o_ev"], p + 1)
                xp = tile_of(x_all, p)
                pool.tensor_tensor(xp, xp, otmp[:], ALU.add).then_inc(s["x_add"], 1)

            def sum_two(p, j):
                pool.wait_ge(s["ev"], WIN * p + 2 * j + 2)
                after(pool, s["quad"], QUADS * p + max(j // 2 - 1, 0))
                pool.tensor_tensor(evs[:, j % 4], ev[:, 2 * j % 4], ev[:, (2 * j + 1) % 4], ALU.add)\
                    .then_inc(s["pair"], 1)

            def low_part(p, i):
                pool.wait_ge(s["prod_hi"], len(halved) * (p - 1) + i + 1)
                pool.tensor_tensor(prodl[:, i % 2], prod[:, halved[i] % DEPTH],
                                   prodh[:, i % 2].bitcast(F32), ALU.subtract)\
                    .then_inc(s["prod_lo"], 1)

            def body(p, more=True, before=True):
                if before:
                    split_wk(p)
                    sum_two(p - 1, WIN // 2 - 1)
                    for i in range(EARLY):
                        low_part(p, i)
                    if more:
                        norm.root(pool, p + 1)
                    for i in range(EARLY, len(halved)):
                        low_part(p, i)
                rotate_k(p, 0)
                if before:
                    x_update(p - 1)
                rotate_k(p, 1)
                for j in range(WIN // 2 - 1 if more else WIN // 2):
                    sum_two(p, j)

            ctx_low(pool, range(KT // 2, KT), s["ctx_lo_b"])
            split_wk(0)
            norm.root(pool, 1)
            for k in range(KT):
                pool.wait_ge(s["wv_hi"], k + 1)
                pool.tensor_tensor(wvl[:, k], big[:, k], wvh[:, k].bitcast(F32), ALU.subtract).then_inc(s["wv_lo"], 1)
            body(0, before=False)
            with pool.Fori(1, PAIRS - 1) as p:
                body(p)
            body(PAIRS - 1, more=False)
            x_update(PAIRS - 1)

        @block.vector
        def _(dve):
            def k_cos(p, h):
                dve.wait_ge(s[f"k{h}"], p + 1)
                after(dve, s["k_st"], 16 * p)
                dve.tensor_tensor(krot[:, h].rearrange("p (b q) -> p b q", q=SEQ),
                                  kv_ps[1 - h][:].rearrange("p (b q) -> p b q", q=SEQ),
                                  cosk[:].rearrange("p (o q) -> p o q", o=1).broadcast_to([P, D // SEQ, SEQ]),
                                  ALU.mult).then_inc(s["kcos"], 1)

            def weigh_v(p, w):
                dve.wait_ge(s["e"], WIN * p + w + 1)
                if w % 2 == 0:
                    after(dve, s["pair"], 8 * p + max(w // 2 - 1, 0))
                dve.tensor_tensor(ev[:, w % 4], e_ps[w % 4], vpad[:, w:w + D], ALU.mult).then_inc(s["ev"], 1)

            def sum_four(p, m):
                dve.wait_ge(s["pair"], 8 * p + 2 * m + 2)
                after(dve, s["osum"], QUADS * p + max(m - 1, 0))
                dve.tensor_tensor(evq[:, m % 2], evs[:, 2 * m % 4], evs[:, (2 * m + 1) % 4], ALU.add)\
                   .then_inc(s["quad"], 1)

            def body(p, more=True, before=True):
                dve.wait_ge(s["l0q"], p + 1)
                dve.wait_ge(s["k_ev"], p + 1)
                for w in range(WIN):
                    if w - DEPTH in halved and before:
                        dve.wait_ge(s["prod_lo"], len(halved) * (p - 1) + halved.index(w - DEPTH) + 1)
                    elif w >= DEPTH:
                        dve.wait_ge(s["score"], WIN * p + 1 + (score_order.index(w - DEPTH) if before else w - DEPTH))
                    else:
                        after(dve, s["score"], WIN * p)
                    dve.scalar_tensor_tensor(prod[:, w % DEPTH], q_ps[:], bias[:, 0:1], kpad[:, w:w + D],
                                             ALU.add, ALU.mult).then_inc(s["prod"], 1)
                    if w in (1, 3) and before:
                        weigh_v(p - 1, WIN - 2 + w // 2)
                    if w == 6 and before:
                        sum_four(p - 1, QUADS - 1)
                    if w == 4 and not more:
                        ffn.mix_gates(dve)
                    if w == 8 and more:
                        norm.moments_of(dve, tile_of(x_all, p + 1), p + 1)
                    if w == 12 and more:
                        norm.apply(dve, xn[:], tile_of(x_all, p + 1), p + 1)
                    if w == 10:
                        if not before:
                            dve.wait_ge(s["tab_in"], TABLES)
                        k_cos(p, 0)
                scores = s_ps[:].rearrange("p h n -> p (h n)").rearrange("p (t w r) -> p t w r", t=4, w=WIN)
                dve.wait_ge(s["sc"], p + 1)
                dve.tensor_reduce(smax[:], scores.rearrange("p t w r -> p t r w"), AX_X, ALU.max).then_inc(s["mx"], 1)
                dve.wait_ge(s["mx"], p + 1)
                after(dve, s["rep"], WIN * p)

                def by_row(stat):
                    return stat[:].rearrange("p t (o r) -> p t o r", o=1).broadcast_to([P, 4, WIN, ROWS0])

                dve.tensor_tensor(probs[:], scores, by_row(smax), ALU.subtract).then_inc(s["sub"], 1)
                k_cos(p, 1)
                dve.wait_ge(s["expd"], p + 1)
                dve.tensor_reduce(ssum[:], probs[:].rearrange("p t w r -> p t r w"), AX_X, ALU.add)\
                   .then_inc(s["ssum"], 1)
                dve.wait_ge(s["ssum"], p + 1)
                dve.reciprocal(srec[:], ssum[:]).then_inc(s["srec"], 1)
                dve.wait_ge(s["srec"], p + 1)
                dve.tensor_tensor(probs[:], probs[:], by_row(srec), ALU.mult).then_inc(s["norm"], 1)
                dve.wait_ge(s["v_ev"], p + 1)
                for w in range(WIN - 2 if more else WIN):
                    weigh_v(p, w)
                    if w in (6, 10, 13):
                        sum_four(p, (w - 5) // 4)

            dve.wait_ge(s["x0_in"], 16)
            norm.moments_of(dve, x_all[:, 0], 0)
            norm.apply(dve, xn[:], x_all[:, 0], 0)
            ctx_low(dve, range(KT // 2), s["ctx_lo_a"])
            dve.wait_ge(s["small_in"], SMALL)
            dve.wait_ge(s["x1_in"], 16)
            body(0, before=False)
            dve.wait_ge(s["x_in"], 16)
            with dve.Fori(1, PAIRS - 1) as p:
                body(p)
            body(PAIRS - 1, more=False)
            sum_four(PAIRS - 1, QUADS - 1)

        @block.tensor
        def _(pe):
            def k_proj(h):
                return three_passes(pe, kv_ps[1 - h][:], lambda k: (wh[:, k], wl[:, k]),
                                    lambda k: (ctxTh[:, k, h * D:h * D + D], ctxTl[:, k, h * D:h * D + D]), KT)

            def v_proj(h, part=None):
                return three_passes(pe, kv_ps[1 - h][:], lambda k: (tokh[:, k], tokl[:, k]),
                                    lambda k: (wvh[:, k, h * D:h * D + D], wvl[:, k, h * D:h * D + D]), KT, part)

            def q_and_k(p):
                pe.wait_ge(norm.applied, p + 1)
                pe.matmul(q_ps[:], w_diag[:, 0], xn[:], start=True, stop=True).then_inc(s["l0q"], 1)
                pe.wait_ge(s["ctx_in"], 16 * p + 16)
                if not isinstance(p, int) or p >= 2:
                    pe.wait_ge(s["o_ev"], p - 1)
                pe.matmul(k_ps[:], w_diag[:, 1], tile_of(ctx_t, p % 2), start=True, stop=True).then_inc(s["l0k"], 1)

            def out_sum(p, j):
                pe.wait_ge(s["quad"], QUADS * p + j + 1)
                pe.matmul(po[:], w_diag[:, 3], evq[:, j % 2], start=(j == 0), stop=(j == QUADS - 1))\
                    .then_inc(s["osum"], 1)

            def body(p, more=True, before=True):
                after(pe, s["v1_ev"], p)
                pe.matmul(kv_ps[0][:], w_diag[:, 2], tile_of(ctx_t, p % 2), start=True, stop=True)\
                   .then_inc(s["l0v"], 1)
                if before:
                    pe.wait_ge(s["ev"], WIN * p - 2)
                    out_sum(p - 1, 2)
                for n, w in enumerate(score_order if before else range(WIN)):
                    c = (7 - w % 8) * ROWS0
                    start, stop = n % 8 == 0, n % 8 == 7
                    if w in halved and before:
                        i = halved.index(w)
                        pe.wait_ge(s["prod_lo"], len(halved) * (p - 1) + i + 1)
                        pe.matmul(s_ps[:, w // 8], pick_r[:, c:c + P], prodl[:, i % 2], start=start, stop=False)
                        last = pe.matmul(s_ps[:, w // 8], pick_r[:, c:c + P], prodh[:, i % 2], start=False, stop=stop)
                    else:
                        pe.wait_ge(s["prod"], WIN * p + w + 1)
                        last = pe.matmul(s_ps[:, w // 8], pick[:, c:c + P], prod[:, w % DEPTH], start=start, stop=stop)
                    last.then_inc(s["score"], 1)
                    if n == (3 if before else 6):
                        pe.wait_ge(s["wlo"], p + 1)
                        after(pe, s["v0_ev"], p)
                        if not before:
                            pe.wait_ge(s["ctx_lo_a"], KT // 2)
                            pe.wait_ge(s["ctx_lo_b"], KT // 2)
                        k_proj(0).then_inc(s["k0"], 1)
                if before:
                    out_sum(p - 1, QUADS - 1)
                else:
                    pe.wait_ge(s["tab_in"], TABLES)
                pe.wait_ge(s["sT_ev"], 2 * p + 2)
                for t in range(4):
                    for h in range(2):
                        c = (2 * (t % 2) + h) * P
                        last = pe.transpose(s_ps[:, t // 2, c:c + P], sT[:, h, t * P:t * P + P], ident[:])
                last.then_inc(s["sc"], 1)
                pe.wait_ge(s["v_ev"], p + 1)
                k_proj(1).then_inc(s["k1"], 1)
                pe.wait_ge(s["ksw"], 4 * p + 2)
                pe.wait_ge(s["kcos"], 2 * p + 1)
                pe.wait_ge(s["tok"], p + 1)
                if isinstance(p, int) and p == 0:
                    pe.wait_ge(s["wv_lo"], KT)
                v_proj(0).then_inc(s["v0"], 1)
                if more:
                    q_and_k(p + 1)
                pe.wait_ge(s["ksw"], 4 * p + 4)
                pe.wait_ge(s["kcos"], 2 * p + 2)
                v_proj(1, [0])
                for w in range(WIN):
                    pe.wait_ge(s["rep"], WIN * p + w + 1)
                    after(pe, s["ev"], WIN * p + max(w - 3, 0))
                    for t in range(4):
                        last = pe.transpose(e_ps[w % 4][:, t * P:t * P + P], rep[:, w % 4, t], ident[:])
                    last.then_inc(s["e"], 1)
                    if w in (2, 5, 8):
                        k = (w + 1) // 3
                        last = v_proj(1, [k])
                        if k == KT - 1:
                            last.then_inc(s["v1"], 1)
                    if w == 10:
                        if more:
                            pe.wait_ge(s["k_ev"], p + 2)
                        elif before:
                            pe.wait_ge(s["o_ev"], p)
                        out_sum(p, 0)
                    if w == 13:
                        out_sum(p, 1)

            pe.wait_ge(s["small_in"], SMALL)
            q_and_k(0)
            pe.wait_ge(s["pick_in"], 16)
            body(0, before=False)
            pe.wait_ge(s["pick_r"], 1)
            with pe.Fori(1, PAIRS - 1) as p:
                body(p)
            body(PAIRS - 1, more=False)
            pe.wait_ge(s["v1_ev"], PAIRS)
            ffn.effective_a(pe, eff_ps[0], 0)
            out_sum(PAIRS - 1, 2)
            ffn.effective_a(pe, eff_ps[1], 1)
            out_sum(PAIRS - 1, QUADS - 1)
            ffn.effective_a(pe, eff_ps[0], 2)
            ffn.effective_a(pe, eff_ps[1], 3)


class FfnInputs:

    LOADS = 5

    def __init__(self, al):
        self.lora = al.sb("lora", [P, 2 * LORA_CHUNKS, D])
        self.lora_a, self.lora_b = self.lora[:, 0:LORA_CHUNKS], self.lora[:, LORA_CHUNKS:]
        self.a_all = al.sb("a_all", [P, KT, PAIRS, 2 * RANK])
        self.gcol = al.sb("gcol", [P, LORA_CHUNKS, PAIRS])
        self.eye_r = al.sb("eye_r", [P, RANK])
        self.a_shared = al.sb("a_shared", [P, KT, RANK])
        self.mix = al.sb("mix", [P, LORA_CHUNKS, PAIRS, RANK])
        self.loaded, self.mixed, self.a, self.a_ev = (al.sem(n) for n in ("loaded", "mixed", "a", "a_ev"))

    def mix_gates(self, dve):
        dve.wait_ge(self.loaded, 16 * self.LOADS)
        for c in range(LORA_CHUNKS):
            dve.tensor_tensor(self.mix[:, c], self.gcol[:, c].rearrange("p (b o) -> p b o", o=1)
                              .broadcast_to([P, PAIRS, RANK]),
                              self.eye_r[:].rearrange("p (o r) -> p o r", o=1).broadcast_to([P, PAIRS, RANK]),
                              ALU.mult).then_inc(self.mixed, 1)

    def effective_a(self, pe, bank, k):
        if k == 0:
            pe.wait_ge(self.mixed, LORA_CHUNKS)
        after(pe, self.a_ev, max(k - 1, 0))
        for c in range(LORA_CHUNKS):
            last = pe.matmul(bank, self.lora_a[:, c, k * P:k * P + P], self.mix[:, c].rearrange("p b r -> p (b r)"),
                             start=(c == 0), stop=(c == LORA_CHUNKS - 1))
        last.then_inc(self.a, 1)

    def keep_a(self, act, bank, k):
        act.wait_ge(self.a, k + 1)
        act.activation(self.a_all[:, k, :, 0:RANK], bank.rearrange("p (b r) -> p b r", r=RANK), ACT.Copy)\
           .then_inc(self.a_ev, 1)

    def load(self, sp, a):
        for tensor, view in ((self.gcol[:], a["gate"].rearrange("(c p) b -> p c b", p=P)),
                             (self.eye_r[:], a["eye_r"]),
                             (self.lora_a, a["lora_A"].rearrange("(c p) i -> p c i", p=P)),
                             (self.lora_b, a["lora_B"].rearrange("(c p) o -> p c o", p=P)),
                             (self.a_shared[:], a["A_shared"].rearrange("(k p) r -> p k r", p=P))):
            sp.dma_start(tensor, view).then_inc(self.loaded, 16)


def layer_0_ffn(nc, a, x_all, ident, gates, xTh, xTl, ffn, att):
    with ExitStack() as ctx:
        al = Pool(nc, ctx, "f")
        lora_b, mix = ffn.lora_b, ffn.mix
        kern = al.sb("kern", [P, KT, D])
        a_all = ffn.a_all
        b_all = al.sb("b_all", [INNER, PAIRS, D])
        xn, xn2 = al.sb("xn", [P, D]), al.sb("xn2", [P, D])
        norm1, norm2 = RowNorm(al, "norm1"), RowNorm(al, "norm2")
        xnT = al.sb("xnT", [P, KT, P])
        ax = al.sb("ax", [P, 2 * RANK])
        axT = al.sb("axT", [INNER, P])

        t1_ps = al.ps("t1_ps", [P, KT, P])
        ax_ps = al.ps("ax_ps", [P, 2 * RANK])
        axT_ps = al.ps("axT_ps", [2 * RANK, P])
        out_ps = al.ps("out_ps", [P, 2, D])
        t2_ps = al.ps("t2_ps", [P, KT, P])
        s = {n: al.sem(n) for n in (
            "eff", "eff_ev", "shared", "b_in", "kern_in", "t1", "t1_ev", "ax", "ax_ev", "axT", "axT_ev", "base", "out",
            "x2", "t2", "hi", "lo", "ones")}
        block = ctx.enter_context(nc.Block())

        @block.sync
        def _(sp):
            sp.dma_start(kern[:], a["kernel"].rearrange("(k p) o -> p k o", p=P)).then_inc(s["kern_in"], 16)
            sp.dma_start(b_all[RANK:INNER], a["B_shared"].rearrange("r (o n) -> r o n", o=1)
                         .broadcast_to([RANK + 1, PAIRS, D])).then_inc(s["b_in"], 16)
            att.load_first(sp, a)

        @block.gpsimd
        def _(pool):
            pool.memset(axT[2 * RANK:INNER, :], 1.0).then_inc(s["ones"], 1)
            pool.wait_ge(s["ones"], 1)
            norm1.start(pool)
            norm2.start(pool)
            norm1.root(pool, 0)
            norm1.root(pool, 1)
            for k in range(KT):
                pool.tensor_copy(a_all[:, k, :, RANK:], ffn.a_shared[:, k].rearrange("p (o r) -> p o r", o=1)
                                 .broadcast_to([P, PAIRS, RANK])).then_inc(s["shared"], 1)

            def tile(p, more=True):
                norm2.root(pool, p)
                if more:
                    norm1.root(pool, p + 2)

            for p in range(KT):
                tile(p)
                att.wq_low(pool, 0, [p])
            with pool.Fori(KT, PAIRS - 2) as p:
                tile(p)
            tile(PAIRS - 2, False)
            tile(PAIRS - 1, False)

        @block.scalar
        def _(act):

            def transposed(p):
                act.wait_ge(s["t1"], p + 1)
                after(act, s["base"], p)
                act.activation(xnT[:], t1_ps[:], ACT.Copy).then_inc(s["t1_ev"], 1)

            def middle(p):
                act.wait_ge(s["ax"], p + 1)
                after(act, s["axT"], p)
                act.activation(ax[:], ax_ps[:], ACT.Copy).then_inc(s["ax_ev"], 1)
                act.wait_ge(s["axT"], p + 1)
                after(act, s["out"], p)
                act.activation(axT[0:2 * RANK, :], axT_ps[:], ACT.Copy).then_inc(s["axT_ev"], 1)

            def high(p):
                act.wait_ge(s["t2"], p + 1)
                act.activation(xTh[:, :, ds(p * P, P)], t2_ps[:], ACT.Copy).then_inc(s["hi"], 1)

            for h in range(2):
                act.wait_ge(s["eff"], h + 1)
                for q in range(HALF):
                    act.activation(b_all[0:RANK, h * HALF + q], out_ps[q * RANK:q * RANK + RANK, h], ACT.Copy)\
                       .then_inc(s["eff_ev"], 1)
                if h == 0:
                    transposed(0)
            middle(0)
            transposed(1)
            att.wq_high(act, 0)
            with act.Fori(1, PAIRS - 1) as p:
                middle(p)
                high(p - 1)
                transposed(p + 1)
            middle(PAIRS - 1)
            high(PAIRS - 2)
            high(PAIRS - 1)

        @block.vector
        def _(dve):
            def apply1(p):
                after(dve, s["t1"], p)
                norm1.apply(dve, xn[:], tile_of(x_all, p), p)

            def update(p, more=True):
                xp = tile_of(x_all, p)
                dve.wait_ge(s["out"], p + 1)
                dve.scalar_tensor_tensor(xp, tile_of(out_ps, p % 2), gates[:, 2:3], xp, ALU.mult, ALU.add)\
                   .then_inc(s["x2"], 1)
                dve.wait_ge(s["x2"], p + 1)
                norm2.moments_of(dve, xp, p)
                if more:
                    norm1.moments_of(dve, tile_of(x_all, p + 2), p + 2)
                after(dve, s["t2"], p)
                norm2.apply(dve, xn2[:], xp, p)

            def low(p):
                dve.wait_ge(s["hi"], p + 1)
                cols = ds(p * P, P)
                dve.tensor_tensor(xTl[:, :, cols], t2_ps[:], xTh[:, :, cols].bitcast(F32), ALU.subtract)\
                    .then_inc(s["lo"], 1)

            def tile(p, more=True):
                update(p, more)
                if more:
                    apply1(p + 2)
                low(p)

            for p in range(2):
                norm1.moments_of(dve, x_all[:, p], p)
                apply1(p)
            tile(0)
            with dve.Fori(1, PAIRS - 2) as p:
                tile(p)
            tile(PAIRS - 2, more=False)
            tile(PAIRS - 1, more=False)

        @block.tensor
        def _(pe):
            def effective_b(h):
                for c in range(LORA_CHUNKS):
                    last = pe.matmul(out_ps[:, h], mix[:, c, h * HALF:h * HALF + HALF].rearrange("p b r -> p (b r)"),
                                     lora_b[:, c], start=(c == 0), stop=(c == LORA_CHUNKS - 1))
                last.then_inc(s["eff"], 1)

            def transpose(p):
                pe.wait_ge(norm1.applied, p + 1)
                after(pe, s["t1_ev"], p)
                for k in range(KT):
                    last = pe.transpose(t1_ps[:, k], xn[:, k * P:k * P + P], ident[:])
                last.then_inc(s["t1"], 1)

            def base(p):
                pe.wait_ge(s["t1_ev"], p + 1)
                after(pe, s["ax_ev"], p)
                for k in range(KT):
                    last = pe.matmul(ax_ps[:], xnT[:, k], a_all[:, k, ds(p, 1), :].rearrange("p o r -> p (o r)"),
                                     start=(k == 0), stop=(k == KT - 1))
                last.then_inc(s["ax"], 1)
                if not isinstance(p, int) or p >= 2:
                    pe.wait_ge(s["x2"], p - 1)
                for k in range(KT):
                    if k == 2:
                        pe.wait_ge(s["ax_ev"], p + 1)
                        after(pe, s["axT_ev"], p)
                    last = pe.matmul(tile_of(out_ps, p % 2), xnT[:, k], kern[:, k], start=(k == 0), stop=False)
                    if k == 2:
                        pe.transpose(axT_ps[:], ax[:], ident[:]).then_inc(s["axT"], 1)
                last.then_inc(s["base"], 1)

            def again(p):
                pe.wait_ge(norm2.applied, p + 1)
                after(pe, s["lo"], p)
                for k in range(KT):
                    last = pe.transpose(t2_ps[:, k], xn2[:, k * P:k * P + P], ident[:])
                last.then_inc(s["t2"], 1)

            def lora(p):
                pe.wait_ge(s["axT_ev"], p + 1)
                pe.matmul(tile_of(out_ps, p % 2), axT[:], b_all[:, ds(p, 1), :].rearrange("p o n -> p (o n)"),
                          start=False, stop=True).then_inc(s["out"], 1)

            effective_b(0)
            transpose(0)
            effective_b(1)
            pe.wait_ge(s["eff_ev"], HALF)
            pe.wait_ge(s["shared"], KT)
            pe.wait_ge(s["kern_in"], 16)
            base(0)
            transpose(1)
            pe.wait_ge(s["ones"], 1)
            pe.wait_ge(s["b_in"], 16)
            lora(0)
            pe.wait_ge(s["eff_ev"], 2 * HALF)
            base(1)
            again(0)
            transpose(2)
            lora(1)
            with pe.Fori(2, PAIRS - 1) as p:
                base(p)
                again(p - 1)
                transpose(p + 1)
                lora(p)
            base(PAIRS - 1)
            again(PAIRS - 2)
            lora(PAIRS - 1)
            pe.wait_ge(att.s["wq_lo"], KT)
            pe.wait_ge(s["hi"], HALF)
            pe.wait_ge(s["lo"], HALF)
            att.q_tile(pe, att.a_ps[0][:], 0, xTh, xTl)
            again(PAIRS - 1)


class Experts:

    LOADS = 4

    def __init__(self, al):
        self.router_a = al.sb("router_a", [P, KT, MID + EXPERTS])
        self.b = al.sb("b", [2 * MID, D])
        self.bh, self.bl = al.sb("bh", [2 * MID, D], F32R), al.sb("bl", [2 * MID, D], F32R)
        self.first = al.sb("first", [P, EXPERTS, EXPERTS])
        self.xn = al.sb("xn", [P, 2, D])
        self.xnT = al.sb("xnT", [P, 2, KT, P])
        self.mid = al.sb("mid", [P, PAIRS, MID + EXPERTS])
        self.norm = RowNorm(al, "norm")
        self.loaded, self.t, self.t_ev, self.m, self.m_ev, self.b_hi, self.b_lo = (
            al.sem(n) for n in ("loaded", "t", "t_ev", "m", "m_ev", "b_hi", "b_lo"))

    def load(self, sp, a):
        sp.dma_start(self.router_a[:], a["router_A"].rearrange("(k p) n -> p k n", p=P)).then_inc(self.loaded, 16)
        for half in (slice(0, MID), slice(MID, 2 * MID)):
            sp.dma_start(self.b[half], a["B"]).then_inc(self.loaded, 16)
        sp.dma_start(self.first[:].rearrange("p a b -> p (a b)"), a["first"]).then_inc(self.loaded, 16)

    def b_high(self, act):
        act.wait_ge(self.loaded, 16 * self.LOADS)
        act.activation(self.bh[:], self.b[:], ACT.Copy).then_inc(self.b_hi, 1)

    def b_low(self, pool):
        pool.wait_ge(self.b_hi, 1)
        pool.tensor_tensor(self.bl[:], self.b[:], self.bh[:].bitcast(F32), ALU.subtract).then_inc(self.b_lo, 1)

    def moments(self, dve, x_all, x_added, before, t):
        dve.wait_ge(x_added, before + t + 1)
        self.norm.moments_of(dve, x_all[:, t], t)

    def apply(self, dve, x_all, t):
        after(dve, self.t, t - 1)
        self.norm.apply(dve, self.xn[:, t % 2], x_all[:, t], t)

    def transpose(self, pe, ident, t_ps, t):
        if 0 <= t < PAIRS:
            pe.wait_ge(self.norm.applied, t + 1)
            after(pe, self.t_ev, t)
            for k in range(KT):
                last = pe.transpose(t_ps[:, k], self.xn[:, t % 2, k * P:k * P + P], ident[:])
            last.then_inc(self.t, 1)

    def copy(self, act, t_ps, t):
        act.wait_ge(self.t, t + 1)
        after(act, self.m, t - 1)
        act.activation(self.xnT[:, t % 2], t_ps[:], ACT.Copy).then_inc(self.t_ev, 1)

    def logits(self, pe, m_ps, t):
        if t == 0:
            pe.wait_ge(self.loaded, 16 * self.LOADS)
        if 0 <= t < PAIRS:
            pe.wait_ge(self.t_ev, t + 1)
            after(pe, self.m_ev, t)
            for k in range(KT):
                last = pe.matmul(m_ps[:], self.xnT[:, t % 2, k], self.router_a[:, k],
                                 start=(k == 0), stop=(k == KT - 1))
            last.then_inc(self.m, 1)

    def keep(self, dve, m_ps, t):
        if t >= 0:
            dve.wait_ge(self.m, t + 1)
            dve.tensor_copy(self.mid[:, t], m_ps[:]).then_inc(self.m_ev, 1)


class AttentionInputs:

    def __init__(self, al, k_dram, v_dram):
        self.cosq, self.sinq = al.sb("cosq", [P, SEQ]), al.sb("sinq", [P, SEQ])
        self.cap = al.sb("cap", [P, PAIRS, 2, SEQ])
        self.wq_land = al.sb("wq_land", [P, KT, GH * DK])
        self.wqh, self.wql = al.sb("wqh", [P, KT, GH * DK], F32R), al.sb("wql", [P, KT, GH * DK], F32R)
        self.wo_land = al.sb("wo_land", [P, GH, D])
        self.kT = al.sb("kT", [P, PAIRS * P])
        self.vr = al.sb("vr", [P, PAIRS, DK])
        self.s = {n: al.sem(n) for n in ("tab_in", "mask_in", "wq_in", "wo_in", "k_in", "v_in", "wq_hi", "wq_lo", "q")}
        self.a_ps = [al.ps("a_ps0", [P, D]), al.ps("a_ps1", [P, D])]
        self.k_dram, self.v_dram = k_dram, v_dram

    def load_wq(self, sp, a, g):
        sp.dma_start(self.wq_land[:], a["wq"].rearrange("(k p) n -> p k n", p=P)[:, :, ds(g * (GH * DK), GH * DK)])\
          .then_inc(self.s["wq_in"], 16)

    def load_wo(self, sp, a, g):
        sp.dma_start(self.wo_land[:], a["wo"].rearrange("(h p) n -> p h n", p=P)[:, ds(g * GH, GH), :])\
          .then_inc(self.s["wo_in"], 16)

    def load_k(self, sp, g):
        sp.dma_start(self.kT[:], self.k_dram[ds(g, 1)].rearrange("o p n -> p (o n)")).then_inc(self.s["k_in"], 16)

    def load_v(self, sp, g):
        sp.dma_start(self.vr[:], self.v_dram[ds(g, 1)].rearrange("o p t n -> p (o t) n")).then_inc(self.s["v_in"], 16)

    def load_first(self, sp, a):
        self.load_wq(sp, a, 0)
        sp.dma_start(self.cosq[:], a["cosq"]).then_inc(self.s["tab_in"], 16)
        sp.dma_start(self.sinq[:], a["sinq"]).then_inc(self.s["tab_in"], 16)
        for h in (0, 64):
            sp.dma_start(self.cap[h:h + 64].rearrange("p t b k -> p (t b) k"), a["mask"].rearrange("b q k -> q b k"))\
              .then_inc(self.s["mask_in"], 16)
        self.load_k(sp, 0)
        self.load_wo(sp, a, 0)
        self.load_v(sp, 0)
        sp.wait_ge(self.s["wq_lo"], KT)
        self.load_wq(sp, a, 1)

    def q_tile(self, pe, bank, i, xTh, xTl):
        h, half = i % GH, i // GH
        three_passes(pe, bank, lambda k: (self.wqh[:, k, h * DK:h * DK + DK], self.wql[:, k, h * DK:h * DK + DK]),
                     lambda k: (xTh[:, k, half * D:half * D + D], xTl[:, k, half * D:half * D + D]), KT)\
            .then_inc(self.s["q"], 1)

    def wq_high(self, act, g):
        act.wait_ge(self.s["wq_in"], 16 * g + 16)
        for k in range(KT):
            act.activation(self.wqh[:, k], self.wq_land[:, k], ACT.Copy).then_inc(self.s["wq_hi"], 1)

    def wq_low(self, pool, g, part=None):
        for k in part or range(KT):
            pool.wait_ge(self.s["wq_hi"], KT * g + k + 1)
            pool.tensor_tensor(self.wql[:, k], self.wq_land[:, k], self.wqh[:, k].bitcast(F32), ALU.subtract)\
                .then_inc(self.s["wq_lo"], 1)


def layer_1_attention(nc, a, x_all, gates, ident, xTh, xTl, att, experts):
    with ExitStack() as ctx:
        al = Pool(nc, ctx, "g")
        cosq, sinq, cap, wqh, wql = att.cosq, att.sinq, att.cap, att.wqh, att.wql
        wo_land, kT, vr = att.wo_land, att.kT, att.vr
        woh, wol = al.sb("woh", [P, GH, D], F32R), al.sb("wol", [P, GH, D], F32R)
        qT = al.sb("qT", [P, BATCH, GH, SEQ])
        qcos, qsw = al.sb("qcos", [P, 2, D]), al.sb("qsw", [P, 2, D])
        S = al.sb("S", [P, PAIRS, 2, P])
        smax, ssum, srec = (al.sb(n, [P, PAIRS, 4]) for n in ("smax", "ssum", "srec"))
        PT = al.sb("PT", [P, PAIRS, 2 * P])
        oh, ol = al.sb("oh", [P, 2, GH, 2, SEQ], F32R), al.sb("ol", [P, 2, GH, 2, SEQ], F32R)

        a_ps = att.a_ps
        s_ps = [al.ps("s_ps0", [P, D]), al.ps("s_ps1", [P, D])]
        o_ps = [al.ps(f"o_ps{b}", [P, GH, SEQ]) for b in range(2)]
        s = {n: al.sem(n) for n in (
            "cap0", "wo_hi", "wo_lo",
            "qsw", "qcos", "qsin", "qrot", "score", "cap", "mx", "sub", "expd", "ssum", "srec", "norm",
            "t", "pt", "av", "ohi", "olo", "wo", "x")}
        s.update(att.s)
        xt_ps, m_ps = al.ps("xt_ps", [P, KT, P]), al.ps("m_ps", [P, MID + EXPERTS])
        QT = 2 * GH
        CH = 4
        AHEAD = 3
        LATE = range(PAIRS - 2, PAIRS)
        order = [("late", t) for t in LATE] + [("q", i) for i in range(AHEAD)]
        for t in range(PAIRS + 1):
            order += [("q", t + AHEAD)] * (t + AHEAD < QT) + [("out", t - 1)] * (t > 0)
        place = {use: n for n, use in enumerate(order)}

        def bank(kind, i, alone=False):
            return a_ps[(i if alone else place[kind, i]) % 2]

        def late(g):
            return not isinstance(g, int) or g > 0

        per_seq = "p (b q) -> p b q"
        block = ctx.enter_context(nc.Block())

        @block.sync
        def _(sp):
            experts.load(sp, a)

            def group(g, wq=True):
                if wq:
                    sp.wait_ge(s["wq_lo"], KT * g + 2 * KT)
                    att.load_wq(sp, a, g + 2)
                sp.wait_ge(s["score"], CH * g + CH)
                att.load_k(sp, g + 1)
                sp.wait_ge(s["wo_lo"], GH * g + GH)
                att.load_wo(sp, a, g + 1)
                sp.wait_ge(s["av"], PAIRS * g + PAIRS)
                att.load_v(sp, g + 1)

            group(0)
            with sp.Fori(1, GROUPS - 2) as g:
                group(g)
            group(GROUPS - 2, wq=False)

        @block.scalar
        def _(act):
            def swap(g, i, first=False):
                n = QT * g + i
                act.wait_ge(s["q"], n + 1)
                if not first or i >= 2:
                    act.wait_ge(s["qrot"], n - 1)
                for h in (0, 64):
                    act.activation(qsw[h:h + 64, i % 2], bank("q", i, first)[64 - h:128 - h, :], ACT.Copy)\
                       .then_inc(s["qsw"], 1)

            def wo_high(g, high):
                act.wait_ge(s["wo_in"], 16 * g + 16)
                for h in range(GH):
                    act.activation(high[:, h], wo_land[:, h], ACT.Copy).then_inc(s["wo_hi"], 1)

            def exp(g, c):
                act.wait_ge(s["sub"], CH * g + c + 1)
                t = S[:, 2 * c:2 * c + 2]
                act.activation(t, t, ACT.Exp).then_inc(s["expd"], 1)

            def group(g, q=True, wq=True):
                def out_high(t):
                    act.wait_ge(s["av"], PAIRS * g + t + 1)
                    after(act, s["wo"], PAIRS * g + max(t - 1, 0))
                    for b in range(2):
                        act.activation(oh[:, t % 2, :, b], o_ps[b][:], ACT.Copy).then_inc(s["ohi"], 1)

                def transposed(t):
                    act.wait_ge(s["t"], PAIRS * g + t + 1)
                    act.activation(PT[:, t], s_ps[t % 2][:, 0:2 * P], ACT.Copy).then_inc(s["pt"], 1)

                exp(g, 0)
                exp(g, 1)
                exp(g, 2)
                if q and late(g):
                    act.wait_ge(s["wo"], PAIRS * g)
                    wo_high(g, woh)
                if not q:
                    transposed(0)
                    transposed(1)
                    out_high(0)
                if late(g):
                    exp(g, 3)
                for i in range(AHEAD):
                    if i == 1 and not late(g):
                        exp(g, 3)
                    if i == AHEAD - 1 and q:
                        transposed(0)
                        transposed(1)
                    if q:
                        swap(g + 1, i)
                if not late(g):
                    wo_high(g, woh)
                for t in range(PAIRS):
                    if q or t:
                        out_high(t)
                    if t + 2 < PAIRS:
                        transposed(t + 2)
                    if q and t + AHEAD < QT:
                        swap(g + 1, t + AHEAD)
                    if t + AHEAD == QT and q:
                        act.wait_ge(s["q"], QT * (g + 2))
                        if wq:
                            att.wq_high(act, g + 2)
                        else:
                            wo_high(g + 1, wqh)
                    if not q and t >= 3:
                        experts.copy(act, xt_ps, t - 3)
                if not q:
                    for t in range(PAIRS - 3, PAIRS):
                        experts.copy(act, xt_ps, t)

            for i in range(QT):
                swap(0, i, first=True)
            act.wait_ge(s["q"], QT)
            att.wq_high(act, 1)
            group(0)
            experts.b_high(act)
            with act.Fori(1, GROUPS - 2) as g:
                group(g)
            group(GROUPS - 2, wq=False)
            group(GROUPS - 1, q=False, wq=False)

        @block.gpsimd
        def _(pool):
            def sine(g, i):
                n = QT * g + i
                pool.wait_ge(s["qsw"], 2 * n + 2)
                t = qsw[:, i % 2].rearrange(per_seq, q=SEQ)
                pool.tensor_tensor(t, t, sinq[:].rearrange("p (o q) -> p o q", o=1).broadcast_to([P, D // SEQ, SEQ]),
                                   ALU.mult).then_inc(s["qsin"], 1)

            def wo_low(g, high, low):
                for h in range(GH):
                    pool.wait_ge(s["wo_hi"], GH * g + h + 1)
                    pool.tensor_tensor(low[:, h], wo_land[:, h], high[:, h].bitcast(F32), ALU.subtract)\
                        .then_inc(s["wo_lo"], 1)

            def group(g, q=True, wq=True):
                if q:
                    if late(g):
                        wo_low(g, woh, wol)
                    for i in range(QT):
                        sine(g + 1, i)
                        if i == AHEAD - 1 and not late(g):
                            wo_low(g, woh, wol)
                    if wq:
                        att.wq_low(pool, g + 2)
                    else:
                        wo_low(g + 1, wqh, wql)

            pool.wait_ge(s["tab_in"], 32)
            for i in range(QT):
                sine(0, i)
            att.wq_low(pool, 1)
            group(0)
            experts.b_low(pool)
            with pool.Fori(1, GROUPS - 2) as g:
                group(g)
            group(GROUPS - 2, wq=False)
            group(GROUPS - 1, q=False, wq=False)
            experts.norm.start(pool)
            for t in range(PAIRS):
                experts.norm.root(pool, t)

        @block.vector
        def _(dve):
            dve.wait_ge(s["tab_in"], 32)
            dve.wait_ge(s["mask_in"], 32)
            flat = cap[:].rearrange("p t b k -> p (t b k)")
            dve.tensor_scalar(flat, flat, 0.0, HUGE, ALU.not_equal, ALU.mult).then_inc(s["cap0"], 1)
            dve.wait_ge(s["cap0"], 1)
            dve.tensor_scalar(flat, flat, MASKED, None, ALU.add).then_inc(s["cap0"], 1)
            dve.wait_ge(s["cap0"], 2)

            def cosine(g, i, first=False):
                n = QT * g + i
                dve.wait_ge(s["qsw"], 2 * n + 2)
                dve.tensor_tensor(qcos[:, i % 2].rearrange(per_seq, q=SEQ),
                                  bank("q", i, first)[:].rearrange(per_seq, q=SEQ),
                                  cosq[:].rearrange("p (o q) -> p o q", o=1).broadcast_to([P, D // SEQ, SEQ]),
                                  ALU.mult).then_inc(s["qcos"], 1)

            def rotate(g, i):
                n = QT * g + i
                if i == 0:
                    after(dve, s["score"], CH * g)
                dve.wait_ge(s["qcos"], n + 1)
                dve.wait_ge(s["qsin"], n + 1)
                h, half = i % GH, i // GH
                dve.tensor_tensor(qT[:, half * 8:half * 8 + 8, h, :], qcos[:, i % 2].rearrange(per_seq, q=SEQ),
                                  qsw[:, i % 2].rearrange(per_seq, q=SEQ), ALU.add).then_inc(s["qrot"], 1)

            def rows(t, c):
                return t[:, 2 * c:2 * c + 2].rearrange("p t n -> p (t n)").rearrange("p (n o) -> p n o", o=1)\
                    .broadcast_to([P, 8, SEQ])

            def chunk(c):
                return S[:, 2 * c:2 * c + 2].rearrange("p t h n -> p (t h n)").rearrange("p (n k) -> p n k", k=SEQ)

            def stat(t, c):
                return t[:, 2 * c:2 * c + 2].rearrange("p t n -> p (t n)")

            def group(g, q=True):
                def limit(c):
                    dve.wait_ge(s["score"], CH * g + c + 1)
                    for t in range(2):
                        last = dve.tensor_tensor(
                            S[:, 2 * c + t], s_ps[c % 2][:, t * 2 * P:(t + 1) * 2 * P]
                                .rearrange("p (h n) -> p h n", h=2),
                            cap[:, 2 * c + t].rearrange("p b k -> p (b k)").rearrange("p (o n) -> p o n", o=1)
                            .broadcast_to([P, 2, P]), ALU.min)
                    last.then_inc(s["cap"], 1)

                def less_max(c):
                    dve.wait_ge(s["cap"], CH * g + c + 1)
                    dve.tensor_reduce(stat(smax, c), chunk(c), AX_X, ALU.max).then_inc(s["mx"], 1)
                    dve.wait_ge(s["mx"], CH * g + c + 1)
                    dve.tensor_tensor(chunk(c), chunk(c), rows(smax, c), ALU.subtract).then_inc(s["sub"], 1)

                def normalise(c):
                    dve.wait_ge(s["expd"], CH * g + c + 1)
                    dve.tensor_reduce(stat(ssum, c), chunk(c), AX_X, ALU.add).then_inc(s["ssum"], 1)
                    dve.wait_ge(s["ssum"], CH * g + c + 1)
                    dve.reciprocal(stat(srec, c), stat(ssum, c)).then_inc(s["srec"], 1)
                    dve.wait_ge(s["srec"], CH * g + c + 1)
                    dve.tensor_tensor(chunk(c), chunk(c), rows(srec, c), ALU.mult).then_inc(s["norm"], 1)

                def out_low(t):
                    for b in range(2):
                        dve.wait_ge(s["ohi"], 2 * (PAIRS * g + t) + b + 1)
                        dve.tensor_tensor(ol[:, t % 2, :, b], o_ps[b][:], oh[:, t % 2, :, b].bitcast(F32),
                                          ALU.subtract).then_inc(s["olo"], 1)

                def add(g, t, alone=False):
                    dve.wait_ge(s["wo"], PAIRS * g + t + 1)
                    after(dve, s["x"], PAIRS * g + t)
                    dve.scalar_tensor_tensor(x_all[:, t], bank("out", t, alone)[:], gates[:, 1:2], x_all[:, t],
                                             ALU.mult, ALU.add).then_inc(s["x"], 1)

                after(dve, s["t"], PAIRS * g)
                limit(0)
                limit(1)
                less_max(0)
                limit(2)
                less_max(1)
                limit(3)
                normalise(0)
                less_max(2)
                if late(g):
                    add(g - 1, PAIRS - 2)
                normalise(1)
                if late(g):
                    add(g - 1, PAIRS - 1)
                if not q:
                    out_low(0)
                if not late(g):
                    cosine(g + 1, 0)
                less_max(3)
                normalise(2)
                if not q:
                    out_low(1)
                for i in range(AHEAD):
                    if q and (i or late(g)):
                        cosine(g + 1, i)
                    if i == 0:
                        normalise(3)
                    if q and i < AHEAD - 1:
                        rotate(g + 1, i)
                for t in range(PAIRS):
                    if q or t > 1:
                        out_low(t)
                    if q and t + AHEAD <= QT:
                        rotate(g + 1, t + AHEAD - 1)
                    if q and t + AHEAD < QT:
                        cosine(g + 1, t + AHEAD)
                    if not q:
                        experts.keep(dve, m_ps, t - 5)
                    if t and (t - 1 not in LATE or not q):
                        add(g, t - 1, alone=not q)
                    if not q and t:
                        experts.moments(dve, x_all, s["x"], PAIRS * g, t - 1)
                        experts.apply(dve, x_all, t - 1)
                if not q:
                    experts.keep(dve, m_ps, PAIRS - 5)
                    add(g, PAIRS - 1, alone=True)
                    experts.moments(dve, x_all, s["x"], PAIRS * g, PAIRS - 1)
                    experts.keep(dve, m_ps, PAIRS - 4)
                    experts.apply(dve, x_all, PAIRS - 1)
                    for t in range(PAIRS - 3, PAIRS):
                        experts.keep(dve, m_ps, t)

            for i in range(QT + 1):
                if i < QT:
                    cosine(0, i, first=True)
                if i:
                    rotate(0, i - 1)
            group(0)
            with dve.Fori(1, GROUPS - 1) as g:
                group(g)
            group(GROUPS - 1, q=False)

        @block.tensor
        def _(pe):
            def wait_bank(g, kind, i, alone=False):
                n = place[kind, i] - 2
                if alone or n < 0:
                    pe.wait_ge(s["x"], PAIRS * g + i - 1)
                elif order[n][0] == "q":
                    pe.wait_ge(s["qcos"], QT * (g + 1) + order[n][1] + 1)
                elif order[n][0] == "out":
                    pe.wait_ge(s["x"], PAIRS * g + order[n][1] + 1)
                elif late(g):
                    pe.wait_ge(s["x"], PAIRS * (g - 1) + order[n][1] + 1)
                else:
                    pe.wait_ge(s["qcos"], QT)

            def project_q(g, i, first=False):
                if i == 0:
                    pe.wait_ge(s["wq_lo"], KT * g + KT)
                if not first:
                    wait_bank(g - 1, "q", i)
                elif i >= 2:
                    pe.wait_ge(s["qcos"], i - 1)
                att.q_tile(pe, bank("q", i, first)[:], i, xTh, xTl)

            def group(g, q=True):
                pe.wait_ge(s["k_in"], 16 * g + 16)
                for c in range(CH):
                    if c % 2 == 0:
                        pe.wait_ge(s["qrot"], QT * g + GH * (1 + c // 2))
                    if c < 2:
                        after(pe, s["pt"], PAIRS * g)
                    else:
                        pe.wait_ge(s["cap"], CH * g + c - 1)
                    for t in range(2):
                        for h in range(2):
                            for b in range(2):
                                n = 4 * c + 2 * t + b
                                col = ((2 * t + h) * 2 + b) * SEQ
                                last = pe.matmul(s_ps[c % 2][:, col:col + SEQ],
                                                 qT[:, n, 2 * h:2 * h + 2, :].rearrange("p h q -> p (h q)"),
                                                 kT[:, n * SEQ:n * SEQ + SEQ], start=True, stop=True)
                    last.then_inc(s["score"], 1)
                def attend(t):
                    pe.wait_ge(s["pt"], PAIRS * g + t + 1)
                    after(pe, s["olo"], 2 * (PAIRS * g + t))
                    for b in range(2):
                        r = slice(b * SEQ, b * SEQ + SEQ)
                        last = pe.matmul(o_ps[b][:].rearrange("p h q -> p (h q)"), vr[r, t, :], PT[r, t, :],
                                         start=True, stop=True)
                    last.then_inc(s["av"], 1)

                parts = (wqh, wql) if not q else (woh, wol)

                def project_out(g, t, kind="out", parts=(woh, wol), alone=False):
                    if t == 0:
                        pe.wait_ge(s["wo_lo"], GH * g + GH)
                    wait_bank(g, kind, t, alone)
                    pe.wait_ge(s["olo"], 2 * (PAIRS * g + t) + 2)
                    three_passes(pe, bank("out", t, alone)[:], lambda h: (oh[:, t % 2, h].rearrange("p b q -> p (b q)"),
                                            ol[:, t % 2, h].rearrange("p b q -> p (b q)")),
                                 lambda h: (parts[0][:, h], parts[1][:, h]), GH).then_inc(s["wo"], 1)

                def transpose(t):
                    pe.wait_ge(s["norm"], CH * g + t // 2 + 1)
                    if t >= 2:
                        pe.wait_ge(s["pt"], PAIRS * g + t - 1)
                    for h in range(2):
                        last = pe.transpose(s_ps[t % 2][:, h * P:h * P + P], S[:, t, h], ident[:])
                    last.then_inc(s["t"], 1)

                if late(g):
                    for t in LATE:
                        project_out(g - 1, t, "late")
                if q:
                    for i in range(AHEAD - 1):
                        project_q(g + 1, i)
                pe.wait_ge(s["cap"], CH * g + CH)
                transpose(0)
                transpose(1)
                if q:
                    project_q(g + 1, AHEAD - 1)
                pe.wait_ge(s["v_in"], 16 * g + 16)
                for t in range(PAIRS):
                    attend(t)
                    if t + 2 < PAIRS:
                        transpose(t + 2)
                    if q and t + AHEAD < QT:
                        project_q(g + 1, t + AHEAD)
                    if t and (t - 1 not in LATE or not q):
                        project_out(g, t - 1, parts=parts, alone=not q)
                    if not q and t >= 3:
                        experts.transpose(pe, ident, xt_ps, t - 3)
                        experts.logits(pe, m_ps, t - 4)
                if not q:
                    project_out(g, PAIRS - 1, parts=parts, alone=True)
                    for t in range(PAIRS - 3, PAIRS + 1):
                        experts.transpose(pe, ident, xt_ps, t)
                        experts.logits(pe, m_ps, t - 1)

            for i in range(1, QT):
                project_q(0, i, first=True)
            group(0)
            with pe.Fori(1, GROUPS - 1) as g:
                group(g)
            group(GROUPS - 1, q=False)


def layer_1_ffn(nc, a, x_all, ident, gates, experts, out):
    with ExitStack() as ctx:
        al = Pool(nc, ctx, "h")
        mid, first = experts.mid, experts.first
        g4 = al.sb("g4", [P, 1])
        beats = al.sb("beats", [P, PAIRS, EXPERTS, EXPERTS])
        ties = al.sb("ties", [P, PAIRS, EXPERTS, EXPERTS])
        rank = al.sb("rank", [P, PAIRS, EXPERTS])
        chosen = al.sb("chosen", [P, PAIRS, EXPERTS])
        top = al.sb("top", [P, PAIRS])
        e = al.sb("e", [P, PAIRS, EXPERTS])
        total = al.sb("total", [P, PAIRS])
        inverse = al.sb("inverse", [P, PAIRS])
        weighed = al.sb("weighed", [P, PAIRS, 2, MID])
        parts = al.sb("parts", [P, 2, P], F32R)
        t_ps = [al.ps(f"t_ps{i}", [P, P]) for i in range(2)]
        d_ps = [al.ps(f"d_ps{i}", [P, D]) for i in range(2)]
        s = {n: al.sem(n) for n in ("g4", "gate", "expd", "weighed", "mt", "m_hi", "m_lo", "d", "x", "out")}
        block = ctx.enter_context(nc.Block())

        @block.sync
        def _(sp):
            out_rows = out.rearrange("(t p) d -> p t d", p=P)
            for t in range(PAIRS):
                sp.wait_ge(s["x"], t + 1)
                sp.dma_start(out_rows[:, t], x_all[:, t]).then_inc(s["out"], 16)
            sp.wait_ge(s["out"], 16 * PAIRS)

        @block.scalar
        def _(act):
            act.activation(g4[:], gates[:, 3:4], ACT.Copy, scale=LORA_SCALE).then_inc(s["g4"], 1)
            act.wait_ge(s["gate"], 1)
            act.activation(e[:], e[:], ACT.Exp).then_inc(s["expd"], 1)
            for t in range(PAIRS):
                act.wait_ge(s["mt"], t + 1)
                after(act, s["d"], t - 1)
                act.activation(parts[:, t % 2], t_ps[t % 2][:], ACT.Copy).then_inc(s["m_hi"], 1)

        @block.vector
        def _(dve):
            step = [0]

            def link(instruction):
                step[0] += 1
                instruction.then_inc(chain, 1)
                dve.wait_ge(chain, step[0])

            chain = al.sem("chain")
            logits = mid[:, :, MID:]
            rival = logits.rearrange("p t (o j) -> p t o j", o=1).broadcast_to([P, PAIRS, EXPERTS, EXPERTS])
            own = logits.rearrange("p t (j o) -> p t j o", o=1).broadcast_to([P, PAIRS, EXPERTS, EXPERTS])
            link(dve.tensor_tensor(beats[:], rival, own, ALU.is_gt))
            link(dve.tensor_tensor(ties[:], rival, own, ALU.is_equal))
            link(dve.tensor_tensor(ties[:], ties[:], first[:].rearrange("p (o i) j -> p o i j", o=1)
                                   .broadcast_to([P, PAIRS, EXPERTS, EXPERTS]), ALU.mult))
            link(dve.tensor_tensor(beats[:], beats[:], ties[:], ALU.add))
            link(dve.tensor_reduce(rank[:], beats[:], AX_X, ALU.add))
            link(dve.tensor_scalar(chosen[:], rank[:], 1.5, None, ALU.is_lt))
            link(dve.tensor_reduce(top[:], logits, AX_X, ALU.max))
            dve.tensor_tensor(e[:], logits, top[:].rearrange("p (t o) -> p t o", o=1)
                              .broadcast_to([P, PAIRS, EXPERTS]), ALU.subtract).then_inc(s["gate"], 1)
            dve.wait_ge(s["expd"], 1)
            link(dve.tensor_tensor(e[:], e[:], chosen[:], ALU.mult))
            link(dve.tensor_reduce(total[:], e[:], AX_X, ALU.add))
            link(dve.reciprocal(inverse[:], total[:]))
            link(dve.tensor_tensor(e[:], e[:], inverse[:].rearrange("p (t o) -> p t o", o=1)
                                   .broadcast_to([P, PAIRS, EXPERTS]), ALU.mult))

            def weigh(t):
                dve.tensor_tensor(weighed[:, t].rearrange("p c (e r) -> p c e r", e=EXPERTS),
                                  mid[:, t, 0:MID].rearrange("p (c e r) -> p c e r", c=1, e=EXPERTS)
                                  .broadcast_to([P, 2, EXPERTS, ERANK]),
                                  e[:, t].rearrange("p (c e o) -> p c e o", c=1, o=1)
                                  .broadcast_to([P, 2, EXPERTS, ERANK]), ALU.mult).then_inc(s["weighed"], 1)

            def low(t):
                dve.wait_ge(s["m_hi"], t + 1)
                rows = parts[MID:, t % 2]
                dve.tensor_tensor(rows, t_ps[t % 2][MID:, :], rows.bitcast(F32), ALU.subtract).then_inc(s["m_lo"], 1)

            weigh(0)
            weigh(1)
            dve.wait_ge(s["g4"], 1)
            low(0)
            for t in range(PAIRS):
                if t + 2 < PAIRS:
                    weigh(t + 2)
                if t + 1 < PAIRS:
                    low(t + 1)
                dve.wait_ge(s["d"], t + 1)
                dve.scalar_tensor_tensor(x_all[:, t], d_ps[t % 2][:], g4[:], x_all[:, t], ALU.mult, ALU.add)\
                   .then_inc(s["x"], 1)

        @block.tensor
        def _(pe):
            pe.wait_ge(experts.b_lo, 1)

            def delta(t):
                pe.wait_ge(s["m_lo"], t + 1)
                after(pe, s["x"], t - 1)
                pe.matmul(d_ps[t % 2][:], parts[:, t % 2], experts.bl[:], start=True, stop=False)
                pe.matmul(d_ps[t % 2][:], parts[:, t % 2], experts.bh[:], start=False, stop=True).then_inc(s["d"], 1)

            for t in range(PAIRS):
                pe.wait_ge(s["weighed"], t + 1)
                after(pe, s["m_lo"], t - 1)
                pe.transpose(t_ps[t % 2][:], weighed[:, t].rearrange("p c m -> p (c m)"), ident[:])\
                   .then_inc(s["mt"], 1)
                if t:
                    delta(t - 1)
            delta(PAIRS - 1)


def flamingo_gated(nc, a, out):
    k_dram = nc.dram_tensor("k_scratch", (GROUPS, P, PAIRS * P), F32, kind="Internal").ap()
    v_dram = nc.dram_tensor("v_scratch", (GROUPS, P, PAIRS, DK), F32, kind="Internal").ap()
    with ExitStack() as ctx:
        al = Pool(nc, ctx, "all")
        x_all = al.sb("x_all", [P, PAIRS, D])
        ident = al.sb("ident", [P, P])
        gates = al.sb("gates", [P, 4])
        ffn = FfnInputs(Pool(nc, ctx, "ffn"))
        layer_0_attention(nc, a, x_all, ident, gates, k_dram, v_dram, ffn)
        al = Pool(nc, ctx, "att")
        xTh = al.sb("xTh", [P, KT, PAIRS * P], F32R)
        xTl = al.sb("xTl", [P, KT, PAIRS * P], F32R)
        att = AttentionInputs(al, k_dram, v_dram)
        layer_0_ffn(nc, a, x_all, ident, gates, xTh, xTl, ffn, att)
        experts = Experts(Pool(nc, ctx, "exp"))
        layer_1_attention(nc, a, x_all, gates, ident, xTh, xTl, att, experts)
        layer_1_ffn(nc, a, x_all, ident, gates, experts, out)


def rotary_tables(scale):
    freq = 1.0 / np.float32(10000.0) ** (np.arange(0, DK, 2, dtype=np.float32) / np.float32(DK))
    angle = (np.arange(SEQ, dtype=np.float32)[:, None] * freq[None, :]).T.astype(np.float64)
    cos, sin = np.cos(angle) * scale, np.sin(angle) * scale
    return (np.concatenate([cos, cos]).astype(np.float32), np.concatenate([-sin, sin]).astype(np.float32))


def constants():
    c = {"ident": np.eye(P, dtype=np.float32)}
    pick = np.zeros((P, 15 * ROWS0), np.float32)
    pick[np.arange(P), 7 * ROWS0 + np.arange(P) // HD0] = 1.0
    c["pick"] = pick
    c["cosk"], c["sink"] = rotary_tables(1.0)
    c["cosq"], c["sinq"] = rotary_tables(float(DK) ** -0.5)
    c["eye_r"] = (np.arange(P)[:, None] % RANK == np.arange(RANK)[None, :]).astype(np.float32)
    lower = np.arange(EXPERTS)[None, :] < np.arange(EXPERTS)[:, None]
    c["first"] = np.tile(lower.astype(np.float32).reshape(1, -1), (P, 1))
    return c


def kernel(**inputs):
    import concourse.bacc as bacc
    from concourse.bass_utils import run_bass_kernel_spmd

    i = {k: np.asarray(v) for k, v in inputs.items()}
    rows = BATCH * SEQ
    arrays = {
        "x": i["x"].reshape(rows, D),
        "ctx": i["ctx_4096"].reshape(rows, D),
        "ctxT": i["ctx_4096"].reshape(rows, D).T,
        "mask": i["mask_BxSxS2_ff1"],
        "g4": np.concatenate([i["g_xattn"], i["g_ffn"]]),
        "W4": np.concatenate([i[f"L0_xattn_W{n}"].T for n in "qkvo"], axis=1),
        "b4": np.stack([i[f"L0_xattn_b{n}"] for n in "qkvo"], axis=1),
        "gate": np.repeat(i["L0_ffn_gate"].T, RANK, axis=0),
        "kernel": i["L0_ffn_kernel"],
        "lora_A": i["L0_ffn_lora_A"].reshape(LORAS * RANK, D),
        "lora_B": i["L0_ffn_lora_B"].transpose(0, 2, 1).reshape(LORAS * RANK, D),
        "A_shared": i["L0_ffn_lora_A_shared"].T,
        "B_shared": np.concatenate([i["L0_ffn_lora_B_shared"].T, i["L0_ffn_bias"][None, :]]),
        "wq": i["L1_xattn_wq"], "wk": i["L1_xattn_wk"], "wv": i["L1_xattn_wv"], "wo": i["L1_xattn_wo"],
        "router_A": np.concatenate([i["L1_ffn_A"].reshape(MID, D), i["L1_ffn_router_w"]]).T,
        "B": i["L1_ffn_B"].transpose(0, 2, 1).reshape(MID, D),
        **constants(),
    }
    nc = bacc.Bacc("TRN2", target_bir_lowering=False, num_devices=1)
    feed, a = {}, {}
    for name, array in arrays.items():
        feed[f"in_{name}"] = np.ascontiguousarray(array)
        a[name] = nc.dram_tensor(f"in_{name}", array.shape, F32, kind="ExternalInput").ap()
    out = nc.dram_tensor("out_x", (rows, D), F32, kind="ExternalOutput").ap()
    flamingo_gated(nc, a, out)
    result = run_bass_kernel_spmd(nc, [feed], core_ids=[0])
    return result.results[0]["out_x"].reshape(BATCH, SEQ, D)
```
